# Optimizing a Trainium2 kernel written in Bass

```python
import numpy as np
import jax
import jax.numpy as jnp

def _softmax(x, axis=-1):
    return jax.nn.softmax(x, axis=axis)

def _gelu(x):
    return jax.nn.gelu(x, approximate=True)

def _silu(x):
    return jax.nn.silu(x)

def _sigmoid(x):
    return jax.nn.sigmoid(x)

def _layernorm(x, axis=-1, eps=1e-05):
    m = jnp.mean(x, axis=axis, keepdims=True)
    v = jnp.var(x, axis=axis, keepdims=True)
    return (x - m) / jnp.sqrt(v + eps)

def _scatter_add(tgt, idx, src, axis=0):
    return tgt.at[idx].add(src)

def _segment_sum(src, seg, n):
    return jax.ops.segment_sum(src, seg, n)
kernel_name = 'mk_macaron_d2_jaxref_r8_e02523'

def setup_inputs(seed: int=0):
    np.random.seed(seed)
    _w = jnp.asarray

    def _L0_attn_setup():
        import jax, jax.numpy as jnp
        import numpy as np
        N_LAYERS = 2
        D_MODEL = 128
        D_STATE = 16
        D_CONV = 4
        EXPAND = 2
        D_INNER = EXPAND * D_MODEL
        DT_RANK = (D_MODEL + 15) // 16
        B, T = (2, 128)
        LN_EPS = 1e-05

        def _layer_norm(x, w, b):
            mu = jnp.mean(x, axis=-1, keepdims=True)
            xc = x - mu
            var = jnp.mean(xc * xc, axis=-1, keepdims=True)
            return xc * jax.lax.rsqrt(var + LN_EPS) * w + b

        def _mamba_layer(x, in_w, cw, cb, xp_w, dt_w, dt_b, A_log, Dskip, out_w):
            xz = jnp.einsum('btd,ed->bte', x, in_w)
            xc, z = jnp.split(xz, 2, axis=-1)
            pad = D_CONV - 1
            xpad = jnp.pad(xc, ((0, 0), (pad, 0), (0, 0)))
            Tlen = xc.shape[1]
            conv = sum((xpad[:, k:k + Tlen, :] * cw[:, k] for k in range(D_CONV))) + cb
            u = jax.nn.silu(conv)
            x_dbl = jnp.einsum('btd,ed->bte', u, xp_w)
            dt, Bm, Cm = jnp.split(x_dbl, [DT_RANK, DT_RANK + D_STATE], axis=-1)
            dt = jax.nn.softplus(jnp.einsum('btr,dr->btd', dt, dt_w) + dt_b)
            A = -jnp.exp(A_log)

            def step(h, inp):
                dt_t, B_t, C_t, u_t = inp
                dA = jnp.exp(dt_t[:, :, None] * A)
                h = dA * h + (dt_t * u_t)[:, :, None] * B_t[:, None, :]
                y = jnp.einsum('bdn,bn->bd', h, C_t)
                return (h, y)
            h0 = jnp.zeros((x.shape[0], D_INNER, D_STATE), x.dtype)
            _, ys = jax.lax.scan(step, h0, (dt.transpose(1, 0, 2), Bm.transpose(1, 0, 2), Cm.transpose(1, 0, 2), u.transpose(1, 0, 2)))
            y = ys.transpose(1, 0, 2) + u * Dskip
            y = y * jax.nn.silu(z)
            return jnp.einsum('bti,oi->bto', y, out_w)
        key = jax.random.key(seed)
        ks = jax.random.split(key, 12)
        L = N_LAYERS
        x = jax.random.normal(ks[0], (B, T, D_MODEL), jnp.float32)
        in_proj_w = 0.02 * jax.random.normal(ks[1], (L, 2 * D_INNER, D_MODEL), jnp.float32)
        conv_w = 0.2 * jax.random.normal(ks[2], (L, D_INNER, D_CONV), jnp.float32)
        conv_b = jnp.zeros((L, D_INNER), jnp.float32)
        x_proj_w = 0.02 * jax.random.normal(ks[3], (L, DT_RANK + 2 * D_STATE, D_INNER), jnp.float32)
        dt_proj_w = 0.02 * jax.random.normal(ks[4], (L, D_INNER, DT_RANK), jnp.float32)
        dt_proj_b = jnp.full((L, D_INNER), -4.6, jnp.float32)
        A_log = jnp.broadcast_to(jnp.log(jnp.arange(1, D_STATE + 1, dtype=jnp.float32)), (L, D_INNER, D_STATE))
        Dskip = jnp.ones((L, D_INNER), jnp.float32)
        out_proj_w = 0.02 * jax.random.normal(ks[5], (L, D_MODEL, D_INNER), jnp.float32)
        ln_w = jnp.ones((L, D_MODEL), jnp.float32)
        ln_b = jnp.zeros((L, D_MODEL), jnp.float32)
        return {'x': x, 'in_proj_w': in_proj_w, 'conv_w': conv_w, 'conv_b': conv_b, 'x_proj_w': x_proj_w, 'dt_proj_w': dt_proj_w, 'dt_proj_b': dt_proj_b, 'A_log': A_log, 'Dskip': Dskip, 'out_proj_w': out_proj_w, 'ln_w': ln_w, 'ln_b': ln_b}
    _L0_attn_in = _L0_attn_setup()

    def _L0_ffn_setup():
        import jax, jax.numpy as jnp
        import numpy as np
        H = 128
        I = 88
        E = 64
        TOP_K = 8
        NG = 8
        TOPK_GROUP = 4
        N_SHARED = 2
        ROUTED_SCALE = 2.5
        S_I = I * N_SHARED

        def _route(x, gate_w, gate_bias):
            T = x.shape[0]
            logits = x @ gate_w.T
            scores = jax.nn.sigmoid(logits)
            scores_for_choice = scores + gate_bias[None, :]
            grp = scores_for_choice.reshape(T, NG, E // NG)
            group_scores = jnp.sum(jax.lax.top_k(grp, 2)[0], axis=-1)
            _, gidx = jax.lax.top_k(group_scores, TOPK_GROUP)
            gmask = jnp.zeros((T, NG), dtype=scores.dtype).at[jnp.arange(T)[:, None], gidx].set(1.0)
            emask = jnp.repeat(gmask, E // NG, axis=1)
            masked = jnp.where(emask > 0, scores_for_choice, 0.0)
            _, topk_idx = jax.lax.top_k(masked, TOP_K)
            topk_w = jnp.take_along_axis(scores, topk_idx, axis=1)
            topk_w = topk_w / (jnp.sum(topk_w, axis=-1, keepdims=True) + 1e-20)
            topk_w = topk_w * ROUTED_SCALE
            rw = jnp.zeros((T, E), dtype=scores.dtype).at[jnp.arange(T)[:, None], topk_idx].add(topk_w)
            return rw

        def _mlp(x, gw, uw, dw):
            return jax.nn.silu(x @ gw.T) * (x @ uw.T) @ dw.T
        key = jax.random.key(seed)
        ks = jax.random.split(key, 10)
        sc = 0.02
        return {'hidden_states': jax.random.normal(ks[0], (1, 128, H), dtype=jnp.float32), 'gate_w': sc * jax.random.normal(ks[1], (E, H), dtype=jnp.float32), 'gate_bias': sc * jax.random.normal(ks[2], (E,), dtype=jnp.float32), 'Wg': sc * jax.random.normal(ks[3], (E, I, H), dtype=jnp.float32), 'Wu': sc * jax.random.normal(ks[4], (E, I, H), dtype=jnp.float32), 'Wd': sc * jax.random.normal(ks[5], (E, H, I), dtype=jnp.float32), 'Sg': sc * jax.random.normal(ks[6], (S_I, H), dtype=jnp.float32), 'Su': sc * jax.random.normal(ks[7], (S_I, H), dtype=jnp.float32), 'Sd': sc * jax.random.normal(ks[8], (H, S_I), dtype=jnp.float32)}
    _L0_ffn_in = _L0_ffn_setup()

    def _L1_attn_setup():
        import jax, jax.numpy as jnp
        import numpy as np
        from jax import lax
        B, T, D = (4, 512, 128)

        def _reference_tuple_inner(x, W_in, W_alpha, b_alpha, W_beta, b_beta, W_v, b_v, W_out):
            xp = jax.nn.silu(jnp.einsum('btd,ed->bte', x, W_in))
            alpha = jax.nn.sigmoid(jnp.einsum('bte,fe->btf', xp, W_alpha) + b_alpha)
            beta = jax.nn.sigmoid(jnp.einsum('bte,fe->btf', xp, W_beta) + b_beta)
            v = jnp.tanh(jnp.einsum('bte,fe->btf', xp, W_v) + b_v)
            bv = beta * v

            def step(h, ab):
                a_t, bv_t = ab
                h = a_t * h + bv_t
                return (h, h * jax.nn.silu(h))
            h0 = jnp.zeros((x.shape[0], W_alpha.shape[0]), dtype=x.dtype)
            h_last, outs = lax.scan(step, h0, (alpha.transpose(1, 0, 2), bv.transpose(1, 0, 2)))
            cell_out = outs.transpose(1, 0, 2)
            output = jnp.einsum('btf,df->btd', cell_out, W_out)
            return (output, h_last)
        key = jax.random.key(seed)
        ks = jax.random.split(key, 6)
        s = 1.0 / np.sqrt(D)
        return {'x': jax.random.normal(ks[0], (B, T, D), dtype=jnp.float32), 'W_in': jax.random.normal(ks[1], (D, D), dtype=jnp.float32) * s, 'W_alpha': jax.random.normal(ks[2], (D, D), dtype=jnp.float32) * s, 'b_alpha': jnp.full((D,), 2.0, dtype=jnp.float32), 'W_beta': jax.random.normal(ks[3], (D, D), dtype=jnp.float32) * s, 'b_beta': jnp.zeros((D,), dtype=jnp.float32), 'W_v': jax.random.normal(ks[4], (D, D), dtype=jnp.float32) * s, 'b_v': jnp.zeros((D,), dtype=jnp.float32), 'W_out': jax.random.normal(ks[5], (D, D), dtype=jnp.float32) * s}
    _L1_attn_in = _L1_attn_setup()

    def _L1_ffn_setup():
        import jax, jax.numpy as jnp
        import numpy as np
        DIM = 128
        DEPTH = 2
        HEADS = 8
        DIM_HEAD = 64
        WINDOW = 64
        INNER = HEADS * DIM_HEAD
        HID = int(DIM * 4 * 2 / 3)
        B, N = (2, 1024)
        QK_SCALE = 8.0

        def shift_token(t):
            t1, t2 = jnp.split(t, 2, axis=-1)
            t2 = jnp.pad(t2, ((0, 0), (1, 0), (0, 0)))[:, :-1]
            return jnp.concatenate([t1, t2], axis=-1)

        def l2norm(t):
            return t / jnp.clip(jnp.linalg.norm(t, axis=-1, keepdims=True), 1e-12)

        def rotate_half(x):
            x1, x2 = jnp.split(x, 2, axis=-1)
            return jnp.concatenate([-x2, x1], axis=-1)

        def rotary_xpos(q, k):
            n = q.shape[-2]
            half_idx = jnp.arange(0, DIM_HEAD, 2, dtype=jnp.float32)
            inv_freq = 1.0 / 10000.0 ** (half_idx / DIM_HEAD)
            t = jnp.arange(n, dtype=jnp.float32)
            freqs = t[:, None] * inv_freq[None, :]
            freqs = jnp.concatenate([freqs, freqs], axis=-1)
            base = (half_idx + 0.4 * DIM_HEAD) / (1.4 * DIM_HEAD)
            power = (t - n // 2) / float(WINDOW // 2)
            scale = base[None, :] ** power[:, None]
            scale = jnp.concatenate([scale, scale], axis=-1)
            cos, sin = (jnp.cos(freqs), jnp.sin(freqs))
            q = q * cos * scale + rotate_half(q) * sin * scale
            k = k * cos / scale + rotate_half(k) * sin / scale
            return (q, k)

        def local_attention(q, k, v):
            b, h, n, d = q.shape
            w = n // WINDOW
            bq = q.reshape(b, h, w, WINDOW, d) * QK_SCALE
            bk = k.reshape(b, h, w, WINDOW, d)
            bv = v.reshape(b, h, w, WINDOW, d)

            def look_around(t):
                p = jnp.pad(t, ((0, 0), (0, 0), (1, 0), (0, 0), (0, 0)))
                return jnp.concatenate([p[:, :, :w], p[:, :, 1:]], axis=3)
            bk, bv = (look_around(bk), look_around(bv))
            bt = jnp.arange(n).reshape(w, WINDOW)
            btp = jnp.pad(bt, ((1, 0), (0, 0)), constant_values=-1)
            btk = jnp.concatenate([btp[:w], btp[1:]], axis=1)
            sim = jnp.einsum('bhwid,bhwjd->bhwij', bq, bk)
            i = bt[:, :, None]
            j = btk[:, None, :]
            mask = (i < j) | (i > j + WINDOW) | (j == -1)
            sim = jnp.where(mask, -jnp.finfo(sim.dtype).max, sim)
            attn = jax.nn.softmax(sim, axis=-1)
            out = jnp.einsum('bhwij,bhwjd->bhwid', attn, bv)
            return out.reshape(b, h, n, d)

        def _layer(x, wqkv, qs, ksc, wo, lg, lb, w1, b1, w2, b2):
            b, n, _ = x.shape
            h = shift_token(x)
            qkv = h @ wqkv
            q, k, v = jnp.split(qkv, 3, axis=-1)
            to_heads = lambda t: t.reshape(b, n, HEADS, DIM_HEAD).transpose(0, 2, 1, 3)
            q, k, v = (to_heads(q), to_heads(k), to_heads(v))
            q = l2norm(q) * qs
            k = l2norm(k) * ksc
            q, k = rotary_xpos(q, k)
            o = local_attention(q, k, v)
            o = o.transpose(0, 2, 1, 3).reshape(b, n, INNER)
            x = x + o @ wo
            h = shift_token(x)
            mu = h.mean(-1, keepdims=True)
            var = h.var(-1, keepdims=True)
            h = (h - mu) / jnp.sqrt(var + 1e-05) * lg + lb
            h = h @ w1 + b1
            a, g = jnp.split(h, 2, axis=-1)
            h = a * jax.nn.gelu(g, approximate=False)
            x = x + h @ w2 + b2
            return x
        key = jax.random.key(seed)
        ks = jax.random.split(key, 6)
        return {'x': jax.random.normal(ks[0], (B, N, DIM), jnp.float32), 'wqkv': jax.random.normal(ks[1], (DEPTH, DIM, 3 * INNER), jnp.float32) * 0.02, 'q_scale': jnp.ones((DEPTH, DIM_HEAD), jnp.float32), 'k_scale': jnp.ones((DEPTH, DIM_HEAD), jnp.float32), 'wo': jax.random.normal(ks[2], (DEPTH, INNER, DIM), jnp.float32) * 0.02, 'ln_g': jnp.ones((DEPTH, DIM), jnp.float32), 'ln_b': jnp.zeros((DEPTH, DIM), jnp.float32), 'w1': jax.random.normal(ks[3], (DEPTH, DIM, 2 * HID), jnp.float32) * 0.02, 'b1': jnp.zeros((DEPTH, 2 * HID), jnp.float32), 'w2': jax.random.normal(ks[4], (DEPTH, HID, DIM), jnp.float32) * 0.02, 'b2': jnp.zeros((DEPTH, DIM), jnp.float32)}
    _L1_ffn_in = _L1_ffn_setup()
    _d = {'L0_attn_x': _L0_attn_in['x'], 'L0_attn_in_proj_w': _L0_attn_in['in_proj_w'], 'L0_attn_conv_w': _L0_attn_in['conv_w'], 'L0_attn_conv_b': _L0_attn_in['conv_b'], 'L0_attn_x_proj_w': _L0_attn_in['x_proj_w'], 'L0_attn_dt_proj_w': _L0_attn_in['dt_proj_w'], 'L0_attn_dt_proj_b': _L0_attn_in['dt_proj_b'], 'L0_attn_A_log': _L0_attn_in['A_log'], 'L0_attn_Dskip': _L0_attn_in['Dskip'], 'L0_attn_out_proj_w': _L0_attn_in['out_proj_w'], 'L0_attn_ln_w': _L0_attn_in['ln_w'], 'L0_attn_ln_b': _L0_attn_in['ln_b'], 'L0_ffn_gate_w': _L0_ffn_in['gate_w'], 'L0_ffn_gate_bias': _L0_ffn_in['gate_bias'], 'L0_ffn_Wg': _L0_ffn_in['Wg'], 'L0_ffn_Wu': _L0_ffn_in['Wu'], 'L0_ffn_Wd': _L0_ffn_in['Wd'], 'L0_ffn_Sg': _L0_ffn_in['Sg'], 'L0_ffn_Su': _L0_ffn_in['Su'], 'L0_ffn_Sd': _L0_ffn_in['Sd'], 'L1_attn_W_in': _L1_attn_in['W_in'], 'L1_attn_W_alpha': _L1_attn_in['W_alpha'], 'L1_attn_b_alpha': _L1_attn_in['b_alpha'], 'L1_attn_W_beta': _L1_attn_in['W_beta'], 'L1_attn_b_beta': _L1_attn_in['b_beta'], 'L1_attn_W_v': _L1_attn_in['W_v'], 'L1_attn_b_v': _L1_attn_in['b_v'], 'L1_attn_W_out': _L1_attn_in['W_out'], 'L1_ffn_wqkv': _L1_ffn_in['wqkv'], 'L1_ffn_q_scale': _L1_ffn_in['q_scale'], 'L1_ffn_k_scale': _L1_ffn_in['k_scale'], 'L1_ffn_wo': _L1_ffn_in['wo'], 'L1_ffn_ln_g': _L1_ffn_in['ln_g'], 'L1_ffn_ln_b': _L1_ffn_in['ln_b'], 'L1_ffn_w1': _L1_ffn_in['w1'], 'L1_ffn_b1': _L1_ffn_in['b1'], 'L1_ffn_w2': _L1_ffn_in['w2'], 'L1_ffn_b2': _L1_ffn_in['b2']}
    _x0 = _d['L0_attn_x']
    _d['L0_attn_x'] = jax.random.normal(jax.random.fold_in(jax.random.key(seed), 1), (8, 512, 128), dtype=_x0.dtype)
    del _x0
    return _d

def reference(L0_attn_x, L0_attn_in_proj_w, L0_attn_conv_w, L0_attn_conv_b, L0_attn_x_proj_w, L0_attn_dt_proj_w, L0_attn_dt_proj_b, L0_attn_A_log, L0_attn_Dskip, L0_attn_out_proj_w, L0_attn_ln_w, L0_attn_ln_b, L0_ffn_gate_w, L0_ffn_gate_bias, L0_ffn_Wg, L0_ffn_Wu, L0_ffn_Wd, L0_ffn_Sg, L0_ffn_Su, L0_ffn_Sd, L1_attn_W_in, L1_attn_W_alpha, L1_attn_b_alpha, L1_attn_W_beta, L1_attn_b_beta, L1_attn_W_v, L1_attn_b_v, L1_attn_W_out, L1_ffn_wqkv, L1_ffn_q_scale, L1_ffn_k_scale, L1_ffn_wo, L1_ffn_ln_g, L1_ffn_ln_b, L1_ffn_w1, L1_ffn_b1, L1_ffn_w2, L1_ffn_b2):

    def _L0_attn_ref(x, in_proj_w, conv_w, conv_b, x_proj_w, dt_proj_w, dt_proj_b, A_log, Dskip, out_proj_w, ln_w, ln_b):
        import jax, jax.numpy as jnp
        import numpy as np
        N_LAYERS = 2
        D_MODEL = 128
        D_STATE = 16
        D_CONV = 4
        EXPAND = 2
        D_INNER = EXPAND * D_MODEL
        DT_RANK = (D_MODEL + 15) // 16
        B, T = (2, 128)
        LN_EPS = 1e-05

        def _layer_norm(x, w, b):
            mu = jnp.mean(x, axis=-1, keepdims=True)
            xc = x - mu
            var = jnp.mean(xc * xc, axis=-1, keepdims=True)
            return xc * jax.lax.rsqrt(var + LN_EPS) * w + b

        def _mamba_layer(x, in_w, cw, cb, xp_w, dt_w, dt_b, A_log, Dskip, out_w):
            xz = jnp.einsum('btd,ed->bte', x, in_w)
            xc, z = jnp.split(xz, 2, axis=-1)
            pad = D_CONV - 1
            xpad = jnp.pad(xc, ((0, 0), (pad, 0), (0, 0)))
            Tlen = xc.shape[1]
            conv = sum((xpad[:, k:k + Tlen, :] * cw[:, k] for k in range(D_CONV))) + cb
            u = jax.nn.silu(conv)
            x_dbl = jnp.einsum('btd,ed->bte', u, xp_w)
            dt, Bm, Cm = jnp.split(x_dbl, [DT_RANK, DT_RANK + D_STATE], axis=-1)
            dt = jax.nn.softplus(jnp.einsum('btr,dr->btd', dt, dt_w) + dt_b)
            A = -jnp.exp(A_log)

            def step(h, inp):
                dt_t, B_t, C_t, u_t = inp
                dA = jnp.exp(dt_t[:, :, None] * A)
                h = dA * h + (dt_t * u_t)[:, :, None] * B_t[:, None, :]
                y = jnp.einsum('bdn,bn->bd', h, C_t)
                return (h, y)
            h0 = jnp.zeros((x.shape[0], D_INNER, D_STATE), x.dtype)
            _, ys = jax.lax.scan(step, h0, (dt.transpose(1, 0, 2), Bm.transpose(1, 0, 2), Cm.transpose(1, 0, 2), u.transpose(1, 0, 2)))
            y = ys.transpose(1, 0, 2) + u * Dskip
            y = y * jax.nn.silu(z)
            return jnp.einsum('bti,oi->bto', y, out_w)
        for l in range(N_LAYERS):
            residual = x
            h = _mamba_layer(x, in_proj_w[l], conv_w[l], conv_b[l], x_proj_w[l], dt_proj_w[l], dt_proj_b[l], A_log[l], Dskip[l], out_proj_w[l])
            h = _layer_norm(h, ln_w[l], ln_b[l])
            x = h + residual
        return x

    def _L0_ffn_ref(hidden_states, gate_w, gate_bias, Wg, Wu, Wd, Sg, Su, Sd):
        import jax, jax.numpy as jnp
        import numpy as np
        H = 128
        I = 88
        E = 64
        TOP_K = 8
        NG = 8
        TOPK_GROUP = 4
        N_SHARED = 2
        ROUTED_SCALE = 2.5
        S_I = I * N_SHARED

        def _route(x, gate_w, gate_bias):
            T = x.shape[0]
            logits = x @ gate_w.T
            scores = jax.nn.sigmoid(logits)
            scores_for_choice = scores + gate_bias[None, :]
            grp = scores_for_choice.reshape(T, NG, E // NG)
            group_scores = jnp.sum(jax.lax.top_k(grp, 2)[0], axis=-1)
            _, gidx = jax.lax.top_k(group_scores, TOPK_GROUP)
            gmask = jnp.zeros((T, NG), dtype=scores.dtype).at[jnp.arange(T)[:, None], gidx].set(1.0)
            emask = jnp.repeat(gmask, E // NG, axis=1)
            masked = jnp.where(emask > 0, scores_for_choice, 0.0)
            _, topk_idx = jax.lax.top_k(masked, TOP_K)
            topk_w = jnp.take_along_axis(scores, topk_idx, axis=1)
            topk_w = topk_w / (jnp.sum(topk_w, axis=-1, keepdims=True) + 1e-20)
            topk_w = topk_w * ROUTED_SCALE
            rw = jnp.zeros((T, E), dtype=scores.dtype).at[jnp.arange(T)[:, None], topk_idx].add(topk_w)
            return rw

        def _mlp(x, gw, uw, dw):
            return jax.nn.silu(x @ gw.T) * (x @ uw.T) @ dw.T
        B, S, _ = hidden_states.shape
        x = hidden_states.reshape(B * S, H)
        rw = _route(x, gate_w, gate_bias)
        expert_out = jax.vmap(lambda gw_, uw_, dw_: _mlp(x, gw_, uw_, dw_))(Wg, Wu, Wd)
        routed = jnp.einsum('eth,te->th', expert_out, rw)
        shared = _mlp(x, Sg, Su, Sd)
        out = (routed + shared).reshape(B, S, H)
        return out

    def _L1_attn_ref(x, W_in, W_alpha, b_alpha, W_beta, b_beta, W_v, b_v, W_out):
        import jax, jax.numpy as jnp
        import numpy as np
        from jax import lax
        B, T, D = (4, 512, 128)

        def _reference_tuple_inner(x, W_in, W_alpha, b_alpha, W_beta, b_beta, W_v, b_v, W_out):
            xp = jax.nn.silu(jnp.einsum('btd,ed->bte', x, W_in))
            alpha = jax.nn.sigmoid(jnp.einsum('bte,fe->btf', xp, W_alpha) + b_alpha)
            beta = jax.nn.sigmoid(jnp.einsum('bte,fe->btf', xp, W_beta) + b_beta)
            v = jnp.tanh(jnp.einsum('bte,fe->btf', xp, W_v) + b_v)
            bv = beta * v

            def step(h, ab):
                a_t, bv_t = ab
                h = a_t * h + bv_t
                return (h, h * jax.nn.silu(h))
            h0 = jnp.zeros((x.shape[0], W_alpha.shape[0]), dtype=x.dtype)
            h_last, outs = lax.scan(step, h0, (alpha.transpose(1, 0, 2), bv.transpose(1, 0, 2)))
            cell_out = outs.transpose(1, 0, 2)
            output = jnp.einsum('btf,df->btd', cell_out, W_out)
            return (output, h_last)
        return _reference_tuple_inner(x, W_in, W_alpha, b_alpha, W_beta, b_beta, W_v, b_v, W_out)[0]

    def _L1_ffn_ref(x, wqkv, q_scale, k_scale, wo, ln_g, ln_b, w1, b1, w2, b2):
        import jax, jax.numpy as jnp
        import numpy as np
        DIM = 128
        DEPTH = 2
        HEADS = 8
        DIM_HEAD = 64
        WINDOW = 64
        INNER = HEADS * DIM_HEAD
        HID = int(DIM * 4 * 2 / 3)
        B, N = (2, 1024)
        QK_SCALE = 8.0

        def shift_token(t):
            t1, t2 = jnp.split(t, 2, axis=-1)
            t2 = jnp.pad(t2, ((0, 0), (1, 0), (0, 0)))[:, :-1]
            return jnp.concatenate([t1, t2], axis=-1)

        def l2norm(t):
            return t / jnp.clip(jnp.linalg.norm(t, axis=-1, keepdims=True), 1e-12)

        def rotate_half(x):
            x1, x2 = jnp.split(x, 2, axis=-1)
            return jnp.concatenate([-x2, x1], axis=-1)

        def rotary_xpos(q, k):
            n = q.shape[-2]
            half_idx = jnp.arange(0, DIM_HEAD, 2, dtype=jnp.float32)
            inv_freq = 1.0 / 10000.0 ** (half_idx / DIM_HEAD)
            t = jnp.arange(n, dtype=jnp.float32)
            freqs = t[:, None] * inv_freq[None, :]
            freqs = jnp.concatenate([freqs, freqs], axis=-1)
            base = (half_idx + 0.4 * DIM_HEAD) / (1.4 * DIM_HEAD)
            power = (t - n // 2) / float(WINDOW // 2)
            scale = base[None, :] ** power[:, None]
            scale = jnp.concatenate([scale, scale], axis=-1)
            cos, sin = (jnp.cos(freqs), jnp.sin(freqs))
            q = q * cos * scale + rotate_half(q) * sin * scale
            k = k * cos / scale + rotate_half(k) * sin / scale
            return (q, k)

        def local_attention(q, k, v):
            b, h, n, d = q.shape
            w = n // WINDOW
            bq = q.reshape(b, h, w, WINDOW, d) * QK_SCALE
            bk = k.reshape(b, h, w, WINDOW, d)
            bv = v.reshape(b, h, w, WINDOW, d)

            def look_around(t):
                p = jnp.pad(t, ((0, 0), (0, 0), (1, 0), (0, 0), (0, 0)))
                return jnp.concatenate([p[:, :, :w], p[:, :, 1:]], axis=3)
            bk, bv = (look_around(bk), look_around(bv))
            bt = jnp.arange(n).reshape(w, WINDOW)
            btp = jnp.pad(bt, ((1, 0), (0, 0)), constant_values=-1)
            btk = jnp.concatenate([btp[:w], btp[1:]], axis=1)
            sim = jnp.einsum('bhwid,bhwjd->bhwij', bq, bk)
            i = bt[:, :, None]
            j = btk[:, None, :]
            mask = (i < j) | (i > j + WINDOW) | (j == -1)
            sim = jnp.where(mask, -jnp.finfo(sim.dtype).max, sim)
            attn = jax.nn.softmax(sim, axis=-1)
            out = jnp.einsum('bhwij,bhwjd->bhwid', attn, bv)
            return out.reshape(b, h, n, d)

        def _layer(x, wqkv, qs, ksc, wo, lg, lb, w1, b1, w2, b2):
            b, n, _ = x.shape
            h = shift_token(x)
            qkv = h @ wqkv
            q, k, v = jnp.split(qkv, 3, axis=-1)
            to_heads = lambda t: t.reshape(b, n, HEADS, DIM_HEAD).transpose(0, 2, 1, 3)
            q, k, v = (to_heads(q), to_heads(k), to_heads(v))
            q = l2norm(q) * qs
            k = l2norm(k) * ksc
            q, k = rotary_xpos(q, k)
            o = local_attention(q, k, v)
            o = o.transpose(0, 2, 1, 3).reshape(b, n, INNER)
            x = x + o @ wo
            h = shift_token(x)
            mu = h.mean(-1, keepdims=True)
            var = h.var(-1, keepdims=True)
            h = (h - mu) / jnp.sqrt(var + 1e-05) * lg + lb
            h = h @ w1 + b1
            a, g = jnp.split(h, 2, axis=-1)
            h = a * jax.nn.gelu(g, approximate=False)
            x = x + h @ w2 + b2
            return x
        for l in range(DEPTH):
            x = _layer(x, wqkv[l], q_scale[l], k_scale[l], wo[l], ln_g[l], ln_b[l], w1[l], b1[l], w2[l], b2[l])
        return x
    x = L0_attn_x
    x = x + 0.5 * _L0_ffn_ref(_layernorm(x, axis=-1), L0_ffn_gate_w, L0_ffn_gate_bias, L0_ffn_Wg, L0_ffn_Wu, L0_ffn_Wd, L0_ffn_Sg, L0_ffn_Su, L0_ffn_Sd)
    x = x + _L0_attn_ref(_layernorm(x, axis=-1), L0_attn_in_proj_w, L0_attn_conv_w, L0_attn_conv_b, L0_attn_x_proj_w, L0_attn_dt_proj_w, L0_attn_dt_proj_b, L0_attn_A_log, L0_attn_Dskip, L0_attn_out_proj_w, L0_attn_ln_w, L0_attn_ln_b)
    x = x + 0.5 * _L0_ffn_ref(_layernorm(x, axis=-1), L0_ffn_gate_w, L0_ffn_gate_bias, L0_ffn_Wg, L0_ffn_Wu, L0_ffn_Wd, L0_ffn_Sg, L0_ffn_Su, L0_ffn_Sd)
    x = x + 0.5 * _L1_ffn_ref(_layernorm(x, axis=-1), L1_ffn_wqkv, L1_ffn_q_scale, L1_ffn_k_scale, L1_ffn_wo, L1_ffn_ln_g, L1_ffn_ln_b, L1_ffn_w1, L1_ffn_b1, L1_ffn_w2, L1_ffn_b2)
    x = x + _L1_attn_ref(_layernorm(x, axis=-1), L1_attn_W_in, L1_attn_W_alpha, L1_attn_b_alpha, L1_attn_W_beta, L1_attn_b_beta, L1_attn_W_v, L1_attn_b_v, L1_attn_W_out)
    x = x + 0.5 * _L1_ffn_ref(_layernorm(x, axis=-1), L1_ffn_wqkv, L1_ffn_q_scale, L1_ffn_k_scale, L1_ffn_wo, L1_ffn_ln_g, L1_ffn_ln_b, L1_ffn_w1, L1_ffn_b1, L1_ffn_w2, L1_ffn_b2)
    return x

_drawn_inputs = setup_inputs


def setup_inputs(seed=0):
    import zlib

    import numpy as np

    out = dict(_drawn_inputs(seed))
    spreads = {'L0_attn_conv_b': (0.0, 0.1),
     'L0_attn_dt_proj_b': (-4.599999904632568, 0.6),
     'L0_attn_Dskip': (1.0, 0.2),
     'L0_attn_ln_w': (1.0, 0.2),
     'L0_attn_ln_b': (0.0, 0.1),
     'L1_attn_b_alpha': (2.0, 0.2),
     'L1_attn_b_beta': (0.0, 0.1),
     'L1_attn_b_v': (0.0, 0.1),
     'L1_ffn_q_scale': (1.0, 0.6),
     'L1_ffn_k_scale': (1.0, 0.6),
     'L1_ffn_ln_g': (1.0, 0.6),
     'L1_ffn_ln_b': (0.0, 0.8),
     'L1_ffn_b1': (0.0, 0.8),
     'L1_ffn_b2': (0.0, 0.748)}
    factors = {'L0_attn_x_proj_w': 8.0,
     'L0_attn_dt_proj_w': 60.403,
     'L0_attn_A_log': 8.0,
     'L0_ffn_gate_w': 8.0,
     'L0_ffn_gate_bias': 8.0,
     'L0_ffn_Wg': 8.0,
     'L0_ffn_Wu': 8.0,
     'L0_ffn_Wd': 8.0,
     'L0_ffn_Sg': 8.0,
     'L0_ffn_Su': 8.0,
     'L0_ffn_Sd': 8.0,
     'L1_ffn_wqkv': 4.774,
     'L1_ffn_wo': 4.681,
     'L1_ffn_w1': 8.0,
     'L1_ffn_w2': 8.0}
    for name, (base, spread) in spreads.items():
        noise = np.random.default_rng([zlib.crc32(name.encode()), seed]).standard_normal(out[name].shape)
        drawn = base * np.exp(spread * noise) if base else spread * noise
        out[name] = jnp.asarray(drawn.astype(out[name].dtype))
    for name, factor in factors.items():
        out[name] = (out[name] * factor).astype(out[name].dtype)
    return out
```

```python
from contextlib import ExitStack

import concourse.bass as bass
from concourse import mybir

P = 128
B, T = 8, 512
N = B * T
TB = T // P
NT = N // P

E, I_MOE, TOP_K, NG, KEEP_G = 64, 88, 8, 8, 4
EG = E // NG
E_ALL = E + 2
ROUTED_SCALE = 2.5

DI, DS, DR = 256, 16, 8
HALF = DI // P
PAD = 3

HEADS, DH, WIN = 8, 64, 64
PAIRS = HEADS // 2
NW = T // WIN
HID = 341
HB = [128, 128, 85]
QK_SCALE = 8.0
LN_EPS = 1e-5
MASKED = -1e30

F32 = mybir.dt.float32
BF16 = mybir.dt.bfloat16
U32 = mybir.dt.uint32
ALU = mybir.AluOpType
ACT = mybir.ActivationFunctionType
AX_X = mybir.AxisListType.X
CREDIT = 16


def offsets(parts):
    out, at = {}, 0
    for name, width in parts:
        out[name] = (at, at + width)
        at += width
    out["total"] = at
    return out


MAMBA_PACK = offsets([("in_w", 2 * DI), ("xp_w", HALF * 40), ("dt_w", DI), ("out_w", HALF * P), ("conv_w", HALF * 4),
                      ("conv_b", HALF), ("dt_b", HALF), ("A_log", HALF * DS), ("D", HALF), ("ln_w", 1), ("ln_b", 1)])
CELL_PACK = offsets([("w_in", P), ("w_a", P), ("w_b", P), ("w_v", P), ("w_out", P), ("b_a", 1), ("b_b", 1), ("b_v", 1)])
FFN_PACK = offsets([("wq", 512), ("wqr", 512), ("wk", 512), ("wkr", 512), ("wv", 512), ("wo", 512), ("w1", 2 * HID),
                    ("w2", 3 * P), ("b1", 6), ("ln_g", 1), ("ln_b", 1), ("b2", 1),
                    ("qs", 1), ("qsr", 1), ("ks", 1), ("ksr", 1)])
CONST_PACK = offsets([("ident", P), ("mean", P), ("heads", P), ("tri", NG * NG), ("mask", T), ("mask0", T),
                      ("cos_q", T), ("sin_q", T), ("cos_k", T), ("sin_k", T), ("sel", 2 * DS * P)])


class Step:

    def __init__(self, sem, inc=1):
        self.sem, self.inc, self.base, self.per = sem, inc, CREDIT, 0

    def start(self, per):
        self.per = per * self.inc

    def at(self, i, k):
        return i * self.per + (self.base + k * self.inc)

    def end(self, iterations):
        self.base += iterations * self.per


class Program:
    def __init__(self, nc, ctx):
        self.nc, self.ctx, self.steps = nc, ctx, {}

    def step(self, name, per, inc=1):
        if name not in self.steps:
            self.steps[name] = Step(self.ctx.enter_context(self.nc.semaphore(name)), inc)
        self.steps[name].start(per)
        return self.steps[name]

    def sb(self, name, shape, dt=F32, ctx=None):
        return (ctx or self.ctx).enter_context(self.nc.sbuf_tensor(name, shape, dt))


def cols(t, i):
    return t[:, bass.ds(i * T, T)]


def layer_norm_phase(pr, tag, src, dst):
    nc = pr.nc
    with ExitStack() as ctx:
        xc = pr.sb(f"xc{tag}", [P, 2, T], ctx=ctx)
        sq = pr.sb(f"sq{tag}", [P, 2, T], ctx=ctx)
        sd = pr.sb(f"sd{tag}", [P, 2, T], ctx=ctx)
        rs = pr.sb(f"rs{tag}", [P, 2, T], ctx=ctx)
        ps = pr.psum
        mean = pr.step("ln_mean", 2)
        centered = pr.step("ln_centered", 2)
        squared = pr.step("ln_squared", 2)
        var = pr.step("ln_var", 2)
        root = pr.step("ln_root", 2)
        inv = pr.step("ln_inv", 2)
        normed = pr.step("ln_normed", 2)
        n = B // 2
        block = ctx.enter_context(nc.Block())

        @block.tensor
        def _(pe):
            with pe.Fori(0, n) as i:
                for s in range(2):
                    pe.wait_ge(centered.sem, centered.at(i, s - 1))
                    pe.matmul(ps[:, s, :], lhsT=pr.mean[:, :], rhs=cols(src, 2 * i + s), start=True,
                              stop=True).then_inc(mean.sem, 1)
                for s in range(2):
                    pe.wait_ge(squared.sem, squared.at(i, s + 1))
                    pe.wait_ge(root.sem, root.at(i, s - 1))
                    pe.matmul(ps[:, 2 + s, :], lhsT=pr.mean[:, :], rhs=sq[:, s, :], start=True,
                              stop=True).then_inc(var.sem, 1)

        @block.scalar
        def _(act):
            with act.Fori(0, n) as i:
                for s in range(2):
                    act.wait_ge(centered.sem, centered.at(i, s + 1))
                    act.wait_ge(var.sem, var.at(i, s - 1))
                    act.activation(sq[:, s, :], xc[:, s, :], ACT.Square).then_inc(squared.sem, 1)
                for s in range(2):
                    act.wait_ge(var.sem, var.at(i, s + 1))
                    act.wait_ge(inv.sem, inv.at(i, s - 1))
                    act.activation(sd[:, s, :], ps[:, 2 + s, :], ACT.Sqrt, bias=pr.eps[:, 0:1]).then_inc(root.sem, 1)

        @block.vector
        def _(dve):
            with dve.Fori(0, n) as i:
                for s in range(2):
                    dve.wait_ge(mean.sem, mean.at(i, s + 1))
                    dve.wait_ge(squared.sem, squared.at(i, s - 1))
                    dve.wait_ge(normed.sem, normed.at(i, s - 1))
                    dve.tensor_tensor(xc[:, s, :], cols(src, 2 * i + s), ps[:, s, :],
                                      ALU.subtract).then_inc(centered.sem, 1)
                for s in range(2):
                    dve.wait_ge(root.sem, root.at(i, s + 1))
                    dve.wait_ge(normed.sem, normed.at(i, s - 1))
                    dve.reciprocal(rs[:, s, :], sd[:, s, :]).then_inc(inv.sem, 1)
                    dve.wait_ge(inv.sem, inv.at(i, s + 1))
                    dve.tensor_tensor(cols(dst, 2 * i + s), xc[:, s, :], rs[:, s, :],
                                      ALU.mult).then_inc(normed.sem, 1)

        for s in (mean, centered, squared, var, root, inv, normed):
            s.end(n)


def moe_phase(pr, tag, gate_w, gate_b, experts):
    nc, ps, X, XN = pr.nc, pr.psum, pr.X, pr.XN
    W_COLS = 2 * I_MOE + P
    with ExitStack() as ctx:
        gw = pr.sb(f"gw{tag}", [P, E], ctx=ctx)
        gb = pr.sb(f"gb{tag}", [P, E], ctx=ctx)
        RW = pr.sb(f"RW{tag}", [P, NT, E_ALL], ctx=ctx)
        with ExitStack() as rctx:
            score = pr.sb(f"score{tag}", [P, NT, E], ctx=rctx)
            choice = pr.sb(f"choice{tag}", [P, NT, E], ctx=rctx)
            ta = pr.sb(f"ta{tag}", [P, NT * E], ctx=rctx)
            tb = pr.sb(f"tb{tag}", [P, NT * E], ctx=rctx)
            top = pr.sb(f"top{tag}", [P, NT, 8], ctx=rctx)
            gs = pr.sb(f"gs{tag}", [P, NT, NG], ctx=rctx)
            rank = pr.sb(f"rank{tag}", [P, NT, NG], ctx=rctx)
            tot = pr.sb(f"tot{tag}", [P, NT], ctx=rctx)
            G = NT // 4
            gate_in = pr.step("gate_in", 2, 16)
            logits = pr.step("logits", 4)
            scored = pr.step("scored", 4)
            route = pr.step("route", 400)
            with nc.Block() as block:
                @block.sync
                def _(sp):
                    sp.dma_start(gw[:, :], gate_w).then_inc(gate_in.sem, 16)
                    sp.dma_start(gb[:, :], gate_b).then_inc(gate_in.sem, 16)

                @block.tensor
                def _(pe):
                    pe.wait_ge(gate_in.sem, gate_in.at(0, 2))
                    for g in range(4):
                        for t in range(G):
                            m = (g * G + t) * P
                            last = pe.matmul(ps[:, g, t * E:(t + 1) * E], lhsT=XN[:, m:m + P], rhs=gw[:, :],
                                             start=True, stop=True)
                        last.then_inc(logits.sem, 1)

                @block.scalar
                def _(act):
                    for g in range(4):
                        act.wait_ge(logits.sem, logits.at(0, g + 1))
                        act.activation(score[:, g * G:(g + 1) * G, :].rearrange("p t e -> p (t e)"), ps[:, g, :],
                                       ACT.Sigmoid).then_inc(scored.sem, 1)

                @block.vector
                def _(dve):
                    count = [0]

                    def then(ins):
                        count[0] += 1
                        ins.then_inc(route.sem, 1)
                        dve.wait_ge(route.sem, route.at(0, count[0]))

                    def tt(out, a, b, op):
                        then(dve.tensor_tensor(out, a, b, op))

                    dve.wait_ge(scored.sem, scored.at(0, 4))
                    dve.wait_ge(gate_in.sem, gate_in.at(0, 2))
                    tt(choice[:, :, :], score[:, :, :], gb[:, :].unsqueeze(1).to_broadcast([P, NT, E]), ALU.add)
                    c = choice[:, :, :].rearrange("p t (g j) -> p (t g) j", j=EG)
                    M = NT * NG
                    h1 = ta[:, 0:4 * M].rearrange("p (q j) -> p q j", j=4)
                    l1 = ta[:, 4 * M:8 * M].rearrange("p (q j) -> p q j", j=4)
                    tt(h1, c[:, :, 0:4], c[:, :, 4:8], ALU.max)
                    tt(l1, c[:, :, 0:4], c[:, :, 4:8], ALU.min)
                    v = [tb[:, 2 * M * k:2 * M * (k + 1)].rearrange("p (q j) -> p q j", j=2) for k in range(4)]
                    tt(v[0], h1[:, :, 0:2], h1[:, :, 2:4], ALU.max)
                    tt(v[1], h1[:, :, 0:2], h1[:, :, 2:4], ALU.min)
                    tt(v[2], l1[:, :, 0:2], l1[:, :, 2:4], ALU.max)
                    tt(v[3], v[1], v[2], ALU.max)
                    w = [ta[:, M * k:M * (k + 1)] for k in range(4)]
                    a, b = v[0], v[3]
                    tt(w[0], a[:, :, 0], a[:, :, 1], ALU.max)
                    tt(w[1], a[:, :, 0], a[:, :, 1], ALU.min)
                    tt(w[2], b[:, :, 0], b[:, :, 1], ALU.max)
                    tt(w[3], w[1], w[2], ALU.max)
                    gsf = gs[:, :, :].rearrange("p t g -> p (t g)")
                    tt(gsf, w[0], w[3], ALU.add)
                    shape = [P, NT, NG, NG]
                    other = gs[:, :, :].unsqueeze(2).to_broadcast(shape)
                    own = gs[:, :, :].unsqueeze(3).to_broadcast(shape)
                    above = ta[:, :].rearrange("p (t g j) -> p t g j", g=NG, j=NG)
                    equal = tb[:, :].rearrange("p (t g j) -> p t g j", g=NG, j=NG)
                    tt(above, other, own, ALU.is_gt)
                    tt(equal, other, own, ALU.is_equal)
                    tt(tb[:, :].rearrange("p (t x) -> p t x", t=NT), tb[:, :].rearrange("p (t x) -> p t x", t=NT),
                       pr.tri[:, :].unsqueeze(1).to_broadcast([P, NT, NG * NG]), ALU.mult)
                    tt(ta[:, :], ta[:, :], tb[:, :], ALU.add)
                    then(dve.tensor_reduce(rank[:, :, :].rearrange("p t g -> p (t g)"),
                                           ta[:, :].rearrange("p (q j) -> p q j", j=NG), AX_X, ALU.add))
                    then(dve.tensor_scalar(gs[:, :, :], rank[:, :, :], float(KEEP_G), None, ALU.is_lt))
                    masked = ta[:, :].rearrange("p (q j) -> p q j", j=EG)
                    tt(masked, c, gsf.unsqueeze(2).to_broadcast([P, NT * NG, EG]), ALU.mult)
                    for t in range(NT):
                        mt = ta[:, t * E:(t + 1) * E]
                        last = dve.max(top[:, t, :], mt)
                        last.then_inc(route.sem, 1)
                        count[0] += 1
                    dve.wait_ge(route.sem, route.at(0, count[0]))
                    for t in range(NT):
                        mt = ta[:, t * E:(t + 1) * E]
                        last = dve.match_replace(tb[:, t * E:(t + 1) * E], top[:, t, :], mt, MASKED)
                        last.then_inc(route.sem, 1)
                        count[0] += 1
                    dve.wait_ge(route.sem, route.at(0, count[0]))
                    tt(ta[:, :], ta[:, :], tb[:, :], ALU.not_equal)
                    tat = ta[:, :].rearrange("p (t e) -> p t e", e=E)
                    tt(tat, tat, score[:, :, :], ALU.mult)
                    then(dve.tensor_reduce(tot[:, :], tat, AX_X, ALU.add))
                    then(dve.tensor_scalar(tot[:, :], tot[:, :], 1e-20, None, ALU.add))
                    then(dve.reciprocal(tot[:, :], tot[:, :]))
                    then(dve.tensor_scalar(tot[:, :], tot[:, :], 0.5 * ROUTED_SCALE, None, ALU.mult))
                    then(dve.memset(RW[:, :, E:E_ALL], 0.5))
                    route.start(count[0] + 1)
                    tt(RW[:, :, 0:E], tat, tot[:, :].unsqueeze(2).to_broadcast([P, NT, E]), ALU.mult)

            for s in (gate_in, logits, scored, route):
                s.end(1)

        w = pr.sb(f"w{tag}", [P, 2, W_COLS], ctx=ctx)
        acc = pr.sb(f"acc{tag}", [P, NT, P], ctx=ctx)
        sg = pr.sb(f"sg{tag}", [P, 2, T], ctx=ctx)
        h = pr.sb(f"h{tag}", [P, 2, T], ctx=ctx)
        R = 2 * B
        w_in = [pr.step("w_in_a", 1, 16), pr.step("w_in_b", 1, 16)]
        gate_up = pr.step("gate_up", R)
        silu = pr.step("silu", R)
        hidden = pr.step("hidden", R)
        down = pr.step("down", R)
        summed = pr.step("summed", R)
        zeroed = pr.step("zeroed", 1)
        n = E_ALL // 2
        with nc.Block() as block:
            @block.sync
            def _(sp):
                with sp.Fori(0, n) as i:
                    for s in range(2):
                        sp.wait_ge(down.sem, down.at(i, (s - 1) * B))
                        sp.dma_start(w[:, s, :], experts[bass.ds(2 * i + s, 1), :, :].rearrange(
                            "e p n -> (e p) n")).then_inc(w_in[s].sem, 16)

            @block.tensor
            def _(pe):
                def gate_and_up(i, k):
                    s, b = k // B, k % B
                    if b == 0:
                        pe.wait_ge(w_in[s].sem, w_in[s].at(i, 1))
                    pe.wait_ge(silu.sem, silu.at(i, k - 1))
                    pe.wait_ge(hidden.sem, hidden.at(i, k - 1))
                    x = XN[:, b * T:(b + 1) * T]
                    pe.matmul(ps[0:I_MOE, k % 2, :], lhsT=w[:, s, 0:I_MOE], rhs=x, start=True, stop=True)
                    pe.matmul(ps[0:I_MOE, 2 + k % 2, :], lhsT=w[:, s, I_MOE:2 * I_MOE], rhs=x, start=True,
                              stop=True).then_inc(gate_up.sem, 1)

                def down_product(i, k):
                    s = k // B
                    pe.wait_ge(hidden.sem, hidden.at(i, k + 1))
                    pe.wait_ge(summed.sem, summed.at(i, k - 1))
                    for t in range(TB):
                        last = pe.matmul(ps[:, 4 + k % 2, t * P:(t + 1) * P],
                                         lhsT=h[0:I_MOE, k % 2, t * P:(t + 1) * P],
                                         rhs=w[0:I_MOE, s, 2 * I_MOE:], start=True, stop=True)
                    last.then_inc(down.sem, 1)

                with pe.Fori(0, n) as i:
                    for k in range(R):
                        gate_and_up(i, k)
                        if k:
                            down_product(i, k - 1)
                    down_product(i, R - 1)

            @block.scalar
            def _(act):
                with act.Fori(0, n) as i:
                    for k in range(R):
                        act.wait_ge(gate_up.sem, gate_up.at(i, k + 1))
                        act.wait_ge(hidden.sem, hidden.at(i, k - 1))
                        act.activation(sg[0:I_MOE, k % 2, :], ps[0:I_MOE, k % 2, :], ACT.Silu).then_inc(silu.sem, 1)

            @block.gpsimd
            def _(pool):
                pool.memset(acc[:, :, :], 0.0).then_inc(zeroed.sem, 1)

            @block.vector
            def _(dve):
                dve.wait_ge(zeroed.sem, zeroed.at(0, 1))

                def multiply(i, k):
                    dve.wait_ge(silu.sem, silu.at(i, k + 1))
                    dve.wait_ge(down.sem, down.at(i, k - 1))
                    dve.tensor_tensor(h[0:I_MOE, k % 2, :], ps[0:I_MOE, 2 + k % 2, :], sg[0:I_MOE, k % 2, :],
                                      ALU.mult).then_inc(hidden.sem, 1)

                def add(i, k):
                    s, b = k // B, k % B
                    dve.wait_ge(down.sem, down.at(i, k + 1))
                    dve.wait_ge(summed.sem, summed.at(i, k + 1 - B))
                    for t in range(TB):
                        m = b * TB + t
                        last = dve.scalar_tensor_tensor(
                            out=acc[:, m, :], in0=ps[:, 4 + k % 2, t * P:(t + 1) * P],
                            scalar=RW[:, m, bass.ds(2 * i + s, 1)], in1=acc[:, m, :], op0=ALU.mult, op1=ALU.add)
                    last.then_inc(summed.sem, 1)

                with dve.Fori(0, n) as i:
                    for k in range(R):
                        multiply(i, k)
                        if k:
                            add(i, k - 1)
                    add(i, R - 1)

        for s in (*w_in, gate_up, silu, hidden, down, summed):
            s.end(n)
        zeroed.end(1)

        turned = pr.step("turned", B)
        added = pr.step("added", B)
        with nc.Block() as block:
            @block.tensor
            def _(pe):
                for b in range(B):
                    pe.wait_ge(added.sem, added.at(0, b - 1))
                    for t in range(TB):
                        last = pe.transpose(ps[:, b % 2, t * P:(t + 1) * P], acc[:, b * TB + t, :], pr.ident[:, :])
                    last.then_inc(turned.sem, 1)

            @block.vector
            def _(dve):
                for b in range(B):
                    dve.wait_ge(turned.sem, turned.at(0, b + 1))
                    x = X[:, b * T:(b + 1) * T]
                    dve.tensor_tensor(x, x, ps[:, b % 2, :], ALU.add).then_inc(added.sem, 1)

        turned.end(1)
        added.end(1)


def mamba_layer(pr, tag, packed):
    nc, ps, XR = pr.nc, pr.psum, pr.XN
    o = MAMBA_PACK
    with ExitStack() as ctx:
        def sb(name, shape, dt=F32):
            return pr.sb(name + tag, shape, dt, ctx)

        W = sb("mw", [P, o["total"]])

        def part(name):
            return W[:, o[name][0]:o[name][1]]

        in_w, out_w = part("in_w"), part("out_w").rearrange("p (h n) -> p h n", h=HALF)
        xp_w = part("xp_w").rearrange("p (h n) -> p h n", h=HALF)
        dt_w = W[32:32 + DR, o["dt_w"][0]:o["dt_w"][1]]
        conv_w = part("conv_w").rearrange("p (h k) -> p h k", h=HALF)
        conv_b, dt_b, ln_w, ln_b = part("conv_b"), part("dt_b"), part("ln_w"), part("ln_b")
        skip_d = part("D")
        A = sb("A", [P, HALF, DS])
        diag = sb("diag", [P, HALF, P])
        xp = sb("xp", [P, HALF, PAD + T])
        cv = sb("cv", [P, HALF, T])
        u = sb("u", [P, HALF, T])
        sz = sb("sz", [P, HALF, T])
        dts = sb("dts", [40, T])
        r1 = sb("r1", [32, T])
        r2 = sb("r2", [32, T])
        mid = sb("mid", [32, T], BF16)
        bc = sb("bc", [96, T], BF16)
        av = sb("av", [P, HALF, T])
        dt = sb("dt", [P, HALF, T])
        dtu = sb("dtu", [P, HALF, T])
        dA = sb("dA", [P, 2, HALF, T])
        Bs = sb("Bs", [P, 2, T])
        dBu = sb("dBu", [P, 2, HALF, T])
        hh = sb("hh", [P, 2, HALF, T])
        hc = sb("hc", [P, 2, HALF, T])
        yz = sb("yz", [P, HALF, T])
        ob = sb("ob", [P, T])
        oc = sb("oc", [P, T])
        osq = sb("osq", [P, T])
        osd = sb("osd", [P, T])

        packed_in = pr.step("m_packed", 1, 16)
        ready = pr.step("m_ready", 6)
        with nc.Block() as block:
            @block.sync
            def _(sp):
                sp.dma_start(W[:, :], packed).then_inc(packed_in.sem, 16)

            @block.scalar
            def _(act):
                act.wait_ge(packed_in.sem, packed_in.at(0, 1))
                act.activation(A[:, :, :].rearrange("p h n -> p (h n)"), part("A_log"), ACT.Exp).then_inc(ready.sem, 1)

            @block.vector
            def _(dve):
                dve.memset(xp[:, :, 0:PAD], 0.0).then_inc(ready.sem, 1)
                dve.memset(dA[:, :, :, 0:1], 0.0).then_inc(ready.sem, 1)
                dve.wait_ge(packed_in.sem, packed_in.at(0, 1))
                for f in range(HALF):
                    dve.tensor_scalar(diag[:, f, :], pr.ident[:, :], skip_d[:, f:f + 1], None,
                                      ALU.mult).then_inc(ready.sem, 1)
                dve.wait_ge(ready.sem, ready.at(0, 5))
                dve.tensor_scalar(A[:, :, :], A[:, :, :], -1.0, None, ALU.mult).then_inc(ready.sem, 1)
        packed_in.end(1)
        ready.end(1)

        xz = pr.step("m_xz", 4)
        xpc = pr.step("m_xp_copied", 2)
        szd = pr.step("m_silu_z", 2)
        conv = pr.step("m_conv", 8)
        ud = pr.step("m_u", 2)
        dbl = pr.step("m_x_dbl", 1)
        split = pr.step("m_split", 7)
        dtp = pr.step("m_dt_proj", 1)
        absd = pr.step("m_abs", 1)
        expd = pr.step("m_softplus_exp", 1)
        lnd = pr.step("m_softplus_log", 1)
        dmax = pr.step("m_dt_relu", 1)
        dtd = pr.step("m_dt", 1)
        dtud = pr.step("m_dtu", 1)
        bcast = pr.step("m_bc_spread", DS)
        decay = pr.step("m_decay", DS)
        bcopy = pr.step("m_b_copied", DS)
        driven = pr.step("m_driven", DS)
        scanned = pr.step("m_scanned", DS)
        read = pr.step("m_state_read", DS)
        ysum = pr.step("m_y_summed", DS + 1)
        gated = pr.step("m_gated", 1)
        outp = pr.step("m_out", 1)
        ocopy = pr.step("m_out_copied", 1)
        omean = pr.step("m_mean", 1)
        ocent = pr.step("m_centered", 1)
        osqd = pr.step("m_squared", 1)
        ovar = pr.step("m_var", 1)
        oroot = pr.step("m_root", 1)
        oinv = pr.step("m_inv", 3)
        fin = pr.step("m_done", 1)

        with nc.Block() as block:
            @block.tensor
            def _(pe):
                with pe.Fori(0, B) as i:
                    pe.wait_ge(fin.sem, fin.at(i, 0))
                    for c in range(4):
                        pe.matmul(ps[:, c, :], lhsT=in_w[:, c * P:(c + 1) * P], rhs=cols(XR, i), start=True,
                                  stop=True).then_inc(xz.sem, 1)
                    pe.wait_ge(ud.sem, ud.at(i, 2))
                    for f in range(HALF):
                        last = pe.matmul(ps[0:40, 4, :], lhsT=xp_w[:, f, :], rhs=u[:, f, :], start=(f == 0),
                                         stop=(f == HALF - 1))
                    last.then_inc(dbl.sem, 1)
                    pe.wait_ge(split.sem, split.at(i, 1))
                    for f in range(HALF):
                        last = pe.matmul(ps[:, 5 + f, :], lhsT=dt_w[:, f * P:(f + 1) * P], rhs=dts[32:40, :],
                                         start=True, stop=True)
                    last.then_inc(dtp.sem, 1)
                    for f in range(HALF):
                        last = pe.matmul(ps[:, f, :], lhsT=diag[:, f, :], rhs=u[:, f, :], start=True, stop=False)
                    last.then_inc(ysum.sem, 1)
                    pe.wait_ge(szd.sem, szd.at(i, 2))
                    pe.wait_ge(split.sem, split.at(i, 7))

                    def spread(n):
                        if n >= 2:
                            pe.wait_ge(bcopy.sem, bcopy.at(i, n - 1))
                            pe.wait_ge(read.sem, read.at(i, n - 1))
                        pe.matmul(ps[:, 2 + n % 2, :], lhsT=pr.sel[:, n, :], rhs=bc[:, :], start=True, stop=True)
                        pe.matmul(ps[:, 4 + n % 2, :], lhsT=pr.sel[:, DS + n, :], rhs=bc[:, :], start=True,
                                  stop=True).then_inc(bcast.sem, 1)

                    def sum_y(n):
                        pe.wait_ge(read.sem, read.at(i, n + 1))
                        for f in range(HALF):
                            last = pe.matmul(ps[:, f, :], lhsT=pr.ident[:, :], rhs=hc[:, n % 2, f, :], start=False,
                                             stop=(n == DS - 1))
                        last.then_inc(ysum.sem, 1)

                    pe.wait_ge(dmax.sem, dmax.at(i, 1))
                    pe.wait_ge(absd.sem, absd.at(i, 1))
                    spread(0)
                    for n in range(DS):
                        if n + 1 < DS:
                            spread(n + 1)
                        sum_y(n)
                    pe.wait_ge(gated.sem, gated.at(i, 1))
                    for f in range(HALF):
                        last = pe.matmul(ps[:, 6, :], lhsT=out_w[:, f, :], rhs=yz[:, f, :], start=(f == 0),
                                         stop=(f == HALF - 1))
                    last.then_inc(outp.sem, 1)
                    pe.wait_ge(ocopy.sem, ocopy.at(i, 1))
                    pe.matmul(ps[:, 7, :], lhsT=pr.mean[:, :], rhs=ob[:, :], start=True, stop=True).then_inc(omean.sem, 1)
                    pe.wait_ge(osqd.sem, osqd.at(i, 1))
                    pe.matmul(ps[:, 6, :], lhsT=pr.mean[:, :], rhs=osq[:, :], start=True, stop=True).then_inc(ovar.sem, 1)

            @block.scalar
            def _(act):
                with act.Fori(0, B) as i:
                    for f in range(HALF):
                        act.wait_ge(xz.sem, xz.at(i, f + 1))
                        if f == 0:
                            act.wait_ge(fin.sem, fin.at(i, 0))
                        act.activation(xp[:, f, PAD:], ps[:, f, :], ACT.Copy).then_inc(xpc.sem, 1)
                    for f in range(HALF):
                        act.wait_ge(xz.sem, xz.at(i, 3 + f))
                        act.activation(sz[:, f, :], ps[:, 2 + f, :], ACT.Silu).then_inc(szd.sem, 1)
                    for f in range(HALF):
                        act.wait_ge(conv.sem, conv.at(i, 4 * HALF - 1 + f))
                        act.activation(u[:, f, :], cv[:, f, :], ACT.Silu).then_inc(ud.sem, 1)
                    act.wait_ge(dtp.sem, dtp.at(i, 1))
                    for f in range(HALF):
                        last = act.activation(av[:, f, :], ps[:, 5 + f, :], ACT.Abs, bias=dt_b[:, f:f + 1])
                    last.then_inc(absd.sem, 1)
                    act.wait_ge(absd.sem, absd.at(i, 1))
                    act.activation(av[:, :, :], av[:, :, :], ACT.Exp, scale=-1.0).then_inc(expd.sem, 1)
                    act.wait_ge(expd.sem, expd.at(i, 1))
                    act.activation(av[:, :, :], av[:, :, :], ACT.Ln, bias=1.0).then_inc(lnd.sem, 1)
                    act.wait_ge(dtd.sem, dtd.at(i, 1))
                    for n in range(DS):
                        s = n % 2
                        if n >= 2:
                            act.wait_ge(scanned.sem, scanned.at(i, n - 1))
                        for f in range(HALF):
                            last = act.activation(dA[:, s, f, 1:], dt[:, f, 1:], ACT.Exp, scale=A[:, f, n:n + 1])
                        last.then_inc(decay.sem, 1)
                        act.wait_ge(bcast.sem, bcast.at(i, n + 1))
                        if n >= 2:
                            act.wait_ge(driven.sem, driven.at(i, n - 1))
                        act.activation(Bs[:, s, :], ps[:, 2 + s, :], ACT.Copy).then_inc(bcopy.sem, 1)
                    act.wait_ge(outp.sem, outp.at(i, 1))
                    act.activation(ob[:, :], ps[:, 6, :], ACT.Copy).then_inc(ocopy.sem, 1)
                    act.wait_ge(ocent.sem, ocent.at(i, 1))
                    act.activation(osq[:, :], oc[:, :], ACT.Square).then_inc(osqd.sem, 1)
                    act.wait_ge(ovar.sem, ovar.at(i, 1))
                    act.activation(osd[:, :], ps[:, 6, :], ACT.Sqrt, bias=pr.eps[:, 0:1]).then_inc(oroot.sem, 1)

            @block.gpsimd
            def _(pool):
                with pool.Fori(0, B) as i:
                    pool.wait_ge(dtud.sem, dtud.at(i, 1))
                    for n in range(DS):
                        s = n % 2
                        pool.wait_ge(bcopy.sem, bcopy.at(i, n + 1))
                        if n >= 2:
                            pool.wait_ge(scanned.sem, scanned.at(i, n - 1))
                        pool.tensor_tensor(dBu[:, s, :, :], dtu[:, :, :],
                                           Bs[:, s, :].unsqueeze(1).to_broadcast([P, HALF, T]),
                                           ALU.mult).then_inc(driven.sem, 1)

            @block.vector
            def _(dve):
                with dve.Fori(0, B) as i:
                    for k in range(4):
                        for f in range(HALF):
                            if k == 0:
                                dve.wait_ge(xpc.sem, xpc.at(i, f + 1))
                                ins = dve.tensor_scalar(cv[:, f, :], xp[:, f, 0:T], conv_w[:, f, 0:1],
                                                        conv_b[:, f:f + 1], ALU.mult, ALU.add)
                            else:
                                dve.wait_ge(conv.sem, conv.at(i, 2 * k + f - 1))
                                ins = dve.scalar_tensor_tensor(out=cv[:, f, :], in0=xp[:, f, k:k + T],
                                                               scalar=conv_w[:, f, k:k + 1], in1=cv[:, f, :],
                                                               op0=ALU.mult, op1=ALU.add)
                            ins.then_inc(conv.sem, 1)
                    dve.wait_ge(dbl.sem, dbl.at(i, 1))
                    dve.tensor_copy(dts[32:40, :], ps[32:40, 4, :]).then_inc(split.sem, 1)
                    dve.tensor_copy(bc[0:32, :], ps[0:32, 4, :]).then_inc(split.sem, 1)
                    dve.wait_ge(split.sem, split.at(i, 2))
                    dve.tensor_tensor(r1[:, :], ps[0:32, 4, :], bc[0:32, :], ALU.subtract).then_inc(split.sem, 1)
                    dve.wait_ge(split.sem, split.at(i, 3))
                    dve.tensor_copy(mid[:, :], r1[:, :]).then_inc(split.sem, 1)
                    dve.tensor_copy(bc[32:64, :], r1[:, :]).then_inc(split.sem, 1)
                    dve.wait_ge(split.sem, split.at(i, 4))
                    dve.tensor_tensor(r2[:, :], r1[:, :], mid[:, :], ALU.subtract).then_inc(split.sem, 1)
                    dve.wait_ge(split.sem, split.at(i, 6))
                    dve.tensor_copy(bc[64:96, :], r2[:, :]).then_inc(split.sem, 1)
                    dve.wait_ge(dtp.sem, dtp.at(i, 1))
                    dve.wait_ge(absd.sem, absd.at(i, 1))
                    for f in range(HALF):
                        last = dve.tensor_scalar(dt[:, f, :], ps[:, 5 + f, :], dt_b[:, f:f + 1], 0.0, ALU.add, ALU.max)
                    last.then_inc(dmax.sem, 1)
                    dve.wait_ge(dmax.sem, dmax.at(i, 1))
                    dve.wait_ge(lnd.sem, lnd.at(i, 1))
                    dve.tensor_tensor(dt[:, :, :], dt[:, :, :], av[:, :, :], ALU.add).then_inc(dtd.sem, 1)
                    dve.wait_ge(dtd.sem, dtd.at(i, 1))
                    dve.wait_ge(ud.sem, ud.at(i, 2))
                    dve.tensor_tensor(dtu[:, :, :], dt[:, :, :], u[:, :, :], ALU.mult).then_inc(dtud.sem, 1)
                    for n in range(DS):
                        s = n % 2
                        dve.wait_ge(decay.sem, decay.at(i, n + 1))
                        dve.wait_ge(driven.sem, driven.at(i, n + 1))
                        if n >= 2:
                            dve.wait_ge(read.sem, read.at(i, n - 1))
                        dve.tensor_tensor_scan(hh[:, s, :, :].rearrange("p h t -> p (h t)"),
                                               dA[:, s, :, :].rearrange("p h t -> p (h t)"),
                                               dBu[:, s, :, :].rearrange("p h t -> p (h t)"), 0.0,
                                               ALU.mult, ALU.add).then_inc(scanned.sem, 1)
                        dve.wait_ge(scanned.sem, scanned.at(i, n + 1))
                        dve.wait_ge(bcast.sem, bcast.at(i, n + 1))
                        if n >= 2:
                            dve.wait_ge(ysum.sem, ysum.at(i, n))
                        dve.tensor_tensor(hc[:, s, :, :], hh[:, s, :, :],
                                          ps[:, 4 + s, :].unsqueeze(1).to_broadcast([P, HALF, T]),
                                          ALU.mult).then_inc(read.sem, 1)
                    dve.wait_ge(ysum.sem, ysum.at(i, DS + 1))
                    dve.wait_ge(szd.sem, szd.at(i, 2))
                    dve.tensor_tensor(yz[:, :, :], ps[:, 0:2, :], sz[:, :, :], ALU.mult).then_inc(gated.sem, 1)
                    dve.wait_ge(omean.sem, omean.at(i, 1))
                    dve.tensor_tensor(oc[:, :], ob[:, :], ps[:, 7, :], ALU.subtract).then_inc(ocent.sem, 1)
                    dve.wait_ge(oroot.sem, oroot.at(i, 1))
                    dve.reciprocal(osd[:, :], osd[:, :]).then_inc(oinv.sem, 1)
                    dve.wait_ge(oinv.sem, oinv.at(i, 1))
                    dve.wait_ge(ocent.sem, ocent.at(i, 1))
                    dve.wait_ge(osqd.sem, osqd.at(i, 1))
                    dve.tensor_tensor(oc[:, :], oc[:, :], osd[:, :], ALU.mult).then_inc(oinv.sem, 1)
                    dve.wait_ge(oinv.sem, oinv.at(i, 2))
                    dve.tensor_scalar(oc[:, :], oc[:, :], ln_w, ln_b, ALU.mult, ALU.add).then_inc(oinv.sem, 1)
                    dve.wait_ge(oinv.sem, oinv.at(i, 3))
                    dve.tensor_tensor(cols(XR, i), cols(XR, i), oc[:, :], ALU.add).then_inc(fin.sem, 1)

        for s in (xz, xpc, szd, conv, ud, dbl, split, dtp, absd, expd, lnd, dmax, dtd, dtud, bcast, decay, bcopy, driven,
                  scanned, read, ysum, gated, outp, ocopy, omean, ocent, osqd, ovar, oroot, oinv, fin):
            s.end(B)


def add_stream(pr, scale):
    nc, added = pr.nc, pr.step("stream_added", B)
    with nc.Block() as block:
        @block.vector
        def _(dve):
            for b in range(B):
                x, y = pr.X[:, b * T:(b + 1) * T], pr.XN[:, b * T:(b + 1) * T]
                dve.scalar_tensor_tensor(out=x, in0=y, scalar=scale, in1=x, op0=ALU.mult,
                                         op1=ALU.add).then_inc(added.sem, 1)
    added.end(1)


def cell_phase(pr, tag, packed):
    nc, ps, X, XN = pr.nc, pr.psum, pr.X, pr.XN
    o = CELL_PACK
    with ExitStack() as ctx:
        def sb(name):
            return pr.sb(name + tag, [P, 2, T], ctx=ctx)

        W = pr.sb("cw" + tag, [P, o["total"]], ctx=ctx)

        def part(name):
            return W[:, o[name][0]:o[name][1]]

        xp, al, be, v, bv, h, sh, co = (sb(x) for x in ("cxp", "cal", "cbe", "cv_", "cbv", "ch", "csh", "cco"))
        w_in = pr.step("c_packed", 1, 16)
        proj = pr.step("c_proj", 2)
        xpd = pr.step("c_xp", 2)
        gates = pr.step("c_gates", 2)
        acts = pr.step("c_acts", 2)
        bvd = pr.step("c_bv", 2)
        scanned = pr.step("c_scanned", 2)
        shd = pr.step("c_silu_h", 2)
        cod = pr.step("c_out", 2)
        outp = pr.step("c_out_proj", 2)
        fin = pr.step("c_done", 2)
        n = B // 2
        with nc.Block() as block:
            @block.sync
            def _(sp):
                sp.dma_start(W[:, :], packed).then_inc(w_in.sem, 16)

            @block.tensor
            def _(pe):
                pe.wait_ge(w_in.sem, w_in.at(0, 1))
                with pe.Fori(0, n) as i:
                    for s in range(2):
                        pe.wait_ge(xpd.sem, xpd.at(i, s - 1))
                        pe.wait_ge(fin.sem, fin.at(i, s - 1))
                        pe.matmul(ps[:, 4 * s, :], lhsT=part("w_in"), rhs=cols(XN, 2 * i + s), start=True,
                                  stop=True).then_inc(proj.sem, 1)
                    for s in range(2):
                        pe.wait_ge(xpd.sem, xpd.at(i, s + 1))
                        pe.wait_ge(acts.sem, acts.at(i, s - 1))
                        for k, name in enumerate(("w_a", "w_b", "w_v")):
                            last = pe.matmul(ps[:, 4 * s + 1 + k, :], lhsT=part(name), rhs=xp[:, s, :], start=True, stop=True)
                        last.then_inc(gates.sem, 1)
                    for s in range(2):
                        pe.wait_ge(cod.sem, cod.at(i, s + 1))
                        pe.matmul(ps[:, 4 * s, :], lhsT=part("w_out"), rhs=co[:, s, :], start=True,
                                  stop=True).then_inc(outp.sem, 1)

            @block.scalar
            def _(act):
                with act.Fori(0, n) as i:
                    for s in range(2):
                        act.wait_ge(proj.sem, proj.at(i, s + 1))
                        act.wait_ge(gates.sem, gates.at(i, s - 1))
                        act.activation(xp[:, s, :], ps[:, 4 * s, :], ACT.Silu).then_inc(xpd.sem, 1)
                    for s in range(2):
                        act.wait_ge(gates.sem, gates.at(i, s + 1))
                        act.wait_ge(scanned.sem, scanned.at(i, s - 1))
                        act.activation(al[:, s, :], ps[:, 4 * s + 1, :], ACT.Sigmoid, bias=part("b_a"))
                        act.activation(be[:, s, :], ps[:, 4 * s + 2, :], ACT.Sigmoid, bias=part("b_b"))
                        act.activation(v[:, s, :], ps[:, 4 * s + 3, :], ACT.Tanh, bias=part("b_v")).then_inc(acts.sem, 1)
                    for s in range(2):
                        act.wait_ge(scanned.sem, scanned.at(i, s + 1))
                        act.wait_ge(cod.sem, cod.at(i, s - 1))
                        act.activation(sh[:, s, :], h[:, s, :], ACT.Silu).then_inc(shd.sem, 1)

            @block.vector
            def _(dve):
                with dve.Fori(0, n) as i:
                    for s in range(2):
                        dve.wait_ge(acts.sem, acts.at(i, s + 1))
                        dve.wait_ge(scanned.sem, scanned.at(i, s - 1))
                        dve.tensor_tensor(bv[:, s, :], be[:, s, :], v[:, s, :], ALU.mult).then_inc(bvd.sem, 1)
                    for s in range(2):
                        dve.wait_ge(bvd.sem, bvd.at(i, s + 1))
                        dve.wait_ge(shd.sem, shd.at(i, s - 1))
                        dve.wait_ge(cod.sem, cod.at(i, s - 1))
                        dve.tensor_tensor_scan(h[:, s, :], al[:, s, :], bv[:, s, :], 0.0, ALU.mult,
                                               ALU.add).then_inc(scanned.sem, 1)
                    for s in range(2):
                        dve.wait_ge(shd.sem, shd.at(i, s + 1))
                        dve.wait_ge(scanned.sem, scanned.at(i, s + 1))
                        dve.wait_ge(outp.sem, outp.at(i, s - 1))
                        dve.tensor_tensor(co[:, s, :], h[:, s, :], sh[:, s, :], ALU.mult).then_inc(cod.sem, 1)
                    for s in range(2):
                        dve.wait_ge(outp.sem, outp.at(i, s + 1))
                        x = cols(X, 2 * i + s)
                        dve.tensor_tensor(x, x, ps[:, 4 * s, :], ALU.add).then_inc(fin.sem, 1)

        w_in.end(1)
        for s in (proj, xpd, gates, acts, bvd, scanned, shd, cod, outp, fin):
            s.end(n)


def attention_layer(pr, tag, packed, tables):
    nc, ps, XR = pr.nc, pr.psum, pr.XN
    o = FFN_PACK
    with ExitStack() as ctx:
        def sb(name, shape, dt=F32):
            return pr.sb(name + tag, shape, dt, ctx)

        W = sb("fw", [P, o["total"]])

        def part(name):
            return W[:, o[name][0]:o[name][1]]

        wo, w1 = part("wo").rearrange("p (c n) -> p c n", c=PAIRS), part("w1")
        w2 = part("w2").rearrange("p (c n) -> p c n", c=3)
        b1, b2 = part("b1"), part("b2")
        rot = sb("rot", [P, 4, T])
        hT = sb("hT", [P, WIN + T])
        sq = sb("sq_", [P, 4, T])
        rot_a = sb("rot_a", [P, 2, T])
        rot_b = sb("rot_b", [P, 2, T])
        qf = sb("qf", [P, PAIRS, T])
        kr = sb("kr", [P, PAIRS, T])
        kn = sb("kn", [P, 2, T])
        kf = sb("kf", [P, PAIRS, WIN + T])
        cq = sb("cq", [P, PAIRS * NW])
        V = sb("V", [P, NW, HEADS * DH])
        mx = sb("mx", [P, 2, NW])
        nb = sb("nb", [P, 2, NW])
        sm = sb("sm", [P, 2, NW])
        rsm = sb("rsm", [P, 2, NW])
        Pr = sb("Pr", [P, 2, NW, P])
        Pn = sb("Pn", [P, 2, NW, P])
        PT = sb("PT", [P, NW, P])
        oT = sb("oT", [P, PAIRS, T])
        x1 = sb("x1", [P, T])
        h2 = sb("h2", [P, T])
        xc = sb("fxc", [P, T])
        fsq = sb("fsq", [P, T])
        fsd = sb("fsd", [P, T])
        gg = sb("gg", [P, 3, T])
        hm = sb("hm", [P, 3, T])

        w_in = pr.step("f_packed", 2, 16)
        ready = pr.step("f_ready", 7)
        with nc.Block() as block:
            @block.sync
            def _(sp):
                sp.dma_start(W[:, :], packed).then_inc(w_in.sem, 16)
                sp.dma_start(rot[:, :, :].rearrange("p c t -> p (c t)"), tables).then_inc(w_in.sem, 16)

            @block.vector
            def _(dve):
                dve.memset(hT[:, 0:WIN + 1], 0.0).then_inc(ready.sem, 1)
                dve.memset(kf[:, :, 0:WIN], 0.0).then_inc(ready.sem, 1)
                dve.memset(h2[:, 0:1], 0.0).then_inc(ready.sem, 1)
                dve.wait_ge(w_in.sem, w_in.at(0, 2))
                for k, name in enumerate(("qs", "qsr", "ks", "ksr")):
                    dve.tensor_scalar(rot[:, k, :], rot[:, k, :], part(name), None, ALU.mult).then_inc(ready.sem, 1)
        w_in.end(1)
        ready.end(1)

        shifted = pr.step("f_shifted", 2)
        proj = pr.step("f_proj", 8)
        squared = pr.step("f_squared", 8)
        rota = pr.step("f_rotated_a", 8)
        rotb = pr.step("f_rotated", 8)
        knorm = pr.step("f_k_norm", 4)
        kroot = pr.step("f_k_root", 4)
        kinv = pr.step("f_k_inv", 8)
        kfd = pr.step("f_k", 4)
        qnorm = pr.step("f_q_norm", PAIRS)
        qroot = pr.step("f_q_root", 1)
        qinv = pr.step("f_q_inv", 3)
        vp = pr.step("f_v_proj", NW)
        vd = pr.step("f_v", NW)
        sim = pr.step("f_sim", PAIRS)
        maxed = pr.step("f_max", PAIRS)
        nbd = pr.step("f_bias", PAIRS)
        expd = pr.step("f_exp", PAIRS)
        rsd = pr.step("f_sum_inv", PAIRS)
        pn = pr.step("f_probs", PAIRS)
        turned = pr.step("f_turned", PAIRS)
        ptd = pr.step("f_turned_copied", 2 * PAIRS)
        pv = pr.step("f_pv", PAIRS)
        oTd = pr.step("f_o", PAIRS)
        wod = pr.step("f_wo", 1)
        x1d = pr.step("f_x1", 1)
        h2d = pr.step("f_shifted2", 2)
        mean = pr.step("f_mean", 1)
        cent = pr.step("f_centered", 1)
        fsqd = pr.step("f_ln_squared", 1)
        var = pr.step("f_var", 1)
        root = pr.step("f_root", 1)
        lnd = pr.step("f_ln", 3)
        up = pr.step("f_up", 3)
        gelu = pr.step("f_gelu", 3)
        hid = pr.step("f_hidden", 3)
        dn = pr.step("f_down", 1)
        fin = pr.step("f_done", 1)

        def bank(unit):
            return 2 * (unit % 3)

        def k_root(act, i, p):
            act.wait_ge(knorm.sem, knorm.at(i, p + 1))
            if p >= 2:
                act.wait_ge(kfd.sem, kfd.at(i, p - 1))
            act.activation(kn[:, p % 2, :], ps[:, 6, :], ACT.Sqrt).then_inc(kroot.sem, 1)

        def k_inverse(dve, p, i):
            s = p % 2
            dve.wait_ge(kroot.sem, kroot.at(i, p + 1))
            dve.tensor_scalar(kn[:, s, :], kn[:, s, :], 1e-12, None, ALU.max).then_inc(kinv.sem, 1)
            dve.wait_ge(kinv.sem, kinv.at(i, 2 * p + 1))
            dve.reciprocal(kn[:, s, :], kn[:, s, :]).then_inc(kinv.sem, 1)

        with nc.Block() as block:
            @block.tensor
            def _(pe):
                with pe.Fori(0, B) as i:
                    pe.wait_ge(shifted.sem, shifted.at(i, 2))
                    hx = hT[:, WIN:WIN + T]

                    def k_norm(p):
                        pe.wait_ge(squared.sem, squared.at(i, 2 * p + 2))
                        pe.wait_ge(kroot.sem, kroot.at(i, p))
                        pe.matmul(ps[:, 6, :], lhsT=pr.heads[:, :], rhs=sq[:, (2 * p + 1) % 4, :], start=True,
                                  stop=True).then_inc(knorm.sem, 1)

                    def q_norm(p):
                        for w in range(NW):
                            for a in range(2):
                                r = slice(a * DH, (a + 1) * DH)
                                last = pe.matmul(ps[r, 7, p * NW + w:p * NW + w + 1],
                                                 lhsT=sq[r, (2 * p) % 4, w * WIN:(w + 1) * WIN],
                                                 rhs=pr.ones[r, 0:1], start=True, stop=True)
                        last.then_inc(qnorm.sem, 1)

                    for unit in range(2 * PAIRS):
                        p, isk = unit // 2, unit % 2
                        if unit >= 3:
                            pe.wait_ge(squared.sem, squared.at(i, unit - 2))
                            pe.wait_ge(rota.sem, rota.at(i, unit - 2))
                        for r, name in enumerate(("wk", "wkr") if isk else ("wq", "wqr")):
                            last = pe.matmul(ps[:, bank(unit) + r, :], lhsT=part(name)[:, p * P:(p + 1) * P], rhs=hx,
                                             start=True, stop=True)
                        last.then_inc(proj.sem, 1)
                        if isk and p:
                            k_norm(p - 1)
                            q_norm(p - 1)
                    k_norm(PAIRS - 1)
                    q_norm(PAIRS - 1)
                    pe.wait_ge(squared.sem, squared.at(i, 8))
                    pe.wait_ge(rota.sem, rota.at(i, 8))
                    for w in range(NW):
                        if w >= 4:
                            pe.wait_ge(vd.sem, vd.at(i, w - 3))
                        pe.matmul(ps[:, w % 4, :], lhsT=hT[:, w * WIN:(w + 2) * WIN], rhs=part("wv"), start=True,
                                  stop=True).then_inc(vp.sem, 1)

                    def scores(p):
                        pe.wait_ge(kfd.sem, kfd.at(i, p + 1))
                        pe.wait_ge(rotb.sem, rotb.at(i, 2 * p + 1))
                        if p == 0:
                            pe.wait_ge(vd.sem, vd.at(i, NW))
                        if p >= 2:
                            pe.wait_ge(expd.sem, expd.at(i, p - 1))
                        at = 2 * (p % 2)
                        for half in range(2):
                            pe.matmul(ps[:, at + half, :], lhsT=pr.ident_b[:, :],
                                      rhs=pr.mask0[:, :] if half == 0 else pr.mask[:, :], start=True, stop=False,
                                      skip_group_check=True)
                        for w in range(NW):
                            for a in range(2):
                                r = slice(a * DH, (a + 1) * DH)
                                last = pe.matmul(ps[r, at + w // 4, (w % 4) * P:(w % 4 + 1) * P],
                                                 lhsT=qf[r, p, w * WIN:(w + 1) * WIN],
                                                 rhs=kf[r, p, w * WIN:(w + 2) * WIN], start=False, stop=True,
                                                 skip_group_check=True)
                        last.then_inc(sim.sem, 1)

                    def turn(p):
                        pe.wait_ge(pn.sem, pn.at(i, p + 1))
                        if p:
                            pe.wait_ge(ptd.sem, ptd.at(i, 2 * p))
                        for w in range(NW):
                            last = pe.transpose(ps[:, 4 + w // 4, (w % 4) * P:(w % 4 + 1) * P], Pn[:, p % 2, w, :],
                                                pr.ident[:, :])
                        last.then_inc(turned.sem, 1)

                    def values(p):
                        pe.wait_ge(ptd.sem, ptd.at(i, 2 * p + 2))
                        if p:
                            pe.wait_ge(oTd.sem, oTd.at(i, p))
                        else:
                            pe.wait_ge(kroot.sem, kroot.at(i, PAIRS))
                        for w in range(NW):
                            for a in range(2):
                                last = pe.matmul(ps[a * DH:(a + 1) * DH, 6, w * WIN:(w + 1) * WIN],
                                                 lhsT=V[:, w, (2 * p + a) * DH:(2 * p + a + 1) * DH],
                                                 rhs=PT[:, w, a * WIN:(a + 1) * WIN], start=True, stop=True)
                        last.then_inc(pv.sem, 1)

                    scores(0)
                    scores(1)
                    for p in range(PAIRS):
                        turn(p)
                        if p + 2 < PAIRS:
                            scores(p + 2)
                        values(p)
                    pe.wait_ge(oTd.sem, oTd.at(i, PAIRS))
                    pe.wait_ge(qroot.sem, qroot.at(i, 1))
                    for p in range(PAIRS):
                        last = pe.matmul(ps[:, 7, :], lhsT=wo[:, p, :], rhs=oT[:, p, :], start=(p == 0),
                                         stop=(p == PAIRS - 1))
                    last.then_inc(wod.sem, 1)
                    pe.wait_ge(h2d.sem, h2d.at(i, 2))
                    pe.matmul(ps[:, 4, :], lhsT=pr.mean[:, :], rhs=h2[:, :], start=True, stop=True).then_inc(mean.sem, 1)
                    pe.wait_ge(fsqd.sem, fsqd.at(i, 1))
                    pe.matmul(ps[:, 5, :], lhsT=pr.mean[:, :], rhs=fsq[:, :], start=True, stop=True).then_inc(var.sem, 1)
                    pe.wait_ge(lnd.sem, lnd.at(i, 3))
                    for c in range(3):
                        for half in range(2):
                            at = half * HID + c * P
                            last = pe.matmul(ps[0:HB[c], 2 * c + half, :], lhsT=w1[:, at:at + HB[c]], rhs=xc[:, :],
                                             start=True, stop=True)
                        last.then_inc(up.sem, 1)
                    pe.wait_ge(oTd.sem, oTd.at(i, PAIRS))
                    for c in range(3):
                        pe.wait_ge(hid.sem, hid.at(i, c + 1))
                        last = pe.matmul(ps[:, 6, :], lhsT=w2[0:HB[c], c, :], rhs=hm[0:HB[c], c, :], start=(c == 0),
                                         stop=(c == 2))
                    last.then_inc(dn.sem, 1)

            @block.scalar
            def _(act):
                with act.Fori(0, B) as i:
                    for unit in range(2 * PAIRS):
                        act.wait_ge(proj.sem, proj.at(i, unit + 1))
                        if unit >= 4:
                            act.wait_ge(qnorm.sem, qnorm.at(i, unit // 2 - 1))
                        act.activation(sq[:, unit % 4, :], ps[:, bank(unit), :], ACT.Square).then_inc(squared.sem, 1)
                        if unit >= 3 and unit % 2:
                            k_root(act, i, unit // 2 - 1)
                    k_root(act, i, PAIRS - 1)
                    act.wait_ge(qnorm.sem, qnorm.at(i, PAIRS))
                    act.activation(cq[:, :], ps[:, 7, 0:PAIRS * NW], ACT.Sqrt).then_inc(qroot.sem, 1)
                    for w in range(NW):
                        act.wait_ge(vp.sem, vp.at(i, w + 1))
                        act.activation(V[:, w, :], ps[:, w % 4, :], ACT.Copy).then_inc(vd.sem, 1)

                    def probs(p):
                        act.wait_ge(nbd.sem, nbd.at(i, p + 1))
                        if p >= 2:
                            act.wait_ge(pn.sem, pn.at(i, p - 1))
                        at = 2 * (p % 2)
                        for w in range(NW):
                            last = act.activation(Pr[:, p % 2, w, :], ps[:, at + w // 4, (w % 4) * P:(w % 4 + 1) * P],
                                                  ACT.Exp, bias=nb[:, p % 2, w:w + 1],
                                                  scale=cq[:, p * NW + w:p * NW + w + 1],
                                                  accum_out=sm[:, p % 2, w:w + 1])
                        last.then_inc(expd.sem, 1)

                    def copy_turned(p):
                        act.wait_ge(turned.sem, turned.at(i, p + 1))
                        if p:
                            act.wait_ge(pv.sem, pv.at(i, p))
                        act.activation(PT[:, 0:4, :].rearrange("p w q -> p (w q)"), ps[:, 4, :],
                                       ACT.Copy).then_inc(ptd.sem, 1)

                    probs(0)
                    probs(1)
                    for p in range(PAIRS):
                        copy_turned(p)
                        if p + 2 < PAIRS:
                            probs(p + 2)
                    act.wait_ge(cent.sem, cent.at(i, 1))
                    act.activation(fsq[:, :], xc[:, :], ACT.Square).then_inc(fsqd.sem, 1)
                    act.wait_ge(var.sem, var.at(i, 1))
                    act.activation(fsd[:, :], ps[:, 5, :], ACT.Sqrt, bias=pr.eps[:, 0:1]).then_inc(root.sem, 1)
                    for c in range(3):
                        act.wait_ge(up.sem, up.at(i, c + 1))
                        m = HB[c]
                        act.activation(gg[0:m, c, :], ps[0:m, 2 * c + 1, :], ACT.Gelu,
                                       bias=b1[0:m, 3 + c:4 + c]).then_inc(gelu.sem, 1)

            @block.gpsimd
            def _(pool):
                with pool.Fori(0, B) as i:
                    for unit in range(2 * PAIRS):
                        p, isk = unit // 2, unit % 2
                        pool.wait_ge(rota.sem, rota.at(i, unit + 1))
                        dst = kr if isk else qf
                        pool.tensor_tensor(dst[:, p, :], rot_a[:, unit % 2, :], rot_b[:, unit % 2, :],
                                           ALU.add).then_inc(rotb.sem, 1)
                        if isk:
                            pool.wait_ge(kinv.sem, kinv.at(i, 2 * p + 2))
                            pool.wait_ge(rotb.sem, rotb.at(i, unit + 1))
                            pool.tensor_tensor(kf[:, p, WIN:], kr[:, p, :], kn[:, p % 2, :],
                                               ALU.mult).then_inc(kfd.sem, 1)
                    for p in range(PAIRS):
                        pool.wait_ge(rsd.sem, rsd.at(i, p + 1))
                        if p >= 2:
                            pool.wait_ge(turned.sem, turned.at(i, p - 1))
                        pool.tensor_tensor(Pn[:, p % 2, :, :], Pr[:, p % 2, :, :],
                                           rsm[:, p % 2, :].unsqueeze(2).to_broadcast([P, NW, P]),
                                           ALU.mult).then_inc(pn.sem, 1)

            @block.vector
            def _(dve):
                with dve.Fori(0, B) as i:
                    dve.wait_ge(fin.sem, fin.at(i, 0))
                    dve.tensor_copy(hT[0:DH, WIN:], XR[0:DH, bass.ds(i * T, T)]).then_inc(shifted.sem, 1)
                    dve.tensor_copy(hT[DH:P, WIN + 1:], XR[DH:P, bass.ds(i * T, T - 1)]).then_inc(shifted.sem, 1)
                    for unit in range(2 * PAIRS):
                        isk = unit % 2
                        dve.wait_ge(proj.sem, proj.at(i, unit + 1))
                        dve.wait_ge(squared.sem, squared.at(i, unit + 1))
                        if unit >= 2:
                            dve.wait_ge(rotb.sem, rotb.at(i, unit - 1))
                        dve.tensor_tensor(rot_a[:, unit % 2, :], ps[:, bank(unit), :], rot[:, 2 * isk, :], ALU.mult)
                        dve.tensor_tensor(rot_b[:, unit % 2, :], ps[:, bank(unit) + 1, :], rot[:, 2 * isk + 1, :],
                                          ALU.mult).then_inc(rota.sem, 1)
                        if unit >= 3 and isk:
                            k_inverse(dve, unit // 2 - 1, i)
                    k_inverse(dve, PAIRS - 1, i)
                    dve.wait_ge(qroot.sem, qroot.at(i, 1))
                    dve.tensor_scalar(cq[:, :], cq[:, :], 1e-12, None, ALU.max).then_inc(qinv.sem, 1)
                    dve.wait_ge(qinv.sem, qinv.at(i, 1))
                    dve.reciprocal(cq[:, :], cq[:, :]).then_inc(qinv.sem, 1)
                    dve.wait_ge(qinv.sem, qinv.at(i, 2))
                    dve.tensor_scalar(cq[:, :], cq[:, :], QK_SCALE, None, ALU.mult).then_inc(qinv.sem, 1)
                    dve.wait_ge(qinv.sem, qinv.at(i, 3))

                    def row_max(p):
                        s = p % 2
                        dve.wait_ge(sim.sem, sim.at(i, p + 1))
                        if p >= 2:
                            dve.wait_ge(nbd.sem, nbd.at(i, p - 1))
                        dve.tensor_reduce(mx[:, s, :], ps[:, 2 * s:2 * s + 2, :].rearrange("p b (w k) -> p (b w) k", k=P),
                                          AX_X, ALU.max).then_inc(maxed.sem, 1)
                        dve.wait_ge(maxed.sem, maxed.at(i, p + 1))
                        if p >= 2:
                            dve.wait_ge(expd.sem, expd.at(i, p - 1))
                        dve.scalar_tensor_tensor(out=nb[:, s, :], in0=mx[:, s, :], scalar=-1.0,
                                                 in1=cq[:, p * NW:(p + 1) * NW], op0=ALU.mult,
                                                 op1=ALU.mult).then_inc(nbd.sem, 1)

                    def sum_inverse(p):
                        dve.wait_ge(expd.sem, expd.at(i, p + 1))
                        if p >= 2:
                            dve.wait_ge(pn.sem, pn.at(i, p - 1))
                        dve.reciprocal(rsm[:, p % 2, :], sm[:, p % 2, :]).then_inc(rsd.sem, 1)

                    def copy_turned(p):
                        dve.wait_ge(turned.sem, turned.at(i, p + 1))
                        if p:
                            dve.wait_ge(pv.sem, pv.at(i, p))
                        dve.tensor_copy(PT[:, 4:8, :].rearrange("p w q -> p (w q)"), ps[:, 5, :]).then_inc(ptd.sem, 1)

                    def copy_o(p):
                        dve.wait_ge(pv.sem, pv.at(i, p + 1))
                        dve.tensor_copy(oT[:, p, :], ps[:, 6, :]).then_inc(oTd.sem, 1)

                    row_max(0)
                    row_max(1)
                    sum_inverse(0)
                    for p in range(PAIRS):
                        if p + 1 < PAIRS:
                            sum_inverse(p + 1)
                        copy_turned(p)
                        if p + 2 < PAIRS:
                            row_max(p + 2)
                        copy_o(p)
                    dve.wait_ge(wod.sem, wod.at(i, 1))
                    dve.tensor_tensor(x1[:, :], cols(XR, i), ps[:, 7, :], ALU.add).then_inc(x1d.sem, 1)
                    dve.wait_ge(x1d.sem, x1d.at(i, 1))
                    dve.tensor_copy(h2[0:DH, :], x1[0:DH, :]).then_inc(h2d.sem, 1)
                    dve.tensor_copy(h2[DH:P, 1:], x1[DH:P, 0:T - 1]).then_inc(h2d.sem, 1)
                    dve.wait_ge(h2d.sem, h2d.at(i, 2))
                    dve.wait_ge(mean.sem, mean.at(i, 1))
                    dve.tensor_tensor(xc[:, :], h2[:, :], ps[:, 4, :], ALU.subtract).then_inc(cent.sem, 1)
                    dve.wait_ge(root.sem, root.at(i, 1))
                    dve.reciprocal(fsd[:, :], fsd[:, :]).then_inc(lnd.sem, 1)
                    dve.wait_ge(lnd.sem, lnd.at(i, 1))
                    dve.wait_ge(cent.sem, cent.at(i, 1))
                    dve.wait_ge(fsqd.sem, fsqd.at(i, 1))
                    dve.tensor_tensor(xc[:, :], xc[:, :], fsd[:, :], ALU.mult).then_inc(lnd.sem, 1)
                    dve.wait_ge(lnd.sem, lnd.at(i, 2))
                    dve.tensor_scalar(xc[:, :], xc[:, :], part("ln_g"), part("ln_b"), ALU.mult,
                                      ALU.add).then_inc(lnd.sem, 1)
                    for c in range(3):
                        m = HB[c]
                        dve.wait_ge(gelu.sem, gelu.at(i, c + 1))
                        dve.scalar_tensor_tensor(out=hm[0:m, c, :], in0=ps[0:m, 2 * c, :], scalar=b1[0:m, c:c + 1],
                                                 in1=gg[0:m, c, :], op0=ALU.add, op1=ALU.mult).then_inc(hid.sem, 1)
                    dve.wait_ge(dn.sem, dn.at(i, 1))
                    dve.scalar_tensor_tensor(out=cols(XR, i), in0=ps[:, 6, :], scalar=b2, in1=x1[:, :],
                                             op0=ALU.add, op1=ALU.add).then_inc(fin.sem, 1)

        for s in (shifted, proj, squared, rota, rotb, knorm, kroot, kinv, kfd, qnorm, qroot, qinv, vp, vd, sim, maxed, nbd,
                  expd, rsd, pn, turned, ptd, pv, oTd, wod, x1d, h2d, mean, cent, fsqd, var, root, lnd, up, gelu, hid, dn,
                  fin):
            s.end(B)


def macaron_kernel(nc, x, gate_w, gate_b, experts, mamba, cell, ffn, consts, out):
    o = CONST_PACK
    with ExitStack() as ctx:
        pr = Program(nc, ctx)
        pr.psum = ctx.enter_context(nc.psum_tensor("banks", [P, 8, T], F32))
        pr.X = pr.sb("X", [P, N])
        pr.XN = pr.sb("XN", [P, N])
        pr.ident = pr.sb("ident", [P, P])
        pr.ident_b = pr.sb("ident_b", [P, P], BF16)
        pr.mean = pr.sb("mean", [P, P])
        pr.heads = pr.sb("heads", [P, P])
        pr.tri = pr.sb("tri", [P, NG * NG])
        pr.mask = pr.sb("mask", [P, T], BF16)
        pr.mask0 = pr.sb("mask0", [P, T], BF16)
        pr.sel = pr.sb("sel", [96, 2 * DS, P], BF16)
        pr.eps = pr.sb("eps", [P, 1])
        pr.ones = pr.sb("ones", [P, 1])
        const_in = ctx.enter_context(nc.semaphore("const_in"))
        const_ready = ctx.enter_context(nc.semaphore("const_ready"))
        stored = ctx.enter_context(nc.semaphore("stored"))
        for name, inc in STEP_NAMES:
            pr.step(name, 1, inc)
        with ExitStack() as tctx:
            stage = pr.sb("stage", [P, 2 * T], ctx=tctx)
            sel_f = pr.sb("sel_f", [96, 2 * DS * P], ctx=tctx)
            with nc.Block() as block:
                @block.sync
                def _(sp):
                    sp.dma_start(pr.X[:, :], x).then_inc(const_in, 16)
                    for t, name in ((pr.ident, "ident"), (pr.mean, "mean"), (pr.heads, "heads"), (pr.tri, "tri")):
                        sp.dma_start(t[:, :], consts[:, o[name][0]:o[name][1]]).then_inc(const_in, 16)
                    sp.dma_start(stage[:, :], consts[:, o["mask"][0]:o["mask0"][1]]).then_inc(const_in, 16)
                    sp.dma_start(sel_f[:, :], consts[0:96, o["sel"][0]:o["sel"][1]]).then_inc(const_in, 16)
                    sp.wait_ge(const_in, 16 * 7)

                @block.gpsimd
                def _(pool):
                    for step in pr.steps.values():
                        pool.sem_inc(step.sem, CREDIT)

                @block.vector
                def _(dve):
                    dve.memset(pr.eps[:, :], LN_EPS)
                    dve.memset(pr.ones[:, :], 1.0)
                    dve.wait_ge(const_in, 16 * 7)
                    dve.tensor_copy(pr.ident_b[:, :], pr.ident[:, :])
                    dve.tensor_copy(pr.mask[:, :], stage[:, 0:T])
                    dve.tensor_copy(pr.mask0[:, :], stage[:, T:2 * T])
                    dve.tensor_copy(pr.sel[:, :, :].rearrange("p n q -> p (n q)"), sel_f[:, :]).then_inc(const_ready, 1)
                    dve.wait_ge(const_ready, 1)

        tables = consts[:, o["cos_q"][0]:o["sin_k"][1]]
        X, XN = pr.X, pr.XN

        def moe(tag):
            layer_norm_phase(pr, tag, X, XN)
            moe_phase(pr, tag, gate_w, gate_b, experts)

        def attention(tag):
            layer_norm_phase(pr, tag, X, XN)
            for layer in range(2):
                attention_layer(pr, f"{tag}{layer}", ffn[layer], tables)
            add_stream(pr, 0.5)

        moe("m0")
        if STAGES > 1:
            layer_norm_phase(pr, "n1", X, XN)
            for layer in range(2):
                mamba_layer(pr, f"a{layer}", mamba[layer])
            add_stream(pr, 1.0)
        if STAGES > 2:
            moe("m2")
        if STAGES > 3:
            attention("f3")
        if STAGES > 4:
            layer_norm_phase(pr, "n4", X, XN)
            cell_phase(pr, "c4", cell)
        if STAGES > 5:
            attention("f5")
        with nc.Block() as block:
            @block.sync
            def _(sp):
                sp.dma_start(out, X[:, :]).then_inc(stored, 16)
                sp.wait_ge(stored, 16)


STEP_NAMES = [
    ("ln_mean", 1), ("ln_centered", 1), ("ln_squared", 1), ("ln_var", 1), ("ln_root", 1), ("ln_inv", 1),
    ("ln_normed", 1), ("gate_in", 16), ("logits", 1), ("scored", 1), ("route", 1), ("w_in_a", 16), ("w_in_b", 16), ("gate_up",
    1), ("silu", 1), ("hidden", 1), ("down", 1), ("summed", 1), ("zeroed", 1), ("turned", 1), ("added", 1),
    ("m_packed", 16), ("m_ready", 1), ("m_xz", 1), ("m_xp_copied", 1), ("m_silu_z", 1), ("m_conv", 1), ("m_u",
    1), ("m_x_dbl", 1), ("m_split", 1), ("m_dt_proj", 1), ("m_abs", 1), ("m_softplus_exp", 1),
    ("m_softplus_log", 1), ("m_dt_relu", 1), ("m_dt", 1), ("m_dtu", 1), ("m_bc_spread", 1), ("m_decay", 1),
    ("m_b_copied", 1), ("m_driven", 1), ("m_scanned", 1), ("m_state_read", 1), ("m_y_summed", 1), ("m_gated",
    1), ("m_out", 1), ("m_out_copied", 1), ("m_mean", 1), ("m_centered", 1), ("m_squared", 1), ("m_var", 1),
    ("m_root", 1), ("m_inv", 1), ("m_done", 1), ("stream_added", 1), ("c_packed", 16), ("c_proj", 1), ("c_xp",
    1), ("c_gates", 1), ("c_acts", 1), ("c_bv", 1), ("c_scanned", 1), ("c_silu_h", 1), ("c_out", 1),
    ("c_out_proj", 1), ("c_done", 1), ("f_packed", 16), ("f_ready", 1), ("f_shifted", 1), ("f_proj", 1),
    ("f_squared", 1), ("f_rotated_a", 1), ("f_rotated", 1), ("f_k_norm", 1), ("f_k_root", 1), ("f_k_inv", 1),
    ("f_k", 1), ("f_q_norm", 1), ("f_q_root", 1), ("f_q_inv", 1), ("f_v_proj", 1), ("f_v", 1), ("f_sim", 1),
    ("f_max", 1), ("f_bias", 1), ("f_exp", 1), ("f_sum_inv", 1), ("f_probs", 1), ("f_turned", 1),
    ("f_turned_copied", 1), ("f_pv", 1), ("f_o", 1), ("f_wo", 1), ("f_x1", 1), ("f_shifted2", 1), ("f_mean",
    1), ("f_centered", 1), ("f_ln_squared", 1), ("f_var", 1), ("f_root", 1), ("f_ln", 1), ("f_up", 1),
    ("f_gelu", 1), ("f_hidden", 1), ("f_down", 1), ("f_done", 1),
]
STAGES = 6


def rotary_tables(np):
    f = np.float32
    half = np.arange(0, DH, 2, dtype=f)
    inv_freq = (f(1.0) / np.power(f(10000.0), half / f(DH))).astype(f)
    t = np.arange(T, dtype=f)
    freqs = (t[:, None] * inv_freq[None, :]).astype(f)
    freqs = np.concatenate([freqs, freqs], axis=-1).astype(np.float64)
    base = (half + 0.4 * DH) / (1.4 * DH)
    power = (t - T // 2) / float(WIN // 2)
    scale = base[None, :].astype(np.float64) ** power[:, None]
    scale = np.concatenate([scale, scale], axis=-1)
    sign = np.concatenate([-np.ones(DH // 2), np.ones(DH // 2)])
    cos, sin = np.cos(freqs), np.sin(freqs) * sign
    return [np.tile(a.T, (2, 1)).astype(f) for a in (cos * scale, sin * scale, cos / scale, sin / scale)]


def constants(np):
    f = np.float32
    r = np.arange(P)
    parts = {"ident": np.eye(P, dtype=f), "mean": np.full((P, P), 1.0 / P, f),
             "heads": (r[:, None] // DH == r[None, :] // DH).astype(f)}
    g = np.arange(NG)
    parts["tri"] = np.tile((g[None, :] < g[:, None]).astype(f).reshape(1, -1), (P, 1))
    q, k = (r % WIN)[:, None], r[None, :]
    inside = (q <= k) & (k <= q + WIN)
    mask = np.where(inside, 0.0, MASKED).astype(f)
    first = np.where(inside & (k >= WIN), 0.0, MASKED).astype(f)
    parts["mask"] = np.tile(mask, (1, T // P))
    parts["mask0"] = np.concatenate([first] + [mask] * (T // P - 1), axis=1)
    for name, table in zip(("cos_q", "sin_q", "cos_k", "sin_k"), rotary_tables(np)):
        parts[name] = table
    sel = np.zeros((P, 2 * DS, P), f)
    for p in range(96):
        sel[p, p % 32, :] = 1.0
    parts["sel"] = sel.reshape(P, -1)
    return pack(np, CONST_PACK, parts)


def pack(np, layout, parts):
    out = np.zeros((P, layout["total"]), np.float32)
    for name, a in parts.items():
        lo, hi = layout[name]
        a = np.asarray(a).reshape(a.shape[0], -1)
        assert a.shape[1] == hi - lo, name
        at = 32 if name == "dt_w" else 0
        out[at:at + a.shape[0], lo:hi] = a
    return out


def tiles(np, v, n):
    out = np.zeros((n * P,) + v.shape[1:], np.float32)
    out[:v.shape[0]] = v
    return np.moveaxis(out.reshape((n, P) + v.shape[1:]), 0, 1)


def kernel(**inputs):
    import numpy as np
    import concourse.bacc as _bacc
    from concourse.bass_utils import run_bass_kernel_spmd as _run

    a = {k: np.asarray(v) for k, v in inputs.items()}
    arrays = {"x": a["L0_attn_x"].reshape(N, P).T,
              "gate_w": a["L0_ffn_gate_w"].T,
              "gate_b": np.tile(a["L0_ffn_gate_bias"][None, :], (P, 1)),
              "consts": constants(np)}

    def expert_pack(wg, wu, wd):
        out = np.zeros((P, 2 * I_MOE + P), np.float32)
        out[:, 0:I_MOE], out[:, I_MOE:2 * I_MOE], out[0:I_MOE, 2 * I_MOE:] = wg.T, wu.T, wd.T
        return out

    every = [expert_pack(a["L0_ffn_Wg"][e], a["L0_ffn_Wu"][e], a["L0_ffn_Wd"][e]) for e in range(E)]
    for s in range(2):
        r = slice(s * I_MOE, (s + 1) * I_MOE)
        every.append(expert_pack(a["L0_ffn_Sg"][r], a["L0_ffn_Su"][r], a["L0_ffn_Sd"][:, r]))
    arrays["experts"] = np.stack(every)

    for l in range(2):
        m = {k[len("L0_attn_"):]: v[l] for k, v in a.items() if k.startswith("L0_attn_") and k != "L0_attn_x"}
        xp_w = m["x_proj_w"]
        xp_w = np.concatenate([xp_w[DR:], xp_w[:DR]], axis=0)
        arrays[f"mamba{l}"] = pack(np, MAMBA_PACK, {
            "in_w": m["in_proj_w"].T, "xp_w": tiles(np, xp_w.T, HALF), "dt_w": m["dt_proj_w"].T,
            "out_w": tiles(np, m["out_proj_w"].T, HALF), "conv_w": tiles(np, m["conv_w"], HALF),
            "conv_b": tiles(np, m["conv_b"], HALF), "dt_b": tiles(np, m["dt_proj_b"], HALF),
            "A_log": tiles(np, m["A_log"], HALF), "D": tiles(np, m["Dskip"], HALF),
            "ln_w": m["ln_w"][:, None], "ln_b": m["ln_b"][:, None]})
        w = {k[len("L1_ffn_"):]: v[l] for k, v in a.items() if k.startswith("L1_ffn_")}
        d = np.arange(DH)
        turn = (d + DH // 2) % DH
        order = np.concatenate([h * DH + turn for h in range(HEADS)])
        wq, wk, wv = w["wqkv"][:, 0:512], w["wqkv"][:, 512:1024], w["wqkv"][:, 1024:1536]
        twice = lambda v: np.concatenate([v, v])[:, None]
        b1 = np.concatenate([tiles(np, w["b1"][:HID], 3), tiles(np, w["b1"][HID:], 3)], axis=1)
        arrays[f"ffn{l}"] = pack(np, FFN_PACK, {
            "wq": wq, "wqr": wq[:, order], "wk": wk, "wkr": wk[:, order], "wv": wv, "wo": tiles(np, w["wo"], PAIRS),
            "w1": w["w1"], "w2": tiles(np, w["w2"], 3), "b1": b1, "ln_g": w["ln_g"][:, None],
            "ln_b": w["ln_b"][:, None], "b2": w["b2"][:, None], "qs": twice(w["q_scale"]),
            "qsr": twice(w["q_scale"][turn]), "ks": twice(w["k_scale"]), "ksr": twice(w["k_scale"][turn])})
    c = {k[len("L1_attn_"):]: v for k, v in a.items() if k.startswith("L1_attn_")}
    arrays["cell"] = pack(np, CELL_PACK, {
        "w_in": c["W_in"].T, "w_a": c["W_alpha"].T, "w_b": c["W_beta"].T, "w_v": c["W_v"].T, "w_out": c["W_out"].T,
        "b_a": c["b_alpha"][:, None], "b_b": c["b_beta"][:, None], "b_v": c["b_v"][:, None]})

    nc = _bacc.Bacc("TRN2", target_bir_lowering=False, num_devices=1)
    arrays = {k: np.ascontiguousarray(v) for k, v in arrays.items()}
    t = {k: nc.dram_tensor(f"in_{k}", v.shape, F32, kind="ExternalInput").ap() for k, v in arrays.items()}
    out = nc.dram_tensor("out_x", (P, N), F32, kind="ExternalOutput").ap()
    macaron_kernel(nc, t["x"], t["gate_w"], t["gate_b"], t["experts"], [t["mamba0"], t["mamba1"]], t["cell"],
                   [t["ffn0"], t["ffn1"]], t["consts"], out)
    r = _run(nc, [{f"in_{k}": v for k, v in arrays.items()}], core_ids=[0])
    return np.ascontiguousarray(r.results[0]["out_x"].T.reshape(B, T, P))
```

```python
from contextlib import ExitStack

import concourse.bass as bass
from concourse import mybir

P = 128
B, T = 8, 512
N = B * T
TB = T // P
NT = N // P

E, I_MOE, TOP_K, NG, KEEP_G = 64, 88, 8, 8, 4
EG = E // NG
CHUNKS = -(-2 * I_MOE // P) + E * I_MOE // P
SLOTS = 4
SLOT_USES = [sum(q % SLOTS == s for q in range(CHUNKS)) for s in range(SLOTS)]
ROUTED_SCALE = 2.5

DI, DS, DR = 256, 16, 8
HALF = DI // P
PAD = 3

HEADS, DH, WIN = 8, 64, 64
PAIRS = HEADS // 2
NW = T // WIN
HID = 341
HB = [128, 128, 85]
QK_SCALE = 8.0
LN_EPS = 1e-5
MASKED = -1e30

F32 = mybir.dt.float32
F32R = mybir.dt.float32r
BF16 = mybir.dt.bfloat16
U32 = mybir.dt.uint32
ALU = mybir.AluOpType
ACT = mybir.ActivationFunctionType
AX_X = mybir.AxisListType.X
CREDIT = 16


def offsets(parts):
    out, at = {}, 0
    for name, width in parts:
        out[name] = (at, at + width)
        at += width
    out["total"] = at
    return out


MAMBA_PACK = offsets([("in_w", 2 * DI), ("xp_w", HALF * 40), ("dt_w", DI), ("out_w", HALF * P), ("conv_w", HALF * 4),
                      ("conv_b", HALF), ("dt_b", HALF), ("A_log", HALF * DS), ("D", HALF), ("ln_w", 1), ("ln_b", 1)])
CELL_PACK = offsets([("w_in", P), ("w_a", P), ("w_b", P), ("w_v", P), ("w_out", P), ("b_a", 1), ("b_b", 1), ("b_v", 1)])
FFN_PACK = offsets([("wq", 512), ("wqr", 512), ("wk", 512), ("wkr", 512), ("wv", 512), ("wo", 512), ("w1", 2 * HID),
                    ("w2", 3 * P), ("b1", 6), ("ln_g", 1), ("ln_b", 1), ("b2", 1),
                    ("qs", 1), ("qsr", 1), ("ks", 1), ("ksr", 1)])
CONST_PACK = offsets([("ident", P), ("mean", P), ("heads", P), ("tri", NG * NG), ("mask", T),
                      ("cos_q", T), ("sin_q", T), ("cos_k", T), ("sin_k", T), ("sel", 2 * DS * P)])


class Step:

    def __init__(self, sem, inc=1):
        self.sem, self.inc, self.base, self.per = sem, inc, CREDIT, 0

    def start(self, per):
        self.per = per * self.inc

    def at(self, i, k):
        return i * self.per + (self.base + k * self.inc)

    def end(self, iterations):
        self.base += iterations * self.per


class Program:
    def __init__(self, nc, ctx):
        self.nc, self.ctx, self.steps = nc, ctx, {}

    def step(self, name, per, inc=1):
        if name not in self.steps:
            self.steps[name] = Step(self.ctx.enter_context(self.nc.semaphore(name)), inc)
        self.steps[name].start(per)
        return self.steps[name]

    def sb(self, name, shape, dt=F32, ctx=None):
        return (ctx or self.ctx).enter_context(self.nc.sbuf_tensor(name, shape, dt))


LOG_EXP = "natural_log_exp_and_others"


def cols(t, i):
    return t[:, bass.ds(i * T, T)]


def layer_norm_phase(pr, tag, src, dst):
    nc = pr.nc
    U = 4
    with ExitStack() as ctx:
        xc = pr.sb(f"xc{tag}", [P, U, T], ctx=ctx)
        sq = pr.sb(f"sq{tag}", [P, U, T], ctx=ctx)
        lg = pr.sb(f"lg{tag}", [P, U, T], ctx=ctx)
        rs = pr.sb(f"rs{tag}", [P, U, T], ctx=ctx)
        ps = pr.psum
        mean = pr.step("ln_mean", U)
        centered = pr.step("ln_centered", U)
        squared = pr.step("ln_squared", U)
        var = pr.step("ln_var", U)
        logged = pr.step("ln_log", U)
        inv = pr.step("ln_inv", U)
        normed = pr.step("ln_normed", U)
        n = B // U
        block = ctx.enter_context(nc.Block())

        @block.tensor
        def _(pe):
            with pe.Fori(0, n) as i:
                for s in range(U):
                    pe.wait_ge(centered.sem, centered.at(i, s + 1 - U))
                    pe.matmul(ps[:, s, :], lhsT=pr.mean[:, :], rhs=cols(src, U * i + s), start=True,
                              stop=True).then_inc(mean.sem, 1)
                for s in range(U):
                    pe.wait_ge(squared.sem, squared.at(i, s + 1))
                    pe.wait_ge(logged.sem, logged.at(i, s + 1 - U))
                    pe.matmul(ps[:, U + s, :], lhsT=pr.mean[:, :], rhs=sq[:, s, :], start=True,
                              stop=True).then_inc(var.sem, 1)

        @block.scalar
        def _(act):
            act.preload_act_table_set(LOG_EXP)
            with act.Fori(0, n) as i:
                for s in range(U):
                    act.wait_ge(centered.sem, centered.at(i, s + 1))
                    act.wait_ge(var.sem, var.at(i, s + 1 - U))
                    act.activation(sq[:, s, :], xc[:, s, :], ACT.Square).then_inc(squared.sem, 1)
                for s in range(U):
                    act.wait_ge(var.sem, var.at(i, s + 1))
                    act.activation(lg[:, s, :], ps[:, U + s, :], ACT.Ln, bias=pr.eps[:, 0:1]).then_inc(logged.sem, 1)
                    act.wait_ge(logged.sem, logged.at(i, s + 1))
                    act.wait_ge(normed.sem, normed.at(i, s + 1 - U))
                    act.activation(rs[:, s, :], lg[:, s, :], ACT.Exp, scale=-0.5).then_inc(inv.sem, 1)

        @block.vector
        def _(dve):
            with dve.Fori(0, n) as i:
                for s in range(U):
                    dve.wait_ge(mean.sem, mean.at(i, s + 1))
                    dve.wait_ge(squared.sem, squared.at(i, s + 1 - U))
                    dve.wait_ge(normed.sem, normed.at(i, s + 1 - U))
                    dve.tensor_tensor(xc[:, s, :], cols(src, U * i + s), ps[:, s, :],
                                      ALU.subtract).then_inc(centered.sem, 1)
                for s in range(U):
                    dve.wait_ge(inv.sem, inv.at(i, s + 1))
                    dve.tensor_tensor(cols(dst, U * i + s), xc[:, s, :], rs[:, s, :],
                                      ALU.mult).then_inc(normed.sem, 1)

        for s in (mean, centered, squared, var, logged, inv, normed):
            s.end(n)


def moe_phase(pr, tag, gate_w, gate_b, experts):
    nc, ps, X, XN = pr.nc, pr.psum, pr.X, pr.XN
    with ExitStack() as ctx:
        gw = pr.sb(f"gw{tag}", [P, E], ctx=ctx)
        gb = pr.sb(f"gb{tag}", [P, E], ctx=ctx)
        RW = pr.sb(f"RW{tag}", [P, NT, 2 * E], F32R, ctx=ctx)
        with ExitStack() as rctx:
            score = pr.sb(f"score{tag}", [P, NT, E], ctx=rctx)
            choice = pr.sb(f"choice{tag}", [P, NT, E], ctx=rctx)
            ta = pr.sb(f"ta{tag}", [P, NT * E], ctx=rctx)
            tb = pr.sb(f"tb{tag}", [P, NT * E], ctx=rctx)
            top = pr.sb(f"top{tag}", [P, NT, 8], ctx=rctx)
            gs = pr.sb(f"gs{tag}", [P, NT, NG], ctx=rctx)
            rank = pr.sb(f"rank{tag}", [P, NT, NG], ctx=rctx)
            tot = pr.sb(f"tot{tag}", [P, NT], ctx=rctx)
            G = NT // 4
            gate_in = pr.step("gate_in", 2, 16)
            logits = pr.step("logits", 4)
            scored = pr.step("scored", 4)
            route = pr.step("route", 400)
            with nc.Block() as block:
                @block.sync
                def _(sp):
                    sp.dma_start(gw[:, :], gate_w).then_inc(gate_in.sem, 16)
                    sp.dma_start(gb[:, :], gate_b).then_inc(gate_in.sem, 16)

                @block.tensor
                def _(pe):
                    pe.wait_ge(gate_in.sem, gate_in.at(0, 2))
                    for g in range(4):
                        for t in range(G):
                            m = (g * G + t) * P
                            last = pe.matmul(ps[:, g, t * E:(t + 1) * E], lhsT=XN[:, m:m + P], rhs=gw[:, :],
                                             start=True, stop=True)
                        last.then_inc(logits.sem, 1)

                @block.scalar
                def _(act):
                    for g in range(4):
                        act.wait_ge(logits.sem, logits.at(0, g + 1))
                        act.activation(score[:, g * G:(g + 1) * G, :].rearrange("p t e -> p (t e)"), ps[:, g, :],
                                       ACT.Sigmoid).then_inc(scored.sem, 1)

                @block.vector
                def _(dve):
                    count = [0]

                    def then(ins):
                        count[0] += 1
                        ins.then_inc(route.sem, 1)
                        dve.wait_ge(route.sem, route.at(0, count[0]))

                    def tt(out, a, b, op):
                        then(dve.tensor_tensor(out, a, b, op))

                    dve.wait_ge(scored.sem, scored.at(0, 4))
                    dve.wait_ge(gate_in.sem, gate_in.at(0, 2))
                    tt(choice[:, :, :], score[:, :, :], gb[:, :].unsqueeze(1).to_broadcast([P, NT, E]), ALU.add)
                    c = choice[:, :, :].rearrange("p t (g j) -> p (t g) j", j=EG)
                    M = NT * NG
                    h1 = ta[:, 0:4 * M].rearrange("p (q j) -> p q j", j=4)
                    l1 = ta[:, 4 * M:8 * M].rearrange("p (q j) -> p q j", j=4)
                    tt(h1, c[:, :, 0:4], c[:, :, 4:8], ALU.max)
                    tt(l1, c[:, :, 0:4], c[:, :, 4:8], ALU.min)
                    v = [tb[:, 2 * M * k:2 * M * (k + 1)].rearrange("p (q j) -> p q j", j=2) for k in range(4)]
                    tt(v[0], h1[:, :, 0:2], h1[:, :, 2:4], ALU.max)
                    tt(v[1], h1[:, :, 0:2], h1[:, :, 2:4], ALU.min)
                    tt(v[2], l1[:, :, 0:2], l1[:, :, 2:4], ALU.max)
                    tt(v[3], v[1], v[2], ALU.max)
                    w = [ta[:, M * k:M * (k + 1)] for k in range(4)]
                    a, b = v[0], v[3]
                    tt(w[0], a[:, :, 0], a[:, :, 1], ALU.max)
                    tt(w[1], a[:, :, 0], a[:, :, 1], ALU.min)
                    tt(w[2], b[:, :, 0], b[:, :, 1], ALU.max)
                    tt(w[3], w[1], w[2], ALU.max)
                    gsf = gs[:, :, :].rearrange("p t g -> p (t g)")
                    tt(gsf, w[0], w[3], ALU.add)
                    shape = [P, NT, NG, NG]
                    other = gs[:, :, :].unsqueeze(2).to_broadcast(shape)
                    own = gs[:, :, :].unsqueeze(3).to_broadcast(shape)
                    above = ta[:, :].rearrange("p (t g j) -> p t g j", g=NG, j=NG)
                    equal = tb[:, :].rearrange("p (t g j) -> p t g j", g=NG, j=NG)
                    tt(above, other, own, ALU.is_gt)
                    tt(equal, other, own, ALU.is_equal)
                    tt(tb[:, :].rearrange("p (t x) -> p t x", t=NT), tb[:, :].rearrange("p (t x) -> p t x", t=NT),
                       pr.tri[:, :].unsqueeze(1).to_broadcast([P, NT, NG * NG]), ALU.mult)
                    tt(ta[:, :], ta[:, :], tb[:, :], ALU.add)
                    then(dve.tensor_reduce(rank[:, :, :].rearrange("p t g -> p (t g)"),
                                           ta[:, :].rearrange("p (q j) -> p q j", j=NG), AX_X, ALU.add))
                    then(dve.tensor_scalar(gs[:, :, :], rank[:, :, :], float(KEEP_G), None, ALU.is_lt))
                    masked = ta[:, :].rearrange("p (q j) -> p q j", j=EG)
                    tt(masked, c, gsf.unsqueeze(2).to_broadcast([P, NT * NG, EG]), ALU.mult)
                    for t in range(NT):
                        mt = ta[:, t * E:(t + 1) * E]
                        last = dve.max(top[:, t, :], mt)
                        last.then_inc(route.sem, 1)
                        count[0] += 1
                    dve.wait_ge(route.sem, route.at(0, count[0]))
                    for t in range(NT):
                        mt = ta[:, t * E:(t + 1) * E]
                        last = dve.match_replace(tb[:, t * E:(t + 1) * E], top[:, t, :], mt, MASKED)
                        last.then_inc(route.sem, 1)
                        count[0] += 1
                    dve.wait_ge(route.sem, route.at(0, count[0]))
                    tt(ta[:, :], ta[:, :], tb[:, :], ALU.not_equal)
                    tat = ta[:, :].rearrange("p (t e) -> p t e", e=E)
                    tt(tat, tat, score[:, :, :], ALU.mult)
                    then(dve.tensor_reduce(tot[:, :], tat, AX_X, ALU.add))
                    then(dve.tensor_scalar(tot[:, :], tot[:, :], 1e-20, None, ALU.add))
                    then(dve.reciprocal(tot[:, :], tot[:, :]))
                    then(dve.tensor_scalar(tot[:, :], tot[:, :], 0.5 * ROUTED_SCALE, None, ALU.mult))
                    tt(tat, tat, tot[:, :].unsqueeze(2).to_broadcast([P, NT, E]), ALU.mult)
                    then(dve.tensor_copy(RW[:, :, 0:E], tat))
                    tt(RW[:, :, E:2 * E], tat, RW[:, :, 0:E].bitcast(F32), ALU.subtract)
                    route.start(count[0])

            for s in (gate_in, logits, scored, route):
                s.end(1)

        rT = pr.sb(f"rT{tag}", [P, N], F32R, ctx=ctx)
        xh = pr.sb(f"xh{tag}", [P, N], F32R, ctx=ctx)
        xl = pr.sb(f"xl{tag}", [P, N], F32R, ctx=ctx)
        turned = pr.step("turned", B)
        rcopied = pr.step("weights_turned", B)
        parts = pr.step("token_parts", 2 * B)
        with nc.Block() as block:
            @block.tensor
            def _(pe):
                for b in range(B):
                    pe.wait_ge(rcopied.sem, rcopied.at(0, b - 1))
                    for t in range(TB):
                        last = pe.transpose(ps[:, b % 2, t * P:(t + 1) * P], RW[:, b * TB + t, :].bitcast(F32),
                                            pr.ident[:, :])
                    last.then_inc(turned.sem, 1)

            @block.vector
            def _(dve):
                for b in range(B):
                    dve.wait_ge(turned.sem, turned.at(0, b + 1))
                    dve.tensor_copy(rT[:, b * T:(b + 1) * T], ps[:, b % 2, :]).then_inc(rcopied.sem, 1)

            @block.scalar
            def _(act):
                for b in range(B):
                    c = slice(b * T, (b + 1) * T)
                    act.activation(xh[:, c], XN[:, c], ACT.Copy).then_inc(parts.sem, 1)

            @block.gpsimd
            def _(pool):
                for b in range(B):
                    c = slice(b * T, (b + 1) * T)
                    pool.wait_ge(parts.sem, parts.at(0, B if b else 1))
                    pool.tensor_tensor(xl[:, c], XN[:, c], xh[:, c].bitcast(F32), ALU.subtract)

        turned.end(1)
        rcopied.end(1)
        parts.base += B

        stage = pr.sb(f"stage{tag}", [P, SLOTS, 4 * P], ctx=ctx)
        wh = pr.sb(f"wh{tag}", [P, SLOTS, 4 * P], F32R, ctx=ctx)
        wl = pr.sb(f"wl{tag}", [P, SLOTS, 3 * P], F32R, ctx=ctx)
        sg = pr.sb(f"sg{tag}", [P, 2, T], ctx=ctx)
        gu = pr.sb(f"gu{tag}", [P, 2, T], ctx=ctx)
        h = pr.sb(f"h{tag}", [P, 2, T], ctx=ctx)
        hh = pr.sb(f"hh{tag}", [P, 4, T], F32R, ctx=ctx)
        hl = pr.sb(f"hl{tag}", [P, 4, T], F32R, ctx=ctx)
        PER = 2 * CHUNKS
        loaded = [pr.step(f"chunk_in_{c}", n, 16) for c, n in zip("abcd", SLOT_USES)]
        w_high = pr.step("w_high", CHUNKS)
        w_low = pr.step("w_low", CHUNKS)
        gate_up = pr.step("gate_up", PER)
        silu = pr.step("silu", PER)
        product = pr.step("product", PER)
        hidden = pr.step("hidden", PER)
        high = pr.step("hidden_high", PER)
        low = pr.step("hidden_low", PER)
        down = pr.step("down", PER)
        added = pr.step("added", 2)
        LOOPS = (CHUNKS - 2) // SLOTS
        G = 2 * SLOTS

        def slot(q):
            return q % SLOTS

        def uses(q, i):
            return i + q // SLOTS + 1

        with nc.Block() as block:
            @block.sync
            def _(sp):
                def load(p, q, i):
                    s = slot(q)
                    before = q + SLOTS * i - (2 if q < 2 else SLOTS)
                    sp.wait_ge(w_low.sem, w_low.at(p, before + 1))
                    sp.dma_start(stage[:, s, :], experts[bass.ds(q + SLOTS * i, 1), :, :].rearrange(
                        "e p n -> (e p) n")).then_inc(loaded[s].sem, 16)

                with sp.Fori(0, B // 2) as p:
                    for q in range(2):
                        load(p, q, 0)
                    with sp.Fori(0, LOOPS) as i:
                        for q in range(2, 2 + SLOTS):
                            load(p, q, i)

            @block.tensor
            def _(pe):
                def gates(p, q, i, k):
                    s, m = slot(q), 2 * q + k
                    if k == 0:
                        pe.wait_ge(w_low.sem, w_low.at(p, q + SLOTS * i + 1))
                    pe.wait_ge(hidden.sem, hidden.at(p, m + G * i - 1))
                    c = bass.ds(p * (2 * T) + k * T, T)
                    for bank, at in ((2 + k, 0), (4 + k, P)):
                        pe.matmul(ps[:, bank, :], lhsT=wh[:, s, at:at + P], rhs=xh[:, c], start=True, stop=False)
                        pe.matmul(ps[:, bank, :], lhsT=wl[:, s, at:at + P], rhs=xh[:, c], start=False, stop=False)
                        last = pe.matmul(ps[:, bank, :], lhsT=wh[:, s, at:at + P], rhs=xl[:, c], start=False, stop=True)
                    if q >= 2:
                        last = pe.matmul(ps[:, 6 + k, :], lhsT=wh[:, s, 3 * P:], rhs=rT[:, c], start=True, stop=True)
                    last.then_inc(gate_up.sem, 1)

                def down_product(p, q, i, k):
                    s, m = slot(q), 2 * q + k
                    if q == 0:
                        pe.wait_ge(added.sem, added.at(p, k - 1))
                    pe.wait_ge(low.sem, low.at(p, m + G * i + 1))
                    first, final = q == 0, q == CHUNKS - 1
                    r = m % 4
                    pe.matmul(ps[:, k, :], lhsT=wh[:, s, 2 * P:3 * P], rhs=hh[:, r, :], start=first, stop=False,
                              skip_group_check=True)
                    pe.matmul(ps[:, k, :], lhsT=wl[:, s, 2 * P:3 * P], rhs=hh[:, r, :], start=False, stop=False,
                              skip_group_check=True)
                    pe.matmul(ps[:, k, :], lhsT=wh[:, s, 2 * P:3 * P], rhs=hl[:, r, :], start=False, stop=final,
                              skip_group_check=True).then_inc(down.sem, 1)

                with pe.Fori(0, B // 2) as p:
                    for k in range(2):
                        gates(p, 0, 0, k)
                    for q in (1, 2):
                        for k in range(2):
                            gates(p, q, 0, k)
                            down_product(p, q - 1, 0, k)
                    with pe.Fori(0, LOOPS - 1) as i:
                        for q in range(3, 3 + SLOTS):
                            for k in range(2):
                                gates(p, q, i, k)
                                down_product(p, q - 1, i, k)
                    for q in range(CHUNKS - SLOTS + 1, CHUNKS):
                        for k in range(2):
                            gates(p, q, 0, k)
                            down_product(p, q - 1, 0, k)
                    for k in range(2):
                        down_product(p, CHUNKS - 1, 0, k)

            @block.scalar
            def _(act):
                def chunk(p, q, i, more=True):
                    for k in range(2):
                        m = 2 * q + k + G * i
                        act.wait_ge(gate_up.sem, gate_up.at(p, m + 1))
                        act.wait_ge(product.sem, product.at(p, m - 1))
                        act.activation(sg[:, k, :], ps[:, 2 + k, :], ACT.Silu).then_inc(silu.sem, 1)
                        if k == 0 and more:
                            high_part(p, q + 2, i)

                def high_part(p, q, i):
                    act.wait_ge(loaded[slot(q)].sem, loaded[slot(q)].at(p, uses(q, i)))
                    before = q + SLOTS * i - (2 if q < 2 else SLOTS)
                    act.wait_ge(down.sem, down.at(p, 2 * (before + 1)))
                    act.activation(wh[:, slot(q), :], stage[:, slot(q), :], ACT.Copy).then_inc(w_high.sem, 1)

                with act.Fori(0, B // 2) as p:
                    for q in range(2):
                        high_part(p, q, 0)
                    for q in range(2):
                        chunk(p, q, 0)
                    with act.Fori(0, LOOPS - 1) as i:
                        for q in range(2, 2 + SLOTS):
                            chunk(p, q, i)
                    for q in range(CHUNKS - SLOTS, CHUNKS):
                        chunk(p, q, 0, q + 2 < CHUNKS)

            @block.gpsimd
            def _(pool):
                def low_part(p, q, i):
                    s = slot(q)
                    pool.wait_ge(w_high.sem, w_high.at(p, q + SLOTS * i + 1))
                    pool.tensor_tensor(wl[:, s, :], stage[:, s, 0:3 * P], wh[:, s, 0:3 * P].bitcast(F32),
                                       ALU.subtract).then_inc(w_low.sem, 1)

                def chunk(p, q, i, more=True):
                    for k in range(2):
                        m = 2 * q + k
                        pool.wait_ge(high.sem, high.at(p, m + G * i + 1))
                        pool.wait_ge(down.sem, down.at(p, m + G * i - 3))
                        pool.tensor_tensor(hl[:, m % 4, :], h[:, k, :], hh[:, m % 4, :].bitcast(F32),
                                           ALU.subtract).then_inc(low.sem, 1)
                        if k == 0 and more:
                            low_part(p, q + 2, i)

                with pool.Fori(0, B // 2) as p:
                    for q in range(2):
                        low_part(p, q, 0)
                    for q in range(2):
                        chunk(p, q, 0)
                    with pool.Fori(0, LOOPS - 1) as i:
                        for q in range(2, 2 + SLOTS):
                            chunk(p, q, i)
                    for q in range(CHUNKS - SLOTS, CHUNKS):
                        chunk(p, q, 0, q + 2 < CHUNKS)

            @block.vector
            def _(dve):
                def chunk(p, q, i):
                    for k in range(2):
                        m = 2 * q + k
                        n = m + G * i
                        dve.wait_ge(silu.sem, silu.at(p, n + 1))
                        dve.wait_ge(low.sem, low.at(p, n - 1))
                        if q < 2:
                            dve.scalar_tensor_tensor(out=h[:, k, :], in0=sg[:, k, :], scalar=0.5, in1=ps[:, 4 + k, :],
                                                     op0=ALU.mult, op1=ALU.mult).then_inc(hidden.sem, 1)
                            dve.nop().then_inc(product.sem, 1)
                        else:
                            dve.wait_ge(hidden.sem, hidden.at(p, n - 1))
                            dve.tensor_tensor(gu[:, k, :], ps[:, 4 + k, :], sg[:, k, :],
                                              ALU.mult).then_inc(product.sem, 1)
                            dve.wait_ge(product.sem, product.at(p, n + 1))
                            dve.tensor_tensor(h[:, k, :], ps[:, 6 + k, :], gu[:, k, :], ALU.mult).then_inc(hidden.sem, 1)
                        dve.wait_ge(hidden.sem, hidden.at(p, n + 1))
                        dve.wait_ge(down.sem, down.at(p, n - 3))
                        dve.tensor_copy(hh[:, m % 4, :], h[:, k, :]).then_inc(high.sem, 1)

                with dve.Fori(0, B // 2) as p:
                    for q in range(2):
                        chunk(p, q, 0)
                    with dve.Fori(0, LOOPS) as i:
                        for q in range(2, 2 + SLOTS):
                            chunk(p, q, i)
                    for k in range(2):
                        dve.wait_ge(down.sem, down.at(p, PER - 1 + k))
                        x = X[:, bass.ds(p * (2 * T) + k * T, T)]
                        dve.tensor_tensor(x, x, ps[:, k, :], ALU.add).then_inc(added.sem, 1)

        for step in (*loaded, w_high, w_low, gate_up, silu, product, hidden, high, low, down, added):
            step.end(B // 2)


def mamba_layer(pr, tag, packed):
    nc, ps, XR = pr.nc, pr.psum, pr.XN
    o = MAMBA_PACK
    with ExitStack() as ctx:
        def sb(name, shape, dt=F32):
            return pr.sb(name + tag, shape, dt, ctx)

        W = sb("mw", [P, o["total"]])

        def part(name):
            return W[:, o[name][0]:o[name][1]]

        in_w, out_w = part("in_w"), part("out_w").rearrange("p (h n) -> p h n", h=HALF)
        xp_w = part("xp_w").rearrange("p (h n) -> p h n", h=HALF)
        dt_w = W[32:32 + DR, o["dt_w"][0]:o["dt_w"][1]]
        conv_w = part("conv_w").rearrange("p (h k) -> p h k", h=HALF)
        conv_b, dt_b, ln_w, ln_b = part("conv_b"), part("dt_b"), part("ln_w"), part("ln_b")
        skip_d = part("D")
        A = sb("A", [P, HALF, DS])
        diag = sb("diag", [P, HALF, P])
        xp = sb("xp", [P, HALF, PAD + T])
        cv = sb("cv", [P, HALF, T])
        u = sb("u", [P, HALF, T])
        sz = sb("sz", [P, HALF, T])
        dts = sb("dts", [40, T])
        r1 = sb("r1", [32, T])
        r2 = sb("r2", [32, T])
        mid = sb("mid", [32, T], BF16)
        bc = sb("bc", [96, T], BF16)
        av = sb("av", [P, HALF, T])
        dt = sb("dt", [P, HALF, T])
        dtu = sb("dtu", [P, HALF, T])
        dA = sb("dA", [P, 2, HALF, T])
        Bs = sb("Bs", [P, 2, T])
        dBu = sb("dBu", [P, 2, HALF, T])
        hh = sb("hh", [P, 2, HALF, T])
        hc = sb("hc", [P, 2, HALF, T])
        yz = sb("yz", [P, HALF, T])
        ob = sb("ob", [P, T])
        oc = sb("oc", [P, T])
        osq = sb("osq", [P, T])
        osd = sb("osd", [P, T])

        packed_in = pr.step("m_packed", 1, 16)
        ready = pr.step("m_ready", 6)
        with nc.Block() as block:
            @block.sync
            def _(sp):
                sp.dma_start(W[:, :], packed).then_inc(packed_in.sem, 16)

            @block.scalar
            def _(act):
                act.wait_ge(packed_in.sem, packed_in.at(0, 1))
                act.activation(A[:, :, :].rearrange("p h n -> p (h n)"), part("A_log"), ACT.Exp).then_inc(ready.sem, 1)

            @block.vector
            def _(dve):
                dve.memset(xp[:, :, 0:PAD], 0.0).then_inc(ready.sem, 1)
                dve.memset(dA[:, :, :, 0:1], 0.0).then_inc(ready.sem, 1)
                dve.wait_ge(packed_in.sem, packed_in.at(0, 1))
                for f in range(HALF):
                    dve.tensor_scalar(diag[:, f, :], pr.ident[:, :], skip_d[:, f:f + 1], None,
                                      ALU.mult).then_inc(ready.sem, 1)
                dve.wait_ge(ready.sem, ready.at(0, 5))
                dve.tensor_scalar(A[:, :, :], A[:, :, :], -1.0, None, ALU.mult).then_inc(ready.sem, 1)
        packed_in.end(1)
        ready.end(1)

        xz = pr.step("m_xz", 4)
        xpc = pr.step("m_xp_copied", 2)
        szd = pr.step("m_silu_z", 2)
        conv = pr.step("m_conv", 8)
        ud = pr.step("m_u", 2)
        dbl = pr.step("m_x_dbl", 1)
        split = pr.step("m_split", 7)
        dtp = pr.step("m_dt_proj", 1)
        absd = pr.step("m_abs", 1)
        expd = pr.step("m_softplus_exp", 1)
        lnd = pr.step("m_softplus_log", 1)
        dmax = pr.step("m_dt_relu", 1)
        dtd = pr.step("m_dt", 1)
        dtud = pr.step("m_dtu", 1)
        bcast = pr.step("m_bc_spread", DS)
        decay = pr.step("m_decay", DS)
        bcopy = pr.step("m_b_copied", DS)
        driven = pr.step("m_driven", DS)
        scanned = pr.step("m_scanned", DS)
        read = pr.step("m_state_read", DS)
        ysum = pr.step("m_y_summed", DS + 1)
        gated = pr.step("m_gated", 1)
        outp = pr.step("m_out", 1)
        ocopy = pr.step("m_out_copied", 1)
        omean = pr.step("m_mean", 1)
        ocent = pr.step("m_centered", 1)
        osqd = pr.step("m_squared", 1)
        ovar = pr.step("m_var", 1)
        oroot = pr.step("m_root", 1)
        orsd = pr.step("m_inv", 1)
        oinv = pr.step("m_scaled", 2)
        fin = pr.step("m_done", 1)

        with nc.Block() as block:
            @block.tensor
            def _(pe):
                with pe.Fori(0, B) as i:
                    pe.wait_ge(fin.sem, fin.at(i, 0))
                    for c in range(4):
                        pe.matmul(ps[:, c, :], lhsT=in_w[:, c * P:(c + 1) * P], rhs=cols(XR, i), start=True,
                                  stop=True).then_inc(xz.sem, 1)
                    pe.wait_ge(ud.sem, ud.at(i, 2))
                    for f in range(HALF):
                        last = pe.matmul(ps[0:40, 4, :], lhsT=xp_w[:, f, :], rhs=u[:, f, :], start=(f == 0),
                                         stop=(f == HALF - 1))
                    last.then_inc(dbl.sem, 1)
                    pe.wait_ge(split.sem, split.at(i, 1))
                    for f in range(HALF):
                        last = pe.matmul(ps[:, 5 + f, :], lhsT=dt_w[:, f * P:(f + 1) * P], rhs=dts[32:40, :],
                                         start=True, stop=True)
                    last.then_inc(dtp.sem, 1)
                    for f in range(HALF):
                        last = pe.matmul(ps[:, f, :], lhsT=diag[:, f, :], rhs=u[:, f, :], start=True, stop=False)
                    last.then_inc(ysum.sem, 1)
                    pe.wait_ge(szd.sem, szd.at(i, 2))
                    pe.wait_ge(split.sem, split.at(i, 7))

                    def spread(n):
                        if n >= 2:
                            pe.wait_ge(bcopy.sem, bcopy.at(i, n - 1))
                            pe.wait_ge(read.sem, read.at(i, n - 1))
                        pe.matmul(ps[:, 2 + n % 2, :], lhsT=pr.sel[:, n, :], rhs=bc[:, :], start=True, stop=True)
                        pe.matmul(ps[:, 4 + n % 2, :], lhsT=pr.sel[:, DS + n, :], rhs=bc[:, :], start=True,
                                  stop=True).then_inc(bcast.sem, 1)

                    def sum_y(n):
                        pe.wait_ge(read.sem, read.at(i, n + 1))
                        for f in range(HALF):
                            last = pe.matmul(ps[:, f, :], lhsT=pr.ident[:, :], rhs=hc[:, n % 2, f, :], start=False,
                                             stop=(n == DS - 1))
                        last.then_inc(ysum.sem, 1)

                    pe.wait_ge(dmax.sem, dmax.at(i, 1))
                    pe.wait_ge(absd.sem, absd.at(i, 1))
                    spread(0)
                    for n in range(DS):
                        if n + 1 < DS:
                            spread(n + 1)
                        sum_y(n)
                    pe.wait_ge(gated.sem, gated.at(i, 1))
                    for f in range(HALF):
                        last = pe.matmul(ps[:, 6, :], lhsT=out_w[:, f, :], rhs=yz[:, f, :], start=(f == 0),
                                         stop=(f == HALF - 1))
                    last.then_inc(outp.sem, 1)
                    pe.wait_ge(ocopy.sem, ocopy.at(i, 1))
                    pe.matmul(ps[:, 7, :], lhsT=pr.mean[:, :], rhs=ob[:, :], start=True, stop=True).then_inc(omean.sem, 1)
                    pe.wait_ge(osqd.sem, osqd.at(i, 1))
                    pe.matmul(ps[:, 6, :], lhsT=pr.mean[:, :], rhs=osq[:, :], start=True, stop=True).then_inc(ovar.sem, 1)

            @block.scalar
            def _(act):
                with act.Fori(0, B) as i:
                    for f in range(HALF):
                        act.wait_ge(xz.sem, xz.at(i, f + 1))
                        if f == 0:
                            act.wait_ge(fin.sem, fin.at(i, 0))
                        act.activation(xp[:, f, PAD:], ps[:, f, :], ACT.Copy).then_inc(xpc.sem, 1)
                    for f in range(HALF):
                        act.wait_ge(xz.sem, xz.at(i, 3 + f))
                        act.activation(sz[:, f, :], ps[:, 2 + f, :], ACT.Silu).then_inc(szd.sem, 1)
                    for f in range(HALF):
                        act.wait_ge(conv.sem, conv.at(i, 4 * HALF - 1 + f))
                        act.activation(u[:, f, :], cv[:, f, :], ACT.Silu).then_inc(ud.sem, 1)
                    act.preload_act_table_set(LOG_EXP)
                    act.wait_ge(dtp.sem, dtp.at(i, 1))
                    for f in range(HALF):
                        last = act.activation(av[:, f, :], ps[:, 5 + f, :], ACT.Abs, bias=dt_b[:, f:f + 1])
                    last.then_inc(absd.sem, 1)
                    act.wait_ge(absd.sem, absd.at(i, 1))
                    act.activation(av[:, :, :], av[:, :, :], ACT.Exp, scale=-1.0).then_inc(expd.sem, 1)
                    act.wait_ge(expd.sem, expd.at(i, 1))
                    act.activation(av[:, :, :], av[:, :, :], ACT.Ln, bias=1.0).then_inc(lnd.sem, 1)
                    act.wait_ge(dtd.sem, dtd.at(i, 1))
                    for n in range(DS):
                        s = n % 2
                        if n >= 2:
                            act.wait_ge(scanned.sem, scanned.at(i, n - 1))
                        for f in range(HALF):
                            last = act.activation(dA[:, s, f, 1:], dt[:, f, 1:], ACT.Exp, scale=A[:, f, n:n + 1])
                        last.then_inc(decay.sem, 1)
                        act.wait_ge(bcast.sem, bcast.at(i, n + 1))
                        if n >= 2:
                            act.wait_ge(driven.sem, driven.at(i, n - 1))
                        act.activation(Bs[:, s, :], ps[:, 2 + s, :], ACT.Copy).then_inc(bcopy.sem, 1)
                    act.wait_ge(outp.sem, outp.at(i, 1))
                    act.activation(ob[:, :], ps[:, 6, :], ACT.Copy).then_inc(ocopy.sem, 1)
                    act.wait_ge(ocent.sem, ocent.at(i, 1))
                    act.activation(osq[:, :], oc[:, :], ACT.Square).then_inc(osqd.sem, 1)
                    act.wait_ge(ovar.sem, ovar.at(i, 1))
                    act.activation(osd[:, :], ps[:, 6, :], ACT.Ln, bias=pr.eps[:, 0:1]).then_inc(oroot.sem, 1)
                    act.wait_ge(oroot.sem, oroot.at(i, 1))
                    act.activation(osd[:, :], osd[:, :], ACT.Exp, scale=-0.5).then_inc(orsd.sem, 1)

            @block.gpsimd
            def _(pool):
                with pool.Fori(0, B) as i:
                    pool.wait_ge(dtud.sem, dtud.at(i, 1))
                    for n in range(DS):
                        s = n % 2
                        pool.wait_ge(bcopy.sem, bcopy.at(i, n + 1))
                        if n >= 2:
                            pool.wait_ge(scanned.sem, scanned.at(i, n - 1))
                        pool.tensor_tensor(dBu[:, s, :, :], dtu[:, :, :],
                                           Bs[:, s, :].unsqueeze(1).to_broadcast([P, HALF, T]),
                                           ALU.mult).then_inc(driven.sem, 1)

            @block.vector
            def _(dve):
                with dve.Fori(0, B) as i:
                    for k in range(4):
                        for f in range(HALF):
                            if k == 0:
                                dve.wait_ge(xpc.sem, xpc.at(i, f + 1))
                                ins = dve.tensor_scalar(cv[:, f, :], xp[:, f, 0:T], conv_w[:, f, 0:1],
                                                        conv_b[:, f:f + 1], ALU.mult, ALU.add)
                            else:
                                dve.wait_ge(conv.sem, conv.at(i, 2 * k + f - 1))
                                ins = dve.scalar_tensor_tensor(out=cv[:, f, :], in0=xp[:, f, k:k + T],
                                                               scalar=conv_w[:, f, k:k + 1], in1=cv[:, f, :],
                                                               op0=ALU.mult, op1=ALU.add)
                            ins.then_inc(conv.sem, 1)
                    dve.wait_ge(dbl.sem, dbl.at(i, 1))
                    dve.tensor_copy(dts[32:40, :], ps[32:40, 4, :]).then_inc(split.sem, 1)
                    dve.tensor_copy(bc[0:32, :], ps[0:32, 4, :]).then_inc(split.sem, 1)
                    dve.wait_ge(split.sem, split.at(i, 2))
                    dve.tensor_tensor(r1[:, :], ps[0:32, 4, :], bc[0:32, :], ALU.subtract).then_inc(split.sem, 1)
                    dve.wait_ge(split.sem, split.at(i, 3))
                    dve.tensor_copy(mid[:, :], r1[:, :]).then_inc(split.sem, 1)
                    dve.tensor_copy(bc[32:64, :], r1[:, :]).then_inc(split.sem, 1)
                    dve.wait_ge(split.sem, split.at(i, 4))
                    dve.tensor_tensor(r2[:, :], r1[:, :], mid[:, :], ALU.subtract).then_inc(split.sem, 1)
                    dve.wait_ge(split.sem, split.at(i, 6))
                    dve.tensor_copy(bc[64:96, :], r2[:, :]).then_inc(split.sem, 1)
                    dve.wait_ge(dtp.sem, dtp.at(i, 1))
                    dve.wait_ge(absd.sem, absd.at(i, 1))
                    for f in range(HALF):
                        last = dve.tensor_scalar(dt[:, f, :], ps[:, 5 + f, :], dt_b[:, f:f + 1], 0.0, ALU.add, ALU.max)
                    last.then_inc(dmax.sem, 1)
                    dve.wait_ge(dmax.sem, dmax.at(i, 1))
                    dve.wait_ge(lnd.sem, lnd.at(i, 1))
                    dve.tensor_tensor(dt[:, :, :], dt[:, :, :], av[:, :, :], ALU.add).then_inc(dtd.sem, 1)
                    dve.wait_ge(dtd.sem, dtd.at(i, 1))
                    dve.wait_ge(ud.sem, ud.at(i, 2))
                    dve.tensor_tensor(dtu[:, :, :], dt[:, :, :], u[:, :, :], ALU.mult).then_inc(dtud.sem, 1)
                    for n in range(DS):
                        s = n % 2
                        dve.wait_ge(decay.sem, decay.at(i, n + 1))
                        dve.wait_ge(driven.sem, driven.at(i, n + 1))
                        if n >= 2:
                            dve.wait_ge(read.sem, read.at(i, n - 1))
                        dve.tensor_tensor_scan(hh[:, s, :, :].rearrange("p h t -> p (h t)"),
                                               dA[:, s, :, :].rearrange("p h t -> p (h t)"),
                                               dBu[:, s, :, :].rearrange("p h t -> p (h t)"), 0.0,
                                               ALU.mult, ALU.add).then_inc(scanned.sem, 1)
                        dve.wait_ge(scanned.sem, scanned.at(i, n + 1))
                        dve.wait_ge(bcast.sem, bcast.at(i, n + 1))
                        if n >= 2:
                            dve.wait_ge(ysum.sem, ysum.at(i, n))
                        dve.tensor_tensor(hc[:, s, :, :], hh[:, s, :, :],
                                          ps[:, 4 + s, :].unsqueeze(1).to_broadcast([P, HALF, T]),
                                          ALU.mult).then_inc(read.sem, 1)
                    dve.wait_ge(ysum.sem, ysum.at(i, DS + 1))
                    dve.wait_ge(szd.sem, szd.at(i, 2))
                    dve.tensor_tensor(yz[:, :, :], ps[:, 0:2, :], sz[:, :, :], ALU.mult).then_inc(gated.sem, 1)
                    dve.wait_ge(omean.sem, omean.at(i, 1))
                    dve.tensor_tensor(oc[:, :], ob[:, :], ps[:, 7, :], ALU.subtract).then_inc(ocent.sem, 1)
                    dve.wait_ge(orsd.sem, orsd.at(i, 1))
                    dve.wait_ge(ocent.sem, ocent.at(i, 1))
                    dve.wait_ge(osqd.sem, osqd.at(i, 1))
                    dve.tensor_tensor(oc[:, :], oc[:, :], osd[:, :], ALU.mult).then_inc(oinv.sem, 1)
                    dve.wait_ge(oinv.sem, oinv.at(i, 1))
                    dve.tensor_scalar(oc[:, :], oc[:, :], ln_w, ln_b, ALU.mult, ALU.add).then_inc(oinv.sem, 1)
                    dve.wait_ge(oinv.sem, oinv.at(i, 2))
                    dve.tensor_tensor(cols(XR, i), cols(XR, i), oc[:, :], ALU.add).then_inc(fin.sem, 1)

        for s in (xz, xpc, szd, conv, ud, dbl, split, dtp, absd, expd, lnd, dmax, dtd, dtud, bcast, decay, bcopy, driven,
                  scanned, read, ysum, gated, outp, ocopy, omean, ocent, osqd, ovar, oroot, orsd, oinv, fin):
            s.end(B)


def add_stream(pr, scale):
    nc, added = pr.nc, pr.step("stream_added", B)
    with nc.Block() as block:
        @block.vector
        def _(dve):
            for b in range(B):
                x, y = pr.X[:, b * T:(b + 1) * T], pr.XN[:, b * T:(b + 1) * T]
                dve.scalar_tensor_tensor(out=x, in0=y, scalar=scale, in1=x, op0=ALU.mult,
                                         op1=ALU.add).then_inc(added.sem, 1)
    added.end(1)


def cell_phase(pr, tag, packed):
    nc, ps, X, XN = pr.nc, pr.psum, pr.X, pr.XN
    o = CELL_PACK
    with ExitStack() as ctx:
        def sb(name):
            return pr.sb(name + tag, [P, 2, T], ctx=ctx)

        W = pr.sb("cw" + tag, [P, o["total"]], ctx=ctx)

        def part(name):
            return W[:, o[name][0]:o[name][1]]

        xp, al, be, v, bv, h, sh, co = (sb(x) for x in ("cxp", "cal", "cbe", "cv_", "cbv", "ch", "csh", "cco"))
        w_in = pr.step("c_packed", 1, 16)
        proj = pr.step("c_proj", 2)
        xpd = pr.step("c_xp", 2)
        gates = pr.step("c_gates", 2)
        acts = pr.step("c_acts", 2)
        bvd = pr.step("c_bv", 2)
        scanned = pr.step("c_scanned", 2)
        shd = pr.step("c_silu_h", 2)
        cod = pr.step("c_out", 2)
        outp = pr.step("c_out_proj", 2)
        fin = pr.step("c_done", 2)
        n = B // 2
        with nc.Block() as block:
            @block.sync
            def _(sp):
                sp.dma_start(W[:, :], packed).then_inc(w_in.sem, 16)

            @block.tensor
            def _(pe):
                pe.wait_ge(w_in.sem, w_in.at(0, 1))
                with pe.Fori(0, n) as i:
                    for s in range(2):
                        pe.wait_ge(xpd.sem, xpd.at(i, s - 1))
                        pe.wait_ge(fin.sem, fin.at(i, s - 1))
                        pe.matmul(ps[:, 4 * s, :], lhsT=part("w_in"), rhs=cols(XN, 2 * i + s), start=True,
                                  stop=True).then_inc(proj.sem, 1)
                    for s in range(2):
                        pe.wait_ge(xpd.sem, xpd.at(i, s + 1))
                        pe.wait_ge(acts.sem, acts.at(i, s - 1))
                        for k, name in enumerate(("w_a", "w_b", "w_v")):
                            last = pe.matmul(ps[:, 4 * s + 1 + k, :], lhsT=part(name), rhs=xp[:, s, :], start=True, stop=True)
                        last.then_inc(gates.sem, 1)
                    for s in range(2):
                        pe.wait_ge(cod.sem, cod.at(i, s + 1))
                        pe.matmul(ps[:, 4 * s, :], lhsT=part("w_out"), rhs=co[:, s, :], start=True,
                                  stop=True).then_inc(outp.sem, 1)

            @block.scalar
            def _(act):
                with act.Fori(0, n) as i:
                    for s in range(2):
                        act.wait_ge(proj.sem, proj.at(i, s + 1))
                        act.wait_ge(gates.sem, gates.at(i, s - 1))
                        act.activation(xp[:, s, :], ps[:, 4 * s, :], ACT.Silu).then_inc(xpd.sem, 1)
                    for s in range(2):
                        act.wait_ge(gates.sem, gates.at(i, s + 1))
                        act.wait_ge(scanned.sem, scanned.at(i, s - 1))
                        act.activation(al[:, s, :], ps[:, 4 * s + 1, :], ACT.Sigmoid, bias=part("b_a"))
                        act.activation(be[:, s, :], ps[:, 4 * s + 2, :], ACT.Sigmoid, bias=part("b_b"))
                        act.activation(v[:, s, :], ps[:, 4 * s + 3, :], ACT.Tanh, bias=part("b_v")).then_inc(acts.sem, 1)
                    for s in range(2):
                        act.wait_ge(scanned.sem, scanned.at(i, s + 1))
                        act.wait_ge(cod.sem, cod.at(i, s - 1))
                        act.activation(sh[:, s, :], h[:, s, :], ACT.Silu).then_inc(shd.sem, 1)

            @block.vector
            def _(dve):
                with dve.Fori(0, n) as i:
                    for s in range(2):
                        dve.wait_ge(acts.sem, acts.at(i, s + 1))
                        dve.wait_ge(scanned.sem, scanned.at(i, s - 1))
                        dve.tensor_tensor(bv[:, s, :], be[:, s, :], v[:, s, :], ALU.mult).then_inc(bvd.sem, 1)
                    for s in range(2):
                        dve.wait_ge(bvd.sem, bvd.at(i, s + 1))
                        dve.wait_ge(shd.sem, shd.at(i, s - 1))
                        dve.wait_ge(cod.sem, cod.at(i, s - 1))
                        dve.tensor_tensor_scan(h[:, s, :], al[:, s, :], bv[:, s, :], 0.0, ALU.mult,
                                               ALU.add).then_inc(scanned.sem, 1)
                    for s in range(2):
                        dve.wait_ge(shd.sem, shd.at(i, s + 1))
                        dve.wait_ge(scanned.sem, scanned.at(i, s + 1))
                        dve.wait_ge(outp.sem, outp.at(i, s - 1))
                        dve.tensor_tensor(co[:, s, :], h[:, s, :], sh[:, s, :], ALU.mult).then_inc(cod.sem, 1)
                    for s in range(2):
                        dve.wait_ge(outp.sem, outp.at(i, s + 1))
                        x = cols(X, 2 * i + s)
                        dve.tensor_tensor(x, x, ps[:, 4 * s, :], ALU.add).then_inc(fin.sem, 1)

        w_in.end(1)
        for s in (proj, xpd, gates, acts, bvd, scanned, shd, cod, outp, fin):
            s.end(n)


def attention_layer(pr, tag, packed, tables):
    nc, ps, XR = pr.nc, pr.psum, pr.XN
    o = FFN_PACK
    cut = o["w2"][1]
    ctx = ExitStack()
    with ctx:
        Wh = pr.sb("fwh" + tag, [P, cut], F32R, ctx)
        Wl = pr.sb("fwl" + tag, [P, cut], F32R, ctx)
        vec = pr.sb("fvec" + tag, [P, o["total"] - cut], ctx=ctx)
        rot = pr.sb("rot" + tag, [P, 4, T], ctx=ctx)

        def both(name):
            return Wh[:, o[name][0]:o[name][1]], Wl[:, o[name][0]:o[name][1]]

        def part(name):
            return vec[:, o[name][0] - cut:o[name][1] - cut]

        w_in = pr.step("f_packed", 3, 16)
        w_high = pr.step("f_w_high", 1)
        ready = pr.step("f_ready", 5)
        with ExitStack() as tctx:
            stage = pr.sb("fstage" + tag, [P, cut], ctx=tctx)
            with nc.Block() as block:
                @block.sync
                def _(sp):
                    sp.dma_start(stage[:, :], packed[:, 0:cut]).then_inc(w_in.sem, 16)
                    sp.dma_start(vec[:, :], packed[:, cut:]).then_inc(w_in.sem, 16)
                    sp.dma_start(rot[:, :, :].rearrange("p c t -> p (c t)"), tables).then_inc(w_in.sem, 16)

                @block.scalar
                def _(act):
                    act.wait_ge(w_in.sem, w_in.at(0, 3))
                    act.activation(Wh[:, :], stage[:, :], ACT.Copy).then_inc(w_high.sem, 1)

                @block.vector
                def _(dve):
                    dve.wait_ge(w_in.sem, w_in.at(0, 3))
                    for k, name in enumerate(("qs", "qsr", "ks", "ksr")):
                        dve.tensor_scalar(rot[:, k, :], rot[:, k, :], part(name), None, ALU.mult).then_inc(ready.sem, 1)
                    dve.wait_ge(w_high.sem, w_high.at(0, 1))
                    dve.tensor_tensor(Wl[:, :], stage[:, :], Wh[:, :].bitcast(F32), ALU.subtract).then_inc(ready.sem, 1)
        w_in.end(1)
        w_high.end(1)
        ready.end(1)
        with ExitStack() as actx:
            attention_phase(pr, tag, actx, both, rot)
        with ExitStack() as fctx:
            feed_forward_phase(pr, tag, fctx, both, part)


def attention_phase(pr, tag, ctx, both, rot):
    nc, ps, XR = pr.nc, pr.psum, pr.XN

    def sb(name, shape, dt=F32):
        return pr.sb(name + tag, shape, dt, ctx)

    hTh = sb("hTh", [P, WIN + T], F32R)
    hTl = sb("hTl", [P, WIN + T], F32R)
    sq = sb("sq_", [P, 4, T])
    rot_a = sb("rot_a", [P, 2, T])
    rot_b = sb("rot_b", [P, 2, T])
    qf = sb("qf", [P, PAIRS, T])
    kr = sb("kr", [P, PAIRS, T])
    kn = sb("kn", [P, PAIRS, T])
    kf = sb("kf", [P, PAIRS, WIN + T])
    cr = sb("cr", [P, PAIRS * NW])
    cq = sb("cq", [P, PAIRS * NW])
    V = sb("V", [P, NW, HEADS * DH])
    mx = sb("mx", [P, NW])
    nb = sb("nb", [P, 2, NW])
    sm = sb("sm", [P, 2, NW])
    rsm = sb("rsm", [P, 2, NW])
    Pr = sb("Pr", [P, 2, NW, P])
    PT = sb("PT", [P, NW, P])
    oTh = sb("oTh", [P, PAIRS, T], F32R)
    oTl = sb("oTl", [P, PAIRS, T], F32R)

    padded = pr.step("f_padded", 3)
    with nc.Block() as block:
        @block.vector
        def _(dve):
            dve.memset(hTh[:, 0:WIN + 1].bitcast(F32), 0.0).then_inc(padded.sem, 1)
            dve.memset(hTl[:, 0:WIN + 1].bitcast(F32), 0.0).then_inc(padded.sem, 1)
            dve.memset(kf[:, :, 0:WIN], 0.0).then_inc(padded.sem, 1)
    padded.end(1)

    shifted = pr.step("f_shifted", 2)
    shift_low = pr.step("f_shifted_low", 2)
    proj = pr.step("f_proj", 2 * PAIRS)
    squared = pr.step("f_squared", 2 * PAIRS)
    rota = pr.step("f_rotated_parts", 2 * PAIRS)
    rotb = pr.step("f_rotated", 2 * PAIRS)
    knorm = pr.step("f_k_norm", PAIRS)
    ksd = pr.step("f_k_norm_kept", PAIRS)
    kroot = pr.step("f_k_root", 1)
    kinv = pr.step("f_k_inv", 1)
    kfd = pr.step("f_k", PAIRS)
    qnorm = pr.step("f_q_norm", PAIRS)
    cqs = pr.step("f_q_norm_kept", PAIRS)
    qroot = pr.step("f_q_root", 1)
    qlog = pr.step("f_q_log", 1)
    vp = pr.step("f_v_proj", NW)
    va = pr.step("f_v_even", NW // 2)
    vb = pr.step("f_v_odd", NW // 2)
    sim = pr.step("f_sim", PAIRS)
    maxed = pr.step("f_max", PAIRS)
    nbd = pr.step("f_bias", PAIRS)
    expd = pr.step("f_exp", PAIRS)
    rsd = pr.step("f_sum_inv", PAIRS)
    pn = pr.step("f_probs", PAIRS)
    turned = pr.step("f_turned", PAIRS)
    pta = pr.step("f_turned_copied_a", PAIRS)
    ptb = pr.step("f_turned_copied_b", PAIRS)
    pv = pr.step("f_pv", PAIRS)
    oTd = pr.step("f_o", 2 * PAIRS)
    wod = pr.step("f_wo", 1)
    x1d = pr.step("f_x1", 1)
    heads = [slice(a * DH, (a + 1) * DH) for a in range(2)]
    SCORE, TURN, PROJ, OUT, NORM = 0, 2, 4, 6, 7

    def three_passes(pe, out, w, x, start, stop):
        (wh, wl), (xh, xl) = w, x
        pe.matmul(out, lhsT=wh, rhs=xh, start=start, stop=False)
        pe.matmul(out, lhsT=wl, rhs=xh, start=False, stop=False)
        return pe.matmul(out, lhsT=wh, rhs=xl, start=False, stop=stop)

    with nc.Block() as block:
        @block.tensor
        def _(pe):
            def project(b, p, isk):
                unit = 2 * p + isk
                if unit == 0:
                    pe.wait_ge(shift_low.sem, shift_low.at(b, 2))
                    pe.wait_ge(va.sem, va.at(b, 0))
                    pe.wait_ge(vb.sem, vb.at(b, 0))
                pe.wait_ge(rota.sem, rota.at(b, unit))
                for r, name in enumerate(("wk", "wkr") if isk else ("wq", "wqr")):
                    h, l = both(name)
                    c = slice(p * P, (p + 1) * P)
                    last = three_passes(pe, ps[:, PROJ + r, :], (h[:, c], l[:, c]), (hTh[:, WIN:], hTl[:, WIN:]),
                                        True, True)
                last.then_inc(proj.sem, 1)

            def k_norm(b, p):
                pe.wait_ge(squared.sem, squared.at(b, 2 * p + 2))
                pe.wait_ge(cqs.sem, cqs.at(b, p))
                pe.matmul(ps[:, NORM, :], lhsT=pr.heads[:, :], rhs=sq[:, (2 * p + 1) % 4, :], start=True,
                          stop=True).then_inc(knorm.sem, 1)

            def q_norm(b, p):
                pe.wait_ge(ksd.sem, ksd.at(b, p + 1))
                for w in range(NW // 2):
                    last = pe.matmul(ps[:, NORM, w:w + NW // 2 + 1:NW // 2], lhsT=sq[:, (2 * p) % 4, w * P:(w + 1) * P],
                                     rhs=pr.heads[:, DH - 1:DH + 1], start=True, stop=True)
                last.then_inc(qnorm.sem, 1)

            def values_of(b):
                pe.wait_ge(rota.sem, rota.at(b, 2 * PAIRS))
                wv = both("wv")
                for w in range(NW):
                    read = vb if w % 2 else va
                    pe.wait_ge(read.sem, read.at(b, w // 2))
                    c = slice(w * WIN, (w + 2) * WIN)
                    three_passes(pe, ps[:, PROJ + w % 2, :], (hTh[:, c], hTl[:, c]), wv, True, True).then_inc(vp.sem, 1)

            def scores(b, p):
                pe.wait_ge(kfd.sem, kfd.at(b, p + 1))
                pe.wait_ge(rotb.sem, rotb.at(b, 2 * p + 1))
                pe.wait_ge(expd.sem, expd.at(b, p))
                for half in range(2):
                    pe.matmul(ps[:, SCORE + half, :], lhsT=pr.ident_b[:, :], rhs=pr.mask[:, :], start=True, stop=False,
                              skip_group_check=True)
                for w in range(NW):
                    for a in range(2):
                        at = w // 2
                        last = pe.matmul(ps[heads[w % 2], SCORE + a, at * P:(at + 1) * P],
                                         lhsT=qf[heads[a], p, w * WIN:(w + 1) * WIN],
                                         rhs=kf[heads[a], p, w * WIN:(w + 2) * WIN], start=False, stop=True,
                                         skip_group_check=True)
                last.then_inc(sim.sem, 1)

            def turn(b, p):
                pe.wait_ge(pn.sem, pn.at(b, p + 1))
                pe.wait_ge(pta.sem, pta.at(b, p))
                pe.wait_ge(ptb.sem, ptb.at(b, p))
                for at in range(NW):
                    last = pe.transpose(ps[:, TURN + at // 4, (at % 4) * P:(at % 4 + 1) * P], Pr[:, p % 2, at, :],
                                        pr.ident[:, :])
                last.then_inc(turned.sem, 1)

            def weigh(b, p):
                pe.wait_ge(pta.sem, pta.at(b, p + 1))
                pe.wait_ge(ptb.sem, ptb.at(b, p + 1))
                if p == 0:
                    pe.wait_ge(va.sem, va.at(b, NW // 2))
                    pe.wait_ge(vb.sem, vb.at(b, NW // 2))
                    pe.wait_ge(x1d.sem, x1d.at(b, 0))
                pe.wait_ge(oTd.sem, oTd.at(b, 2 * p))
                for w in range(NW):
                    for a in range(2):
                        last = pe.matmul(ps[heads[a], OUT, w * WIN:(w + 1) * WIN],
                                         lhsT=V[:, w, (2 * p + a) * DH:(2 * p + a + 1) * DH],
                                         rhs=PT[:, NW // 2 * a + w // 2, heads[w % 2]], start=True, stop=True)
                last.then_inc(pv.sem, 1)

            def out_product(b):
                pe.wait_ge(oTd.sem, oTd.at(b, 2 * PAIRS))
                h, l = both("wo")
                for p in range(PAIRS):
                    c = slice(p * P, (p + 1) * P)
                    last = three_passes(pe, ps[:, OUT, :], (h[:, c], l[:, c]), (oTh[:, p, :], oTl[:, p, :]), p == 0,
                                        p == PAIRS - 1)
                last.then_inc(wod.sem, 1)

            def sequence(b, nxt):
                for p in range(PAIRS):
                    scores(b, p)
                    if nxt is not None:
                        if p:
                            q_norm(nxt, p - 1)
                        project(nxt, p, 0)
                    if p:
                        turn(b, p - 1)
                    if nxt is not None:
                        project(nxt, p, 1)
                    if p:
                        weigh(b, p - 1)
                    if nxt is not None:
                        k_norm(nxt, p)
                turn(b, PAIRS - 1)
                if nxt is not None:
                    q_norm(nxt, PAIRS - 1)
                weigh(b, PAIRS - 1)
                if nxt is not None:
                    values_of(nxt)
                out_product(b)

            for p in range(PAIRS):
                project(0, p, 0)
                project(0, p, 1)
                k_norm(0, p)
                q_norm(0, p)
            values_of(0)
            with pe.Fori(0, B - 1) as i:
                sequence(i, i + 1)
            sequence(B - 1, None)

        @block.scalar
        def _(act):
            act.preload_act_table_set(LOG_EXP)

            def square(b, p, isk):
                unit = 2 * p + isk
                act.wait_ge(proj.sem, proj.at(b, unit + 1))
                act.wait_ge(qnorm.sem, qnorm.at(b, p - 1))
                act.activation(sq[:, unit % 4, :], ps[:, PROJ, :], ACT.Square).then_inc(squared.sem, 1)

            def probs(b, p, half):
                if half == 0:
                    act.wait_ge(nbd.sem, nbd.at(b, p + 1))
                    act.wait_ge(turned.sem, turned.at(b, p - 1))
                    act.wait_ge(rsd.sem, rsd.at(b, p - 1))
                for w in range(4 * half, 4 * half + 4):
                    last = act.activation(Pr[:, p % 2, w, :], ps[:, SCORE + w // 4, (w % 4) * P:(w % 4 + 1) * P],
                                          ACT.Exp, bias=nb[:, p % 2, w:w + 1],
                                          scale=cq[:, p * NW + w:p * NW + w + 1],
                                          accum_out=sm[:, p % 2, w:w + 1])
                if half:
                    last.then_inc(expd.sem, 1)

            def copy_turned(b, p):
                act.wait_ge(turned.sem, turned.at(b, p + 1))
                act.wait_ge(pv.sem, pv.at(b, p))
                act.activation(PT[:, 0:4, :].rearrange("p w q -> p (w q)"), ps[:, TURN, :],
                               ACT.Copy).then_inc(pta.sem, 1)

            def roots(b):
                act.wait_ge(ksd.sem, ksd.at(b, PAIRS))
                act.activation(kn[:, :, :], kn[:, :, :], ACT.Ln).then_inc(kroot.sem, 1)
                act.wait_ge(kroot.sem, kroot.at(b, 1))
                act.activation(kn[:, :, :], kn[:, :, :], ACT.Exp, scale=-0.5).then_inc(kinv.sem, 1)
                act.wait_ge(cqs.sem, cqs.at(b, PAIRS))
                act.wait_ge(expd.sem, expd.at(b, 0))
                act.wait_ge(nbd.sem, nbd.at(b, 0))
                act.activation(cr[:, :], cr[:, :], ACT.Ln).then_inc(qlog.sem, 1)
                act.wait_ge(qlog.sem, qlog.at(b, 1))
                act.activation(cq[:, :], cr[:, :], ACT.Exp, scale=-0.5).then_inc(qroot.sem, 1)

            def copy_values(b):
                act.wait_ge(pv.sem, pv.at(b, 0))
                for w in range(0, NW, 2):
                    act.wait_ge(vp.sem, vp.at(b, w + 1))
                    act.activation(V[:, w, :], ps[:, PROJ, :], ACT.Copy).then_inc(va.sem, 1)

            def sequence(b, nxt):
                for p in range(PAIRS):
                    if nxt is not None:
                        square(nxt, p, 0)
                    probs(b, p, 0)
                    if p:
                        copy_turned(b, p - 1)
                    if nxt is not None:
                        square(nxt, p, 1)
                    probs(b, p, 1)
                copy_turned(b, PAIRS - 1)
                if nxt is not None:
                    roots(nxt)
                    copy_values(nxt)

            for p in range(PAIRS):
                square(0, p, 0)
                square(0, p, 1)
            roots(0)
            copy_values(0)
            with act.Fori(0, B - 1) as i:
                sequence(i, i + 1)
            sequence(B - 1, None)

        @block.gpsimd
        def _(pool):
            def rotate(b, p, isk):
                unit = 2 * p + isk
                pool.wait_ge(rota.sem, rota.at(b, unit + 1))
                if isk:
                    pool.wait_ge(kfd.sem, kfd.at(b, p + 1 - PAIRS))
                else:
                    pool.wait_ge(sim.sem, sim.at(b, p + 1 - PAIRS))
                dst = kr if isk else qf
                pool.tensor_tensor(dst[:, p, :], rot_a[:, unit % 2, :], rot_b[:, unit % 2, :],
                                   ALU.add).then_inc(rotb.sem, 1)

            def normalise(b, p):
                pool.wait_ge(rsd.sem, rsd.at(b, p + 1))
                pool.tensor_tensor(Pr[:, p % 2, :, :], Pr[:, p % 2, :, :],
                                   rsm[:, p % 2, :].unsqueeze(2).to_broadcast([P, NW, P]),
                                   ALU.mult).then_inc(pn.sem, 1)

            def keys(b):
                pool.wait_ge(kinv.sem, kinv.at(b, 1))
                pool.wait_ge(rotb.sem, rotb.at(b, 2 * PAIRS))
                pool.wait_ge(sim.sem, sim.at(b, 0))
                for p in range(PAIRS):
                    pool.tensor_tensor(kf[:, p, WIN:], kr[:, p, :], kn[:, p, :], ALU.mult).then_inc(kfd.sem, 1)

            def sequence(b, nxt):
                for p in range(PAIRS):
                    if p:
                        normalise(b, p - 1)
                    if nxt is not None:
                        rotate(nxt, p, 0)
                        rotate(nxt, p, 1)
                normalise(b, PAIRS - 1)
                if nxt is not None:
                    keys(nxt)

            for p in range(PAIRS):
                rotate(0, p, 0)
                rotate(0, p, 1)
            keys(0)
            with pool.Fori(0, B - 1) as i:
                sequence(i, i + 1)
            sequence(B - 1, None)

        @block.vector
        def _(dve):
            def shift(b):
                dve.wait_ge(vp.sem, vp.at(b, 0))
                dve.tensor_copy(hTh[0:DH, WIN:], XR[0:DH, bass.ds(b * T, T)]).then_inc(shifted.sem, 1)
                dve.tensor_copy(hTh[DH:P, WIN + 1:], XR[DH:P, bass.ds(b * T, T - 1)]).then_inc(shifted.sem, 1)
                dve.wait_ge(shifted.sem, shifted.at(b, 2))
                dve.tensor_tensor(hTl[0:DH, WIN:], XR[0:DH, bass.ds(b * T, T)], hTh[0:DH, WIN:].bitcast(F32),
                                  ALU.subtract).then_inc(shift_low.sem, 1)
                dve.tensor_tensor(hTl[DH:P, WIN + 1:], XR[DH:P, bass.ds(b * T, T - 1)],
                                  hTh[DH:P, WIN + 1:].bitcast(F32), ALU.subtract).then_inc(shift_low.sem, 1)

            def rotate(b, p, isk):
                unit = 2 * p + isk
                dve.wait_ge(proj.sem, proj.at(b, unit + 1))
                dve.wait_ge(squared.sem, squared.at(b, unit + 1))
                dve.wait_ge(rotb.sem, rotb.at(b, unit - 1))
                dve.tensor_tensor(rot_a[:, unit % 2, :], ps[:, PROJ, :], rot[:, 2 * isk, :], ALU.mult)
                dve.tensor_tensor(rot_b[:, unit % 2, :], ps[:, PROJ + 1, :], rot[:, 2 * isk + 1, :],
                                  ALU.mult).then_inc(rota.sem, 1)

            def keep_k(b, p):
                dve.wait_ge(knorm.sem, knorm.at(b, p + 1))
                dve.wait_ge(kfd.sem, kfd.at(b, p + 1 - PAIRS))
                dve.tensor_scalar(kn[:, p, :], ps[:, NORM, :], 1e-24, None, ALU.max).then_inc(ksd.sem, 1)

            def keep_q(b, p):
                dve.wait_ge(qnorm.sem, qnorm.at(b, p + 1))
                dve.wait_ge(qroot.sem, qroot.at(b, 0))
                dve.tensor_scalar(cr[:, p * NW:(p + 1) * NW], ps[:, NORM, 0:NW], 1e-24, QK_SCALE ** -2, ALU.max,
                                  ALU.mult).then_inc(cqs.sem, 1)

            def copy_values(b):
                dve.wait_ge(pv.sem, pv.at(b, 0))
                for w in range(1, NW, 2):
                    dve.wait_ge(vp.sem, vp.at(b, w + 1))
                    dve.tensor_copy(V[:, w, :], ps[:, PROJ + 1, :]).then_inc(vb.sem, 1)

            def row_max(b, p):
                dve.wait_ge(sim.sem, sim.at(b, p + 1))
                dve.wait_ge(nbd.sem, nbd.at(b, p))
                dve.tensor_reduce(mx[:, :], ps[:, SCORE:SCORE + 2, :].rearrange("p b (w k) -> p (b w) k", k=P),
                                  AX_X, ALU.max).then_inc(maxed.sem, 1)
                dve.wait_ge(maxed.sem, maxed.at(b, p + 1))
                dve.wait_ge(qroot.sem, qroot.at(b, 1))
                dve.wait_ge(expd.sem, expd.at(b, p - 1))
                dve.scalar_tensor_tensor(out=nb[:, p % 2, :], in0=mx[:, :], scalar=-1.0,
                                         in1=cq[:, p * NW:(p + 1) * NW], op0=ALU.mult,
                                         op1=ALU.mult).then_inc(nbd.sem, 1)

            def sum_inverse(b, p):
                dve.wait_ge(expd.sem, expd.at(b, p + 1))
                dve.wait_ge(pn.sem, pn.at(b, p - 1))
                dve.reciprocal(rsm[:, p % 2, :], sm[:, p % 2, :]).then_inc(rsd.sem, 1)

            def copy_turned(b, p):
                dve.wait_ge(turned.sem, turned.at(b, p + 1))
                dve.wait_ge(pv.sem, pv.at(b, p))
                dve.tensor_copy(PT[:, 4:8, :].rearrange("p w q -> p (w q)"), ps[:, TURN + 1, :]).then_inc(ptb.sem, 1)

            def split_o(b, p):
                dve.wait_ge(pv.sem, pv.at(b, p + 1))
                dve.wait_ge(wod.sem, wod.at(b, 0))
                dve.tensor_copy(oTh[:, p, :], ps[:, OUT, :]).then_inc(oTd.sem, 1)
                dve.wait_ge(oTd.sem, oTd.at(b, 2 * p + 1))
                dve.tensor_tensor(oTl[:, p, :], ps[:, OUT, :], oTh[:, p, :].bitcast(F32),
                                  ALU.subtract).then_inc(oTd.sem, 1)

            def sequence(b, nxt):
                if nxt is not None:
                    shift(nxt)
                for p in range(PAIRS):
                    if p:
                        sum_inverse(b, p - 1)
                    row_max(b, p)
                    if nxt is not None:
                        if p:
                            keep_q(nxt, p - 1)
                        rotate(nxt, p, 0)
                    if p:
                        copy_turned(b, p - 1)
                    if nxt is not None:
                        rotate(nxt, p, 1)
                    if p:
                        split_o(b, p - 1)
                    if nxt is not None:
                        keep_k(nxt, p)
                sum_inverse(b, PAIRS - 1)
                copy_turned(b, PAIRS - 1)
                if nxt is not None:
                    keep_q(nxt, PAIRS - 1)
                split_o(b, PAIRS - 1)
                if nxt is not None:
                    copy_values(nxt)
                dve.wait_ge(wod.sem, wod.at(b, 1))
                x = XR[:, bass.ds(b * T, T)]
                dve.tensor_tensor(x, x, ps[:, OUT, :], ALU.add).then_inc(x1d.sem, 1)

            shift(0)
            for p in range(PAIRS):
                rotate(0, p, 0)
                rotate(0, p, 1)
                keep_k(0, p)
                keep_q(0, p)
            copy_values(0)
            with dve.Fori(0, B - 1) as i:
                sequence(i, i + 1)
            sequence(B - 1, None)

    for step in (shifted, shift_low, proj, squared, rota, rotb, knorm, ksd, kroot, kinv, kfd, qnorm, cqs, qroot, qlog, vp,
                 va, vb, sim, maxed, nbd, expd, rsd, pn, turned, pta, ptb, pv, oTd, wod, x1d):
        step.end(B)


def feed_forward_phase(pr, tag, ctx, both, part):
    nc, ps, XR = pr.nc, pr.psum, pr.XN

    def sb(name, shape, dt=F32):
        return pr.sb(name + tag, shape, dt, ctx)

    h2 = sb("h2", [P, 2, T])
    xc = sb("fxc", [P, 2, T])
    sq = sb("fsq", [P, 2, T])
    sd = sb("fsd", [P, 2, T])
    xn = sb("fxn", [P, 2, T])
    xh = sb("fxh", [P, 2, T], F32R)
    xl = sb("fxl", [P, 2, T], F32R)
    gg = sb("gg", [P, 2, 3, T])
    hm = sb("hm", [P, 2, 3, T])
    hh = sb("fhh", [P, 2, 3, T], F32R)
    hl = sb("fhl", [P, 2, 3, T], F32R)
    b1, b2 = part("b1"), part("b2")
    (w1h, w1l), (w2h, w2l) = both("w1"), both("w2")

    padded = pr.step("f_padded", 1)
    with nc.Block() as block:
        @block.vector
        def _(dve):
            dve.memset(h2[:, :, 0:1], 0.0).then_inc(padded.sem, 1)
    padded.end(1)

    shifted = pr.step("g_shifted", 4)
    mean = pr.step("g_mean", 2)
    cent = pr.step("g_centered", 2)
    squared = pr.step("g_squared", 2)
    var = pr.step("g_var", 2)
    root = pr.step("g_root", 2)
    inv = pr.step("g_inv", 2)
    scaled = pr.step("g_scaled", 2)
    normed = pr.step("g_normed", 2)
    high = pr.step("g_high", 2)
    low = pr.step("g_low", 2)
    up = pr.step("g_up", 6)
    gelu = pr.step("g_gelu", 6)
    hid = pr.step("g_hidden", 6)
    hhigh = pr.step("g_hidden_high", 6)
    hlow = pr.step("g_hidden_low", 6)
    dn = pr.step("g_down", 2)
    fin = pr.step("g_done", 2)
    n = B // 2

    def bank(s, c):
        return 4 * s + (0 if c == 1 else 2)

    with nc.Block() as block:
        @block.tensor
        def _(pe):
            with pe.Fori(0, n) as i:
                for s in range(2):
                    pe.wait_ge(shifted.sem, shifted.at(i, 2 * s + 2))
                    pe.wait_ge(fin.sem, fin.at(i, s - 1))
                    pe.matmul(ps[:, 4 * s, :], lhsT=pr.mean[:, :], rhs=h2[:, s, :], start=True,
                              stop=True).then_inc(mean.sem, 1)
                for s in range(2):
                    pe.wait_ge(squared.sem, squared.at(i, s + 1))
                    pe.matmul(ps[:, 4 * s + 1, :], lhsT=pr.mean[:, :], rhs=sq[:, s, :], start=True,
                              stop=True).then_inc(var.sem, 1)
                for s in range(2):
                    pe.wait_ge(low.sem, low.at(i, s + 1))
                    for c in range(3):
                        if c == 2:
                            pe.wait_ge(hid.sem, hid.at(i, 3 * s + 1))
                        for half in range(2):
                            at, m = half * HID + c * P, HB[c]
                            out = ps[0:m, bank(s, c) + half, :]
                            pe.matmul(out, lhsT=w1h[:, at:at + m], rhs=xh[:, s, :], start=True, stop=False)
                            pe.matmul(out, lhsT=w1l[:, at:at + m], rhs=xh[:, s, :], start=False, stop=False)
                            last = pe.matmul(out, lhsT=w1h[:, at:at + m], rhs=xl[:, s, :], start=False, stop=True)
                        last.then_inc(up.sem, 1)
                for s in range(2):
                    out = ps[:, 4 * s, :]
                    for c in range(3):
                        m, w = HB[c], slice(c * P, (c + 1) * P)
                        if c == 0:
                            pe.wait_ge(hid.sem, hid.at(i, 3 * s + 2))
                        pe.wait_ge(hlow.sem, hlow.at(i, 3 * s + c + 1))
                        pe.matmul(out, lhsT=w2h[0:m, w], rhs=hh[0:m, s, c, :], start=(c == 0), stop=False)
                        pe.matmul(out, lhsT=w2l[0:m, w], rhs=hh[0:m, s, c, :], start=False, stop=False)
                        last = pe.matmul(out, lhsT=w2h[0:m, w], rhs=hl[0:m, s, c, :], start=False, stop=(c == 2))
                    last.then_inc(dn.sem, 1)

        @block.scalar
        def _(act):
            with act.Fori(0, n) as i:
                for s in range(2):
                    act.wait_ge(cent.sem, cent.at(i, s + 1))
                    act.wait_ge(var.sem, var.at(i, s - 1))
                    act.activation(sq[:, s, :], xc[:, s, :], ACT.Square).then_inc(squared.sem, 1)
                act.preload_act_table_set(LOG_EXP)
                for s in range(2):
                    act.wait_ge(var.sem, var.at(i, s + 1))
                    act.wait_ge(scaled.sem, scaled.at(i, s - 1))
                    act.activation(sd[:, s, :], ps[:, 4 * s + 1, :], ACT.Ln, bias=pr.eps[:, 0:1]).then_inc(root.sem, 1)
                    act.wait_ge(root.sem, root.at(i, s + 1))
                    act.activation(sd[:, s, :], sd[:, s, :], ACT.Exp, scale=-0.5).then_inc(inv.sem, 1)
                for s in range(2):
                    act.wait_ge(normed.sem, normed.at(i, s + 1))
                    act.wait_ge(up.sem, up.at(i, 3 * s - 3))
                    act.activation(xh[:, s, :], xn[:, s, :], ACT.Copy).then_inc(high.sem, 1)
                for s in range(2):
                    for c in range(3):
                        m = HB[c]
                        act.wait_ge(up.sem, up.at(i, 3 * s + c + 1))
                        act.wait_ge(hid.sem, hid.at(i, 3 * s + c - 5))
                        act.activation(gg[0:m, s, c, :], ps[0:m, bank(s, c) + 1, :], ACT.Gelu,
                                       bias=b1[0:m, 3 + c:4 + c]).then_inc(gelu.sem, 1)

        @block.gpsimd
        def _(pool):
            with pool.Fori(0, n) as i:
                for s in range(2):
                    pool.wait_ge(high.sem, high.at(i, s + 1))
                    pool.tensor_tensor(xl[:, s, :], xn[:, s, :], xh[:, s, :].bitcast(F32),
                                       ALU.subtract).then_inc(low.sem, 1)
                for s in range(2):
                    for c in range(3):
                        m = HB[c]
                        pool.wait_ge(hhigh.sem, hhigh.at(i, 3 * s + c + 1))
                        pool.wait_ge(dn.sem, dn.at(i, s - 1))
                        pool.tensor_tensor(hl[0:m, s, c, :], hm[0:m, s, c, :], hh[0:m, s, c, :].bitcast(F32),
                                           ALU.subtract).then_inc(hlow.sem, 1)

        @block.vector
        def _(dve):
            with dve.Fori(0, n) as i:
                for s in range(2):
                    at = (2 * i + s) * T
                    dve.wait_ge(cent.sem, cent.at(i, s - 1))
                    dve.tensor_copy(h2[0:DH, s, :], XR[0:DH, bass.ds(at, T)]).then_inc(shifted.sem, 1)
                    dve.tensor_copy(h2[DH:P, s, 1:], XR[DH:P, bass.ds(at, T - 1)]).then_inc(shifted.sem, 1)
                for s in range(2):
                    dve.wait_ge(shifted.sem, shifted.at(i, 2 * s + 2))
                    dve.wait_ge(mean.sem, mean.at(i, s + 1))
                    dve.wait_ge(scaled.sem, scaled.at(i, s - 1))
                    dve.tensor_tensor(xc[:, s, :], h2[:, s, :], ps[:, 4 * s, :], ALU.subtract).then_inc(cent.sem, 1)
                for s in range(2):
                    dve.wait_ge(inv.sem, inv.at(i, s + 1))
                    dve.wait_ge(squared.sem, squared.at(i, s + 1))
                    dve.wait_ge(low.sem, low.at(i, s - 1))
                    dve.tensor_tensor(xn[:, s, :], xc[:, s, :], sd[:, s, :], ALU.mult).then_inc(scaled.sem, 1)
                    dve.wait_ge(scaled.sem, scaled.at(i, s + 1))
                    dve.tensor_scalar(xn[:, s, :], xn[:, s, :], part("ln_g"), part("ln_b"), ALU.mult,
                                      ALU.add).then_inc(normed.sem, 1)
                for s in range(2):
                    for c in range(3):
                        m = HB[c]
                        dve.wait_ge(gelu.sem, gelu.at(i, 3 * s + c + 1))
                        dve.wait_ge(hlow.sem, hlow.at(i, 3 * s + c - 5))
                        dve.scalar_tensor_tensor(out=hm[0:m, s, c, :], in0=ps[0:m, bank(s, c), :], scalar=b1[0:m, c:c + 1],
                                                 in1=gg[0:m, s, c, :], op0=ALU.add, op1=ALU.mult).then_inc(hid.sem, 1)
                        dve.wait_ge(hid.sem, hid.at(i, 3 * s + c + 1))
                        dve.wait_ge(dn.sem, dn.at(i, s - 1))
                        dve.tensor_copy(hh[0:m, s, c, :], hm[0:m, s, c, :]).then_inc(hhigh.sem, 1)
                for s in range(2):
                    dve.wait_ge(dn.sem, dn.at(i, s + 1))
                    x = XR[:, bass.ds((2 * i + s) * T, T)]
                    dve.scalar_tensor_tensor(out=x, in0=ps[:, 4 * s, :], scalar=b2, in1=x, op0=ALU.add,
                                             op1=ALU.add).then_inc(fin.sem, 1)

    for step in (shifted, mean, cent, squared, var, root, inv, scaled, normed, high, low, up, gelu, hid, hhigh, hlow, dn,
                 fin):
        step.end(n)


def macaron_kernel(nc, x, gate_w, gate_b, experts, mamba, cell, ffn, consts, out):
    o = CONST_PACK
    with ExitStack() as ctx:
        pr = Program(nc, ctx)
        pr.psum = ctx.enter_context(nc.psum_tensor("banks", [P, 8, T], F32))
        pr.X = pr.sb("X", [P, N])
        pr.XN = pr.sb("XN", [P, N])
        pr.ident = pr.sb("ident", [P, P])
        pr.ident_b = pr.sb("ident_b", [P, P], BF16)
        pr.mean = pr.sb("mean", [P, P])
        pr.heads = pr.sb("heads", [P, P])
        pr.tri = pr.sb("tri", [P, NG * NG])
        pr.mask = pr.sb("mask", [P, T], BF16)
        pr.sel = pr.sb("sel", [96, 2 * DS, P], BF16)
        pr.eps = pr.sb("eps", [P, 1])
        pr.ones = pr.sb("ones", [P, 1])
        const_in = ctx.enter_context(nc.semaphore("const_in"))
        const_ready = ctx.enter_context(nc.semaphore("const_ready"))
        stored = ctx.enter_context(nc.semaphore("stored"))
        for name, inc in STEP_NAMES:
            pr.step(name, 1, inc)
        with ExitStack() as tctx:
            stage = pr.sb("stage", [P, T], ctx=tctx)
            sel_f = pr.sb("sel_f", [96, 2 * DS * P], ctx=tctx)
            with nc.Block() as block:
                @block.sync
                def _(sp):
                    sp.dma_start(pr.X[:, :], x).then_inc(const_in, 16)
                    for t, name in ((pr.ident, "ident"), (pr.mean, "mean"), (pr.heads, "heads"), (pr.tri, "tri")):
                        sp.dma_start(t[:, :], consts[:, o[name][0]:o[name][1]]).then_inc(const_in, 16)
                    sp.dma_start(stage[:, :], consts[:, o["mask"][0]:o["mask"][1]]).then_inc(const_in, 16)
                    sp.dma_start(sel_f[:, :], consts[0:96, o["sel"][0]:o["sel"][1]]).then_inc(const_in, 16)
                    sp.wait_ge(const_in, 16 * 7)

                @block.gpsimd
                def _(pool):
                    for step in pr.steps.values():
                        pool.sem_inc(step.sem, CREDIT)

                @block.vector
                def _(dve):
                    dve.memset(pr.eps[:, :], LN_EPS)
                    dve.memset(pr.ones[:, :], 1.0)
                    dve.wait_ge(const_in, 16 * 7)
                    dve.tensor_copy(pr.ident_b[:, :], pr.ident[:, :])
                    dve.tensor_copy(pr.mask[:, :], stage[:, :])
                    dve.tensor_copy(pr.sel[:, :, :].rearrange("p n q -> p (n q)"), sel_f[:, :]).then_inc(const_ready, 1)
                    dve.wait_ge(const_ready, 1)

        tables = consts[:, o["cos_q"][0]:o["sin_k"][1]]
        X, XN = pr.X, pr.XN

        def moe(tag):
            layer_norm_phase(pr, tag, X, XN)
            moe_phase(pr, tag, gate_w, gate_b, experts)

        def attention(tag):
            layer_norm_phase(pr, tag, X, XN)
            for layer in range(2):
                attention_layer(pr, f"{tag}{layer}", ffn[layer], tables)
            add_stream(pr, 0.5)

        moe("m0")
        if STAGES > 1:
            layer_norm_phase(pr, "n1", X, XN)
            for layer in range(2):
                mamba_layer(pr, f"a{layer}", mamba[layer])
            add_stream(pr, 1.0)
        if STAGES > 2:
            moe("m2")
        if STAGES > 3:
            attention("f3")
        if STAGES > 4:
            layer_norm_phase(pr, "n4", X, XN)
            cell_phase(pr, "c4", cell)
        if STAGES > 5:
            attention("f5")
        with nc.Block() as block:
            @block.sync
            def _(sp):
                sp.dma_start(out, X[:, :]).then_inc(stored, 16)
                sp.wait_ge(stored, 16)


STEP_NAMES = [
    ("ln_mean", 1), ("ln_centered", 1), ("ln_squared", 1), ("ln_var", 1), ("ln_log", 1), ("ln_inv", 1),
    ("ln_normed", 1), ("gate_in", 16), ("logits", 1), ("scored", 1), ("route", 1), ("turned", 1),
    ("weights_turned", 1), ("token_parts", 1), ("w_high", 1), ("w_low", 1), ("gate_up", 1), ("silu", 1),
    ("product", 1), ("hidden", 1), ("hidden_high", 1), ("hidden_low", 1), ("down", 1), ("added", 1),
    ("m_packed", 16), ("m_ready", 1), ("m_xz", 1), ("m_xp_copied", 1), ("m_silu_z", 1), ("m_conv", 1), ("m_u",
    1), ("m_x_dbl", 1), ("m_split", 1), ("m_dt_proj", 1), ("m_abs", 1), ("m_softplus_exp", 1),
    ("m_softplus_log", 1), ("m_dt_relu", 1), ("m_dt", 1), ("m_dtu", 1), ("m_bc_spread", 1), ("m_decay", 1),
    ("m_b_copied", 1), ("m_driven", 1), ("m_scanned", 1), ("m_state_read", 1), ("m_y_summed", 1), ("m_gated",
    1), ("m_out", 1), ("m_out_copied", 1), ("m_mean", 1), ("m_centered", 1), ("m_squared", 1), ("m_var", 1),
    ("m_root", 1), ("m_inv", 1), ("m_scaled", 1), ("m_done", 1), ("stream_added", 1), ("c_packed", 16),
    ("c_proj", 1), ("c_xp", 1), ("c_gates", 1), ("c_acts", 1), ("c_bv", 1), ("c_scanned", 1), ("c_silu_h", 1),
    ("c_out", 1), ("c_out_proj", 1), ("c_done", 1), ("f_packed", 16), ("f_w_high", 1), ("f_ready", 1),
    ("f_padded", 1), ("f_shifted", 1), ("f_shifted_low", 1), ("f_proj", 1), ("f_squared", 1),
    ("f_rotated_parts", 1), ("f_rotated", 1), ("f_k_norm", 1), ("f_k_norm_kept", 1), ("f_k_root", 1),
    ("f_k_inv", 1), ("f_k", 1), ("f_q_norm", 1), ("f_q_norm_kept", 1), ("f_q_root", 1), ("f_q_log", 1),
    ("f_v_proj", 1), ("f_v_even", 1), ("f_v_odd", 1), ("f_sim", 1), ("f_max", 1), ("f_bias", 1), ("f_exp", 1),
    ("f_sum_inv", 1), ("f_probs", 1), ("f_turned", 1), ("f_turned_copied_a", 1), ("f_turned_copied_b", 1),
    ("f_pv", 1), ("f_o", 1), ("f_wo", 1), ("f_x1", 1), ("g_shifted", 1), ("g_mean", 1), ("g_centered", 1),
    ("g_squared", 1), ("g_var", 1), ("g_root", 1), ("g_inv", 1), ("g_scaled", 1), ("g_normed", 1), ("g_high",
    1), ("g_low", 1), ("g_up", 1), ("g_gelu", 1), ("g_hidden", 1), ("g_hidden_high", 1), ("g_hidden_low", 1),
    ("g_down", 1), ("g_done", 1), ("chunk_in_a", 16), ("chunk_in_b", 16), ("chunk_in_c", 16), ("chunk_in_d",
    16),
]
STAGES = 6


def rotary_tables(np):
    f = np.float32
    half = np.arange(0, DH, 2, dtype=f)
    inv_freq = (f(1.0) / np.power(f(10000.0), half / f(DH))).astype(f)
    t = np.arange(T, dtype=f)
    freqs = (t[:, None] * inv_freq[None, :]).astype(f)
    freqs = np.concatenate([freqs, freqs], axis=-1).astype(np.float64)
    base = (half + 0.4 * DH) / (1.4 * DH)
    power = (t - T // 2) / float(WIN // 2)
    scale = base[None, :].astype(np.float64) ** power[:, None]
    scale = np.concatenate([scale, scale], axis=-1)
    sign = np.concatenate([-np.ones(DH // 2), np.ones(DH // 2)])
    cos, sin = np.cos(freqs), np.sin(freqs) * sign
    return [np.tile(a.T, (2, 1)).astype(f) for a in (cos * scale, sin * scale, cos / scale, sin / scale)]


def constants(np):
    f = np.float32
    r = np.arange(P)
    parts = {"ident": np.eye(P, dtype=f), "mean": np.full((P, P), 1.0 / P, f),
             "heads": (r[:, None] // DH == r[None, :] // DH).astype(f)}
    g = np.arange(NG)
    parts["tri"] = np.tile((g[None, :] < g[:, None]).astype(f).reshape(1, -1), (P, 1))
    q, k = (r % WIN)[:, None], r[None, :]
    inside = (q <= k) & (k <= q + WIN)
    mask = np.where(inside, 0.0, MASKED).astype(f)
    first = np.where(inside & (k >= WIN), 0.0, MASKED).astype(f)
    opening = np.where((r < WIN)[:, None], first, mask)
    parts["mask"] = np.concatenate([opening] + [mask] * (T // P - 1), axis=1)
    for name, table in zip(("cos_q", "sin_q", "cos_k", "sin_k"), rotary_tables(np)):
        parts[name] = table
    sel = np.zeros((P, 2 * DS, P), f)
    for p in range(96):
        sel[p, p % 32, :] = 1.0
    parts["sel"] = sel.reshape(P, -1)
    return pack(np, CONST_PACK, parts)


def pack(np, layout, parts):
    out = np.zeros((P, layout["total"]), np.float32)
    for name, a in parts.items():
        lo, hi = layout[name]
        a = np.asarray(a).reshape(a.shape[0], -1)
        assert a.shape[1] == hi - lo, name
        at = 32 if name == "dt_w" else 0
        out[at:at + a.shape[0], lo:hi] = a
    return out


def tiles(np, v, n):
    out = np.zeros((n * P,) + v.shape[1:], np.float32)
    out[:v.shape[0]] = v
    return np.moveaxis(out.reshape((n, P) + v.shape[1:]), 0, 1)


def kernel(**inputs):
    import numpy as np
    import concourse.bacc as _bacc
    from concourse.bass_utils import run_bass_kernel_spmd as _run

    a = {k: np.asarray(v) for k, v in inputs.items()}
    arrays = {"x": a["L0_attn_x"].reshape(N, P).T,
              "gate_w": a["L0_ffn_gate_w"].T,
              "gate_b": np.tile(a["L0_ffn_gate_bias"][None, :], (P, 1)),
              "consts": constants(np)}

    def chunk_pack(gate, up, down, experts_of):
        n = -(-gate.shape[0] // P)
        out = np.zeros((n, P, 4, P), np.float32)
        for c in range(n):
            r = slice(c * P, min((c + 1) * P, gate.shape[0]))
            w = r.stop - r.start
            out[c, :, 0, :w], out[c, :, 1, :w], out[c, :w, 2, :] = gate[r].T, up[r].T, down[r]
            if experts_of is not None:
                for d, e in enumerate(experts_of[r]):
                    out[c, [e, E + e], 3, d] = 1.0
        return out.reshape(n, P, 4 * P)

    flat = lambda w: w.reshape(E * I_MOE, P)
    arrays["experts"] = np.concatenate([
        chunk_pack(a["L0_ffn_Sg"], a["L0_ffn_Su"], a["L0_ffn_Sd"].T, None),
        chunk_pack(flat(a["L0_ffn_Wg"]), flat(a["L0_ffn_Wu"]), flat(a["L0_ffn_Wd"].transpose(0, 2, 1)),
                   np.repeat(np.arange(E), I_MOE))])

    for l in range(2):
        m = {k[len("L0_attn_"):]: v[l] for k, v in a.items() if k.startswith("L0_attn_") and k != "L0_attn_x"}
        xp_w = m["x_proj_w"]
        xp_w = np.concatenate([xp_w[DR:], xp_w[:DR]], axis=0)
        arrays[f"mamba{l}"] = pack(np, MAMBA_PACK, {
            "in_w": m["in_proj_w"].T, "xp_w": tiles(np, xp_w.T, HALF), "dt_w": m["dt_proj_w"].T,
            "out_w": tiles(np, m["out_proj_w"].T, HALF), "conv_w": tiles(np, m["conv_w"], HALF),
            "conv_b": tiles(np, m["conv_b"], HALF), "dt_b": tiles(np, m["dt_proj_b"], HALF),
            "A_log": tiles(np, m["A_log"], HALF), "D": tiles(np, m["Dskip"], HALF),
            "ln_w": m["ln_w"][:, None], "ln_b": m["ln_b"][:, None]})
        w = {k[len("L1_ffn_"):]: v[l] for k, v in a.items() if k.startswith("L1_ffn_")}
        d = np.arange(DH)
        turn = (d + DH // 2) % DH
        order = np.concatenate([h * DH + turn for h in range(HEADS)])
        wq, wk, wv = w["wqkv"][:, 0:512], w["wqkv"][:, 512:1024], w["wqkv"][:, 1024:1536]
        twice = lambda v: np.concatenate([v, v])[:, None]
        b1 = np.concatenate([tiles(np, w["b1"][:HID], 3), tiles(np, w["b1"][HID:], 3)], axis=1)
        arrays[f"ffn{l}"] = pack(np, FFN_PACK, {
            "wq": wq, "wqr": wq[:, order], "wk": wk, "wkr": wk[:, order], "wv": wv, "wo": tiles(np, w["wo"], PAIRS),
            "w1": w["w1"], "w2": tiles(np, w["w2"], 3), "b1": b1, "ln_g": w["ln_g"][:, None],
            "ln_b": w["ln_b"][:, None], "b2": w["b2"][:, None], "qs": twice(w["q_scale"]),
            "qsr": twice(w["q_scale"][turn]), "ks": twice(w["k_scale"]), "ksr": twice(w["k_scale"][turn])})
    c = {k[len("L1_attn_"):]: v for k, v in a.items() if k.startswith("L1_attn_")}
    arrays["cell"] = pack(np, CELL_PACK, {
        "w_in": c["W_in"].T, "w_a": c["W_alpha"].T, "w_b": c["W_beta"].T, "w_v": c["W_v"].T, "w_out": c["W_out"].T,
        "b_a": c["b_alpha"][:, None], "b_b": c["b_beta"][:, None], "b_v": c["b_v"][:, None]})

    nc = _bacc.Bacc("TRN2", target_bir_lowering=False, num_devices=1)
    arrays = {k: np.ascontiguousarray(v) for k, v in arrays.items()}
    t = {k: nc.dram_tensor(f"in_{k}", v.shape, F32, kind="ExternalInput").ap() for k, v in arrays.items()}
    out = nc.dram_tensor("out_x", (P, N), F32, kind="ExternalOutput").ap()
    macaron_kernel(nc, t["x"], t["gate_w"], t["gate_b"], t["experts"], [t["mamba0"], t["mamba1"]], t["cell"],
                   [t["ffn0"], t["ffn1"]], t["consts"], out)
    r = _run(nc, [{f"in_{k}": v for k, v in arrays.items()}], core_ids=[0])
    return np.ascontiguousarray(r.results[0]["out_x"].T.reshape(B, T, P))
```

```python
from contextlib import ExitStack

import concourse.bass as bass
from concourse import mybir

P = 128
B, T = 8, 512
N = B * T
TB = T // P
NT = N // P

E, I_MOE, TOP_K, NG, KEEP_G = 64, 88, 8, 8, 4
EG = E // NG
CHUNKS = -(-2 * I_MOE // P) + E * I_MOE // P
SLOTS = 4
SLOT_USES = [sum(q % SLOTS == s for q in range(CHUNKS)) for s in range(SLOTS)]
ROUTED_SCALE = 2.5

DI, DS, DR = 256, 16, 8
HALF = DI // P
PAD = 3
GROUP = 4

HEADS, DH, WIN = 8, 64, 64
PAIRS = HEADS // 2
NW = T // WIN
HID = 341
HB = [128, 128, 85]
QK_SCALE = 8.0
LN_EPS = 1e-5
AHEAD, VARS = 5, 3
MASKED = -1e30

F32 = mybir.dt.float32
F32R = mybir.dt.float32r
BF16 = mybir.dt.bfloat16
ALU = mybir.AluOpType
ACT = mybir.ActivationFunctionType
AX_X = mybir.AxisListType.X
CREDIT = 16


def offsets(parts):
    out, at = {}, 0
    for name, width in parts:
        out[name] = (at, at + width)
        at += width
    out["total"] = at
    return out


MAMBA_PACK = offsets([("in_w", 2 * DI), ("xp_w", HALF * 40), ("dt_w", DI), ("out_w", HALF * P), ("conv_w", HALF * 4),
                      ("conv_b", HALF), ("dt_b", HALF), ("A_log", HALF * DS), ("D", HALF), ("ln_w", 1), ("ln_b", 1)])
CELL_PACK = offsets([("w_in", P), ("w_a", P), ("w_b", P), ("w_v", P), ("w_out", P), ("b_a", 1), ("b_b", 1), ("b_v", 1)])
FFN_PACK = offsets([("wq", 512), ("wqr", 512), ("wk", 512), ("wkr", 512), ("wv", 512), ("wo", 512), ("w1", 2 * HID),
                    ("w2", 3 * P), ("b1", 6), ("ln_g", 1), ("ln_b", 1), ("b2", 1),
                    ("qs", 1), ("qsr", 1), ("ks", 1), ("ksr", 1)])
CONST_PACK = offsets([("ident", P), ("mean", P), ("heads", P), ("tri", NG * NG), ("mask", T),
                      ("cos_q", T), ("sin_q", T), ("cos_k", T), ("sin_k", T), ("sel", 2 * DS * P)])


class Step:

    def __init__(self, sem, inc=1):
        self.sem, self.inc, self.base, self.per = sem, inc, CREDIT, 0

    def start(self, per):
        self.per = per * self.inc

    def at(self, i, k):
        return i * self.per + (self.base + k * self.inc)

    def end(self, iterations):
        self.base += iterations * self.per


class Program:
    def __init__(self, nc, ctx):
        self.nc, self.ctx, self.steps = nc, ctx, {}

    def step(self, name, per, inc=1):
        if name not in self.steps:
            self.steps[name] = Step(self.ctx.enter_context(self.nc.semaphore(name)), inc)
        self.steps[name].start(per)
        return self.steps[name]

    def sb(self, name, shape, dt=F32, ctx=None):
        return (ctx or self.ctx).enter_context(self.nc.sbuf_tensor(name, shape, dt))


LOG_EXP = "natural_log_exp_and_others"


def cols(t, i):
    return t[:, bass.ds(i * T, T)]


def layer_norm_phase(pr, tag, src, dst):
    nc, ps = pr.nc, pr.psum
    U = 4
    with ExitStack() as ctx:
        sq = pr.sb(f"sq{tag}", [P, U, T], ctx=ctx)
        rs = pr.sb(f"rs{tag}", [P, U, T], ctx=ctx)
        centered = pr.step("ln_centered", B)
        squared = pr.step("ln_squared", B)
        var = pr.step("ln_var", B)
        logged = pr.step("ln_log", B)
        inv = pr.step("ln_inv", B)
        normed = pr.step("ln_normed", B)
        block = ctx.enter_context(nc.Block())

        @block.tensor
        def _(pe):
            def center(s):
                if s >= AHEAD:
                    pe.wait_ge(normed.sem, normed.at(0, s + 1 - AHEAD))
                pe.matmul(ps[:, s % AHEAD, :], lhsT=pr.center[:, :], rhs=src[:, s * T:(s + 1) * T], start=True,
                          stop=True).then_inc(centered.sem, 1)

            for s in range(AHEAD):
                center(s)
            for s in range(B):
                pe.wait_ge(squared.sem, squared.at(0, s + 1))
                if s >= VARS:
                    pe.wait_ge(logged.sem, logged.at(0, s + 1 - VARS))
                pe.matmul(ps[:, AHEAD + s % VARS, :], lhsT=pr.mean[:, :], rhs=sq[:, s % U, :], start=True,
                          stop=True).then_inc(var.sem, 1)
                if 1 <= s <= B - AHEAD:
                    center(s - 1 + AHEAD)

        @block.scalar
        def _(act):
            def square(s):
                act.wait_ge(centered.sem, centered.at(0, s + 1))
                if s >= U:
                    act.wait_ge(var.sem, var.at(0, s + 1 - U))
                act.activation(sq[:, s % U, :], ps[:, s % AHEAD, :], ACT.Square).then_inc(squared.sem, 1)

            def log(s):
                act.wait_ge(var.sem, var.at(0, s + 1))
                if s >= U:
                    act.wait_ge(normed.sem, normed.at(0, s + 1 - U))
                act.activation(rs[:, s % U, :], ps[:, AHEAD + s % VARS, :], ACT.Ln, bias=pr.eps[:, 0:1]).then_inc(logged.sem, 1)

            def exp(s):
                act.wait_ge(logged.sem, logged.at(0, s + 1))
                act.activation(rs[:, s % U, :], rs[:, s % U, :], ACT.Exp, scale=-0.5).then_inc(inv.sem, 1)

            act.preload_act_table_set(LOG_EXP)
            square(0)
            square(1)
            for s in range(B):
                if s + 2 < B:
                    square(s + 2)
                log(s)
                exp(s)

        @block.vector
        def _(dve):
            for s in range(B):
                dve.wait_ge(inv.sem, inv.at(0, s + 1))
                dve.wait_ge(centered.sem, centered.at(0, s + 1))
                dve.tensor_tensor(dst[:, s * T:(s + 1) * T], ps[:, s % AHEAD, :], rs[:, s % U, :],
                                  ALU.mult).then_inc(normed.sem, 1)

        for s in (centered, squared, var, logged, inv, normed):
            s.end(1)


def moe_phase(pr, tag, gate_w, gate_b, experts):
    nc, ps, X, XN = pr.nc, pr.psum, pr.X, pr.XN
    with ExitStack() as ctx:
        gw = pr.sb(f"gw{tag}", [P, E], ctx=ctx)
        gb = pr.sb(f"gb{tag}", [P, E], ctx=ctx)
        RW = pr.sb(f"RW{tag}", [P, NT, 2 * E], F32R, ctx=ctx)
        xh = pr.sb(f"xh{tag}", [P, N], F32R, ctx=ctx)
        xl = pr.sb(f"xl{tag}", [P, N], F32R, ctx=ctx)
        with ExitStack() as rctx:
            score = pr.sb(f"score{tag}", [P, NT, E], ctx=rctx)
            choice = pr.sb(f"choice{tag}", [P, NT, E], ctx=rctx)
            ta = pr.sb(f"ta{tag}", [P, NT * E], ctx=rctx)
            tb = pr.sb(f"tb{tag}", [P, NT * E], ctx=rctx)
            top = pr.sb(f"top{tag}", [P, NT, 8], ctx=rctx)
            gs = pr.sb(f"gs{tag}", [P, NT, NG], ctx=rctx)
            rank = pr.sb(f"rank{tag}", [P, NT, NG], ctx=rctx)
            tot = pr.sb(f"tot{tag}", [P, NT], ctx=rctx)
            G = NT // 4
            gate_in = pr.step("gate_in", 2, 16)
            logits = pr.step("logits", 4)
            scored = pr.step("scored", 4)
            route = pr.step("route", 400)
            parts = pr.step("token_parts", B)
            with nc.Block() as block:
                @block.sync
                def _(sp):
                    sp.dma_start(gw[:, :], gate_w).then_inc(gate_in.sem, 16)
                    sp.dma_start(gb[:, :], gate_b).then_inc(gate_in.sem, 16)

                @block.tensor
                def _(pe):
                    pe.wait_ge(gate_in.sem, gate_in.at(0, 2))
                    for g in range(4):
                        for t in range(G):
                            m = (g * G + t) * P
                            last = pe.matmul(ps[:, g, t * E:(t + 1) * E], lhsT=XN[:, m:m + P], rhs=gw[:, :],
                                             start=True, stop=True)
                        last.then_inc(logits.sem, 1)

                @block.scalar
                def _(act):
                    for g in range(4):
                        act.wait_ge(logits.sem, logits.at(0, g + 1))
                        act.activation(score[:, g * G:(g + 1) * G, :].rearrange("p t e -> p (t e)"), ps[:, g, :],
                                       ACT.Sigmoid).then_inc(scored.sem, 1)
                    for b in range(B):
                        c = slice(b * T, (b + 1) * T)
                        act.activation(xh[:, c], XN[:, c], ACT.Copy).then_inc(parts.sem, 1)

                @block.gpsimd
                def _(pool):
                    for b in range(B):
                        c = slice(b * T, (b + 1) * T)
                        pool.wait_ge(parts.sem, parts.at(0, b + 1))
                        pool.tensor_tensor(xl[:, c], XN[:, c], xh[:, c].bitcast(F32), ALU.subtract)

                @block.vector
                def _(dve):
                    count = [0]

                    def then(ins):
                        count[0] += 1
                        ins.then_inc(route.sem, 1)
                        dve.wait_ge(route.sem, route.at(0, count[0]))

                    def tt(out, a, b, op):
                        then(dve.tensor_tensor(out, a, b, op))

                    dve.wait_ge(scored.sem, scored.at(0, 4))
                    dve.wait_ge(gate_in.sem, gate_in.at(0, 2))
                    tt(choice[:, :, :], score[:, :, :], gb[:, :].unsqueeze(1).to_broadcast([P, NT, E]), ALU.add)
                    c = choice[:, :, :].rearrange("p t (g j) -> p (t g) j", j=EG)
                    M = NT * NG
                    h1 = ta[:, 0:4 * M].rearrange("p (q j) -> p q j", j=4)
                    l1 = ta[:, 4 * M:8 * M].rearrange("p (q j) -> p q j", j=4)
                    tt(h1, c[:, :, 0:4], c[:, :, 4:8], ALU.max)
                    tt(l1, c[:, :, 0:4], c[:, :, 4:8], ALU.min)
                    v = [tb[:, 2 * M * k:2 * M * (k + 1)].rearrange("p (q j) -> p q j", j=2) for k in range(4)]
                    tt(v[0], h1[:, :, 0:2], h1[:, :, 2:4], ALU.max)
                    tt(v[1], h1[:, :, 0:2], h1[:, :, 2:4], ALU.min)
                    tt(v[2], l1[:, :, 0:2], l1[:, :, 2:4], ALU.max)
                    tt(v[3], v[1], v[2], ALU.max)
                    w = [ta[:, M * k:M * (k + 1)] for k in range(4)]
                    a, b = v[0], v[3]
                    tt(w[0], a[:, :, 0], a[:, :, 1], ALU.max)
                    tt(w[1], a[:, :, 0], a[:, :, 1], ALU.min)
                    tt(w[2], b[:, :, 0], b[:, :, 1], ALU.max)
                    tt(w[3], w[1], w[2], ALU.max)
                    gsf = gs[:, :, :].rearrange("p t g -> p (t g)")
                    tt(gsf, w[0], w[3], ALU.add)
                    shape = [P, NT, NG, NG]
                    other = gs[:, :, :].unsqueeze(2).to_broadcast(shape)
                    own = gs[:, :, :].unsqueeze(3).to_broadcast(shape)
                    above = ta[:, :].rearrange("p (t g j) -> p t g j", g=NG, j=NG)
                    equal = tb[:, :].rearrange("p (t g j) -> p t g j", g=NG, j=NG)
                    tt(above, other, own, ALU.is_gt)
                    tt(equal, other, own, ALU.is_equal)
                    tt(tb[:, :].rearrange("p (t x) -> p t x", t=NT), tb[:, :].rearrange("p (t x) -> p t x", t=NT),
                       pr.tri[:, :].unsqueeze(1).to_broadcast([P, NT, NG * NG]), ALU.mult)
                    tt(ta[:, :], ta[:, :], tb[:, :], ALU.add)
                    then(dve.tensor_reduce(rank[:, :, :].rearrange("p t g -> p (t g)"),
                                           ta[:, :].rearrange("p (q j) -> p q j", j=NG), AX_X, ALU.add))
                    then(dve.tensor_scalar(gs[:, :, :], rank[:, :, :], float(KEEP_G), None, ALU.is_lt))
                    masked = ta[:, :].rearrange("p (q j) -> p q j", j=EG)
                    tt(masked, c, gsf.unsqueeze(2).to_broadcast([P, NT * NG, EG]), ALU.mult)
                    for t in range(NT):
                        mt = ta[:, t * E:(t + 1) * E]
                        last = dve.max(top[:, t, :], mt)
                        last.then_inc(route.sem, 1)
                        count[0] += 1
                    dve.wait_ge(route.sem, route.at(0, count[0]))
                    for t in range(NT):
                        mt = ta[:, t * E:(t + 1) * E]
                        last = dve.match_replace(tb[:, t * E:(t + 1) * E], top[:, t, :], mt, MASKED)
                        last.then_inc(route.sem, 1)
                        count[0] += 1
                    dve.wait_ge(route.sem, route.at(0, count[0]))
                    tt(ta[:, :], ta[:, :], tb[:, :], ALU.not_equal)
                    tat = ta[:, :].rearrange("p (t e) -> p t e", e=E)
                    tt(tat, tat, score[:, :, :], ALU.mult)
                    then(dve.tensor_reduce(tot[:, :], tat, AX_X, ALU.add))
                    then(dve.tensor_scalar(tot[:, :], tot[:, :], 1e-20, None, ALU.add))
                    then(dve.reciprocal(tot[:, :], tot[:, :]))
                    then(dve.tensor_scalar(tot[:, :], tot[:, :], 0.5 * ROUTED_SCALE, None, ALU.mult))
                    tt(tat, tat, tot[:, :].unsqueeze(2).to_broadcast([P, NT, E]), ALU.mult)
                    then(dve.tensor_copy(RW[:, :, 0:E], tat))
                    tt(RW[:, :, E:2 * E], tat, RW[:, :, 0:E].bitcast(F32), ALU.subtract)
                    route.start(count[0])

            for s in (gate_in, logits, scored, route, parts):
                s.end(1)

        rT = pr.sb(f"rT{tag}", [P, N], F32R, ctx=ctx)
        turned = pr.step("turned", B)
        rcopied = pr.step("weights_turned", B)
        with nc.Block() as block:
            @block.tensor
            def _(pe):
                for b in range(B):
                    pe.wait_ge(rcopied.sem, rcopied.at(0, b - 1))
                    for t in range(TB):
                        last = pe.transpose(ps[:, b % 2, t * P:(t + 1) * P], RW[:, b * TB + t, :].bitcast(F32),
                                            pr.ident[:, :])
                    last.then_inc(turned.sem, 1)

            @block.vector
            def _(dve):
                for b in range(B):
                    dve.wait_ge(turned.sem, turned.at(0, b + 1))
                    dve.tensor_copy(rT[:, b * T:(b + 1) * T], ps[:, b % 2, :]).then_inc(rcopied.sem, 1)

        turned.end(1)
        rcopied.end(1)

        stage = pr.sb(f"stage{tag}", [P, SLOTS, 4 * P], ctx=ctx)
        wh = pr.sb(f"wh{tag}", [P, SLOTS, 4 * P], F32R, ctx=ctx)
        wl = pr.sb(f"wl{tag}", [P, SLOTS, 3 * P], F32R, ctx=ctx)
        sg = pr.sb(f"sg{tag}", [P, 2, T], ctx=ctx)
        gu = pr.sb(f"gu{tag}", [P, 2, T], ctx=ctx)
        h = pr.sb(f"h{tag}", [P, 2, T], ctx=ctx)
        hh = pr.sb(f"hh{tag}", [P, 4, T], F32R, ctx=ctx)
        hl = pr.sb(f"hl{tag}", [P, 4, T], F32R, ctx=ctx)
        PER = 2 * CHUNKS
        loaded = [pr.step(f"chunk_in_{c}", n, 16) for c, n in zip("abcd", SLOT_USES)]
        w_high = pr.step("w_high", CHUNKS)
        w_low = pr.step("w_low", CHUNKS)
        gate_up = pr.step("gate_up", PER)
        silu = pr.step("silu", PER)
        product = pr.step("product", PER)
        hidden = pr.step("hidden", PER)
        high = pr.step("hidden_high", PER)
        low = pr.step("hidden_low", PER)
        down = pr.step("down", PER)
        added = pr.step("added", 2)
        LOOPS = (CHUNKS - 2) // SLOTS
        G = 2 * SLOTS

        def slot(q):
            return q % SLOTS

        def uses(q, i):
            return i + q // SLOTS + 1

        with nc.Block() as block:
            @block.sync
            def _(sp):
                def load(p, q, i):
                    s = slot(q)
                    before = q + SLOTS * i - (2 if q < 2 else SLOTS)
                    sp.wait_ge(w_low.sem, w_low.at(p, before + 1))
                    sp.dma_start(stage[:, s, :], experts[bass.ds(q + SLOTS * i, 1), :, :].rearrange(
                        "e p n -> (e p) n")).then_inc(loaded[s].sem, 16)

                with sp.Fori(0, B // 2) as p:
                    for q in range(2):
                        load(p, q, 0)
                    with sp.Fori(0, LOOPS) as i:
                        for q in range(2, 2 + SLOTS):
                            load(p, q, i)

            @block.tensor
            def _(pe):
                def gates(p, q, i, k):
                    s, m = slot(q), 2 * q + k
                    if k == 0:
                        pe.wait_ge(w_low.sem, w_low.at(p, q + SLOTS * i + 1))
                    pe.wait_ge(hidden.sem, hidden.at(p, m + G * i - 1))
                    c = bass.ds(p * (2 * T) + k * T, T)
                    for bank, at in ((2 + k, 0), (4 + k, P)):
                        pe.matmul(ps[:, bank, :], lhsT=wh[:, s, at:at + P], rhs=xh[:, c], start=True, stop=False)
                        pe.matmul(ps[:, bank, :], lhsT=wl[:, s, at:at + P], rhs=xh[:, c], start=False, stop=False)
                        last = pe.matmul(ps[:, bank, :], lhsT=wh[:, s, at:at + P], rhs=xl[:, c], start=False, stop=True)
                    if q >= 2:
                        last = pe.matmul(ps[:, 6 + k, :], lhsT=wh[:, s, 3 * P:], rhs=rT[:, c], start=True, stop=True)
                    last.then_inc(gate_up.sem, 1)

                def down_product(p, q, i, k):
                    s, m = slot(q), 2 * q + k
                    if q == 0:
                        pe.wait_ge(added.sem, added.at(p, k - 1))
                    pe.wait_ge(low.sem, low.at(p, m + G * i + 1))
                    first, final = q == 0, q == CHUNKS - 1
                    r = m % 4
                    pe.matmul(ps[:, k, :], lhsT=wh[:, s, 2 * P:3 * P], rhs=hh[:, r, :], start=first, stop=False,
                              skip_group_check=True)
                    pe.matmul(ps[:, k, :], lhsT=wl[:, s, 2 * P:3 * P], rhs=hh[:, r, :], start=False, stop=False,
                              skip_group_check=True)
                    pe.matmul(ps[:, k, :], lhsT=wh[:, s, 2 * P:3 * P], rhs=hl[:, r, :], start=False, stop=final,
                              skip_group_check=True).then_inc(down.sem, 1)

                with pe.Fori(0, B // 2) as p:
                    for k in range(2):
                        gates(p, 0, 0, k)
                    for q in (1, 2):
                        for k in range(2):
                            gates(p, q, 0, k)
                            down_product(p, q - 1, 0, k)
                    with pe.Fori(0, LOOPS - 1) as i:
                        for q in range(3, 3 + SLOTS):
                            for k in range(2):
                                gates(p, q, i, k)
                                down_product(p, q - 1, i, k)
                    for q in range(CHUNKS - SLOTS + 1, CHUNKS):
                        for k in range(2):
                            gates(p, q, 0, k)
                            down_product(p, q - 1, 0, k)
                    for k in range(2):
                        down_product(p, CHUNKS - 1, 0, k)

            @block.scalar
            def _(act):
                def chunk(p, q, i, more=True):
                    for k in range(2):
                        m = 2 * q + k + G * i
                        act.wait_ge(gate_up.sem, gate_up.at(p, m + 1))
                        act.wait_ge(product.sem, product.at(p, m - 1))
                        act.activation(sg[:, k, :], ps[:, 2 + k, :], ACT.Silu).then_inc(silu.sem, 1)
                        if k == 0 and more:
                            high_part(p, q + 2, i)

                def high_part(p, q, i):
                    act.wait_ge(loaded[slot(q)].sem, loaded[slot(q)].at(p, uses(q, i)))
                    before = q + SLOTS * i - (2 if q < 2 else SLOTS)
                    act.wait_ge(down.sem, down.at(p, 2 * (before + 1)))
                    act.activation(wh[:, slot(q), :], stage[:, slot(q), :], ACT.Copy).then_inc(w_high.sem, 1)

                with act.Fori(0, B // 2) as p:
                    for q in range(2):
                        high_part(p, q, 0)
                    for q in range(2):
                        chunk(p, q, 0)
                    with act.Fori(0, LOOPS - 1) as i:
                        for q in range(2, 2 + SLOTS):
                            chunk(p, q, i)
                    for q in range(CHUNKS - SLOTS, CHUNKS):
                        chunk(p, q, 0, q + 2 < CHUNKS)

            @block.gpsimd
            def _(pool):
                def low_part(p, q, i):
                    s = slot(q)
                    pool.wait_ge(w_high.sem, w_high.at(p, q + SLOTS * i + 1))
                    pool.tensor_tensor(wl[:, s, :], stage[:, s, 0:3 * P], wh[:, s, 0:3 * P].bitcast(F32),
                                       ALU.subtract).then_inc(w_low.sem, 1)

                def chunk(p, q, i, more=True):
                    for k in range(2):
                        m = 2 * q + k
                        pool.wait_ge(high.sem, high.at(p, m + G * i + 1))
                        pool.wait_ge(down.sem, down.at(p, m + G * i - 3))
                        pool.tensor_tensor(hl[:, m % 4, :], h[:, k, :], hh[:, m % 4, :].bitcast(F32),
                                           ALU.subtract).then_inc(low.sem, 1)
                        if k == 0 and more:
                            low_part(p, q + 2, i)

                with pool.Fori(0, B // 2) as p:
                    for q in range(2):
                        low_part(p, q, 0)
                    for q in range(2):
                        chunk(p, q, 0)
                    with pool.Fori(0, LOOPS - 1) as i:
                        for q in range(2, 2 + SLOTS):
                            chunk(p, q, i)
                    for q in range(CHUNKS - SLOTS, CHUNKS):
                        chunk(p, q, 0, q + 2 < CHUNKS)

            @block.vector
            def _(dve):
                def chunk(p, q, i):
                    for k in range(2):
                        m = 2 * q + k
                        n = m + G * i
                        dve.wait_ge(silu.sem, silu.at(p, n + 1))
                        dve.wait_ge(low.sem, low.at(p, n - 1))
                        if q < 2:
                            dve.scalar_tensor_tensor(out=h[:, k, :], in0=sg[:, k, :], scalar=0.5, in1=ps[:, 4 + k, :],
                                                     op0=ALU.mult, op1=ALU.mult).then_inc(hidden.sem, 1)
                            dve.nop().then_inc(product.sem, 1)
                        else:
                            dve.wait_ge(hidden.sem, hidden.at(p, n - 1))
                            dve.tensor_tensor(gu[:, k, :], ps[:, 4 + k, :], sg[:, k, :],
                                              ALU.mult).then_inc(product.sem, 1)
                            dve.wait_ge(product.sem, product.at(p, n + 1))
                            dve.tensor_tensor(h[:, k, :], ps[:, 6 + k, :], gu[:, k, :], ALU.mult).then_inc(hidden.sem, 1)
                        dve.wait_ge(hidden.sem, hidden.at(p, n + 1))
                        dve.wait_ge(down.sem, down.at(p, n - 3))
                        dve.tensor_copy(hh[:, m % 4, :], h[:, k, :]).then_inc(high.sem, 1)

                with dve.Fori(0, B // 2) as p:
                    for q in range(2):
                        chunk(p, q, 0)
                    with dve.Fori(0, LOOPS) as i:
                        for q in range(2, 2 + SLOTS):
                            chunk(p, q, i)
                    for k in range(2):
                        dve.wait_ge(down.sem, down.at(p, PER - 1 + k))
                        x = X[:, bass.ds(p * (2 * T) + k * T, T)]
                        dve.tensor_tensor(x, x, ps[:, k, :], ALU.add).then_inc(added.sem, 1)

        for step in (*loaded, w_high, w_low, gate_up, silu, product, hidden, high, low, down, added):
            step.end(B // 2)


def mamba_layer(pr, tag, packed):
    nc, ps, XR = pr.nc, pr.psum, pr.XN
    o = MAMBA_PACK
    G = B // GROUP
    with ExitStack() as ctx:
        def sb(name, shape, dt=F32):
            return pr.sb(name + tag, shape, dt, ctx)

        W = sb("mw", [P, o["total"]])

        def part(name):
            return W[:, o[name][0]:o[name][1]]

        in_w, out_w = part("in_w"), part("out_w").rearrange("p (h n) -> p h n", h=HALF)
        xp_w = part("xp_w").rearrange("p (h n) -> p h n", h=HALF)
        dt_w = W[32:32 + DR, o["dt_w"][0]:o["dt_w"][1]]
        conv_w = part("conv_w").rearrange("p (h k) -> p h k", h=HALF)
        conv_b, dt_b, ln_w, ln_b = part("conv_b"), part("dt_b"), part("ln_w"), part("ln_b")
        skip_d = part("D")
        A = sb("A", [P, HALF, DS])
        diag = sb("diag", [P, HALF, P])
        w_mean = sb("w_mean", [P, HALF])
        out_c = sb("out_c", [P, HALF, P])
        xp = sb("xp", [P, 2, HALF, PAD + T])
        u = sb("u", [P, GROUP * HALF, T])
        sz = sb("sz", [P, GROUP * HALF, T])
        dt = sb("dt", [P, GROUP * HALF, T])
        dtu = sb("dtu", [P, GROUP * HALF, T])
        dts = sb("dts", [40, T])
        r1 = sb("r1", [32, T])
        r2 = sb("r2", [32, T])
        mid = sb("mid", [32, T], BF16)
        bc = sb("bc", [96, GROUP, T], BF16)
        dA = sb("dA", [P, 3, HALF, T])
        Bs = sb("Bs", [P, 3, T])
        dBu = sb("dBu", [P, 3, HALF, T])
        hh = sb("hh", [P, 3, HALF, T])
        hc = sb("hc", [P, 2, HALF, T])
        osq, oc, osd = (lambda s: dt[:, 2 * s, :]), (lambda s: dt[:, 2 * s + 1, :]), (lambda s: dtu[:, 2 * s, :])

        packed_in = pr.step("m_packed", 1, 16)
        ready = pr.step("m_ready", 10)
        with nc.Block() as block:
            @block.sync
            def _(sp):
                sp.dma_start(W[:, :], packed).then_inc(packed_in.sem, 16)

            @block.scalar
            def _(act):
                act.wait_ge(packed_in.sem, packed_in.at(0, 1))
                act.activation(A[:, :, :].rearrange("p h n -> p (h n)"), part("A_log"), ACT.Exp).then_inc(ready.sem, 1)

            @block.vector
            def _(dve):
                dve.memset(xp[:, :, :, 0:PAD], 0.0).then_inc(ready.sem, 1)
                dve.memset(dA[:, :, :, 0:1], 0.0).then_inc(ready.sem, 1)
                dve.wait_ge(packed_in.sem, packed_in.at(0, 1))
                for f in range(HALF):
                    dve.tensor_scalar(diag[:, f, :], pr.ident[:, :], skip_d[:, f:f + 1], None,
                                      ALU.mult).then_inc(ready.sem, 1)
                dve.tensor_reduce(w_mean[:, :], out_w, AX_X, ALU.add).then_inc(ready.sem, 1)
                dve.wait_ge(ready.sem, ready.at(0, 6))
                dve.tensor_scalar(A[:, :, :], A[:, :, :], -1.0, None, ALU.mult).then_inc(ready.sem, 1)
                dve.tensor_scalar(w_mean[:, :], w_mean[:, :], 1.0 / P, None, ALU.mult).then_inc(ready.sem, 1)
                dve.wait_ge(ready.sem, ready.at(0, 8))
                for f in range(HALF):
                    dve.tensor_scalar(out_c[:, f, :], out_w[:, f, :], w_mean[:, f:f + 1], None,
                                      ALU.subtract).then_inc(ready.sem, 1)
        packed_in.end(1)
        ready.end(1)

        xz = pr.step("m_xz", 4)
        xpc = pr.step("m_xp_copied", 2)
        szd = pr.step("m_silu_z", 2)
        conv = pr.step("m_conv", 8)
        ud = pr.step("m_u", 2)
        dbl = pr.step("m_x_dbl", 1)
        split = pr.step("m_split", 7)
        dtp = pr.step("m_dt_proj", 1)
        absd = pr.step("m_abs", 1)
        expd = pr.step("m_softplus_exp", 1)
        lnd = pr.step("m_softplus_log", 1)
        dmax = pr.step("m_dt_relu", 1)
        dtd = pr.step("m_dt", 1)
        dtud = pr.step("m_dtu", 1)
        bcast = pr.step("m_b_spread", DS)
        ccast = pr.step("m_c_spread", DS)
        decay = pr.step("m_decay", DS)
        bcopy = pr.step("m_b_copied", DS)
        driven = pr.step("m_driven", DS)
        scanned = pr.step("m_scanned", DS)
        read = pr.step("m_state_read", DS)
        ysum = pr.step("m_y_summed", DS + 1)
        gated = pr.step("m_gated", 1)
        outp = pr.step("m_out", 1)
        osqd = pr.step("m_squared", 1)
        ovar = pr.step("m_var", 1)
        oroot = pr.step("m_root", 1)
        orsd = pr.step("m_inv", 1)
        oinv = pr.step("m_scaled", 1)
        fin = pr.step("m_done", 1)

        def pair(t, s):
            return t[:, HALF * s:HALF * s + HALF, :]

        def y_bank(s):
            return 6 * (s % 2)

        order = [(s, n) for s in range(GROUP) for n in range(DS)]

        with nc.Block() as block:
            @block.tensor
            def _(pe):
                def inputs(b, s):
                    if s < 2:
                        pe.wait_ge(oinv.sem, oinv.at(b - s, 0))
                    else:
                        pe.wait_ge(xpc.sem, xpc.at(b - 2, 2))
                        pe.wait_ge(szd.sem, szd.at(b - 2, 2))
                    for c in range(4):
                        pe.matmul(ps[:, 4 * (s % 2) + c, :], lhsT=in_w[:, c * P:(c + 1) * P], rhs=cols(XR, b),
                                  start=True, stop=True).then_inc(xz.sem, 1)

                def x_dbl(b, s):
                    pe.wait_ge(ud.sem, ud.at(b, 2))
                    if s < 2:
                        pe.wait_ge(xpc.sem, xpc.at(b + 2, 2))
                        pe.wait_ge(szd.sem, szd.at(b + 2, 2))
                    else:
                        pe.wait_ge(split.sem, split.at(b - 2, 7))
                    for f in range(HALF):
                        last = pe.matmul(ps[0:40, 4 * (s % 2), :], lhsT=xp_w[:, f, :], rhs=u[:, HALF * s + f, :],
                                         start=(f == 0), stop=(f == HALF - 1))
                    last.then_inc(dbl.sem, 1)

                def step_size(b, s):
                    pe.wait_ge(split.sem, split.at(b, 1))
                    if s >= 2:
                        pe.wait_ge(dmax.sem, dmax.at(b - 2, 1))
                    for f in range(HALF):
                        last = pe.matmul(ps[:, 4 * (s % 2) + 1 + f, :], lhsT=dt_w[:, f * P:(f + 1) * P],
                                         rhs=dts[32:40, :], start=True, stop=True)
                    last.then_inc(dtp.sem, 1)

                def spread_b(b, s, n):
                    pe.wait_ge(bcopy.sem, bcopy.at(b, n - 1))
                    pe.matmul(ps[:, 2 + n % 2, :], lhsT=pr.sel[:, n, :], rhs=bc[:, s, :], start=True,
                              stop=True).then_inc(bcast.sem, 1)

                def spread_c(b, s, n):
                    pe.wait_ge(read.sem, read.at(b, n - 1))
                    pe.matmul(ps[:, 4 + n % 2, :], lhsT=pr.sel[:, DS + n, :], rhs=bc[:, s, :], start=True,
                              stop=True).then_inc(ccast.sem, 1)

                def skip_y(b, s):
                    pe.wait_ge(gated.sem, gated.at(b, -1))
                    for f in range(HALF):
                        last = pe.matmul(ps[:, y_bank(s) + f, :], lhsT=diag[:, f, :], rhs=u[:, HALF * s + f, :],
                                         start=True, stop=False)
                    last.then_inc(ysum.sem, 1)

                def sum_y(b, s, n):
                    pe.wait_ge(read.sem, read.at(b, n + 1))
                    for f in range(HALF):
                        last = pe.matmul(ps[:, y_bank(s) + f, :], lhsT=pr.ident[:, :], rhs=hc[:, n % 2, f, :], start=False,
                                         stop=(n == DS - 1))
                    last.then_inc(ysum.sem, 1)

                with pe.Fori(0, G) as g:
                    for s in range(GROUP):
                        inputs(GROUP * g + s, s)
                    x_dbl(GROUP * g, 0)
                    for s in range(GROUP):
                        if s + 1 < GROUP:
                            x_dbl(GROUP * g + s + 1, s + 1)
                        step_size(GROUP * g + s, s)
                    pe.wait_ge(split.sem, split.at(GROUP * g + GROUP, 0))
                    pe.wait_ge(dmax.sem, dmax.at(GROUP * g + GROUP, 0))
                    for n in range(4):
                        spread_b(GROUP * g, 0, n)
                        if n < 2:
                            spread_c(GROUP * g, 0, n)
                    for k, (s, n) in enumerate(order):
                        if n == 0:
                            skip_y(GROUP * g + s, s)
                        if k + 2 < len(order):
                            spread_c(GROUP * g + order[k + 2][0], *order[k + 2])
                        if k + 4 < len(order):
                            spread_b(GROUP * g + order[k + 4][0], *order[k + 4])
                        sum_y(GROUP * g + s, s, n)
                    pe.wait_ge(gated.sem, gated.at(GROUP * g + GROUP, 0))
                    for s in range(GROUP):
                        for f in range(HALF):
                            last = pe.matmul(ps[:, s, :], lhsT=out_c[:, f, :], rhs=sz[:, HALF * s + f, :],
                                             start=(f == 0), stop=(f == HALF - 1))
                        last.then_inc(outp.sem, 1)
                    for s in range(GROUP):
                        pe.wait_ge(osqd.sem, osqd.at(GROUP * g + s, 1))
                        pe.matmul(ps[:, 4 + s, :], lhsT=pr.mean[:, :], rhs=osq(s), start=True,
                                  stop=True).then_inc(ovar.sem, 1)

            @block.scalar
            def _(act):
                def inputs(b, s):
                    for f in range(HALF):
                        act.wait_ge(xz.sem, xz.at(b, f + 1))
                        act.wait_ge(conv.sem, conv.at(b - 2, 8))
                        act.activation(xp[:, s % 2, f, PAD:], ps[:, 4 * (s % 2) + f, :], ACT.Copy).then_inc(xpc.sem, 1)
                    for f in range(HALF):
                        act.wait_ge(xz.sem, xz.at(b, 3 + f))
                        act.activation(sz[:, HALF * s + f, :], ps[:, 4 * (s % 2) + 2 + f, :],
                                       ACT.Silu).then_inc(szd.sem, 1)

                def silu_u(b, s):
                    for f in range(HALF):
                        x = u[:, HALF * s + f, :]
                        act.wait_ge(conv.sem, conv.at(b, 7 + f))
                        act.activation(x, x, ACT.Silu).then_inc(ud.sem, 1)

                def softplus_tail(b, s):
                    x = dtu[:, HALF * s:HALF * s + HALF, :]
                    act.wait_ge(dtp.sem, dtp.at(b, 1))
                    for f in range(HALF):
                        last = act.activation(dtu[:, HALF * s + f, :], ps[:, 4 * (s % 2) + 1 + f, :], ACT.Abs,
                                              bias=dt_b[:, f:f + 1])
                    last.then_inc(absd.sem, 1)
                    act.wait_ge(absd.sem, absd.at(b, 1))
                    act.activation(x, x, ACT.Exp, scale=-1.0).then_inc(expd.sem, 1)
                    act.wait_ge(expd.sem, expd.at(b, 1))
                    act.activation(x, x, ACT.Ln, bias=1.0).then_inc(lnd.sem, 1)

                def copy_b(b, n, k):
                    act.wait_ge(bcast.sem, bcast.at(b, n + 1))
                    act.wait_ge(driven.sem, driven.at(b, n - 2))
                    act.activation(Bs[:, k % 3, :], ps[:, 2 + n % 2, :], ACT.Copy).then_inc(bcopy.sem, 1)

                def decays(b, s, n, k):
                    if n == 0:
                        act.wait_ge(dtd.sem, dtd.at(b, 1))
                    act.wait_ge(scanned.sem, scanned.at(b, n - 2))
                    for f in range(HALF):
                        last = act.activation(dA[:, k % 3, f, 1:], dt[:, HALF * s + f, 1:], ACT.Exp,
                                              scale=A[:, f, n:n + 1])
                    last.then_inc(decay.sem, 1)

                with act.Fori(0, G) as g:
                    for s in range(GROUP):
                        inputs(GROUP * g + s, s)
                        if s:
                            silu_u(GROUP * g + s - 1, s - 1)
                    silu_u(GROUP * g + GROUP - 1, GROUP - 1)
                    act.preload_act_table_set(LOG_EXP)
                    for s in range(GROUP):
                        softplus_tail(GROUP * g + s, s)
                    copy_b(GROUP * g, 0, 0)
                    decays(GROUP * g, 0, 0, 0)
                    copy_b(GROUP * g, 1, 1)
                    for k in range(1, len(order)):
                        decays(GROUP * g + order[k][0], *order[k], k)
                        if k + 1 < len(order):
                            copy_b(GROUP * g + order[k + 1][0], order[k + 1][1], k + 1)
                    for s in range(GROUP):
                        act.wait_ge(outp.sem, outp.at(GROUP * g + s, 1))
                        act.activation(osq(s), ps[:, s, :], ACT.Square).then_inc(osqd.sem, 1)
                    for s in range(GROUP):
                        act.wait_ge(ovar.sem, ovar.at(GROUP * g + s, 1))
                        act.activation(osd(s), ps[:, 4 + s, :], ACT.Ln, bias=pr.eps[:, 0:1]).then_inc(oroot.sem, 1)
                        act.wait_ge(oroot.sem, oroot.at(GROUP * g + s, 1))
                        act.activation(osd(s), osd(s), ACT.Exp, scale=-0.5).then_inc(orsd.sem, 1)

            @block.gpsimd
            def _(pool):
                with pool.Fori(0, G) as g:
                    for s in range(GROUP):
                        b, x = GROUP * g + s, slice(HALF * s, HALF * s + HALF)
                        pool.wait_ge(dmax.sem, dmax.at(b, 1))
                        pool.wait_ge(lnd.sem, lnd.at(b, 1))
                        pool.tensor_tensor(dt[:, x, :], dt[:, x, :], dtu[:, x, :], ALU.add).then_inc(dtd.sem, 1)
                        pool.wait_ge(dtd.sem, dtd.at(b, 1))
                        pool.tensor_tensor(dtu[:, x, :], dt[:, x, :], u[:, x, :], ALU.mult).then_inc(dtud.sem, 1)
                    for k, (s, n) in enumerate(order):
                        b, slot = GROUP * g + s, k % 3
                        if n == 0:
                            pool.wait_ge(dtud.sem, dtud.at(b, 1))
                        pool.wait_ge(bcopy.sem, bcopy.at(b, n + 1))
                        pool.wait_ge(scanned.sem, scanned.at(b, n - 2))
                        pool.tensor_tensor(dBu[:, slot, :, :], pair(dtu, s),
                                           Bs[:, slot, :].unsqueeze(1).to_broadcast([P, HALF, T]),
                                           ALU.mult).then_inc(driven.sem, 1)

            @block.vector
            def _(dve):
                def convolve(b, s):
                    for k in range(4):
                        for f in range(HALF):
                            out, x = u[:, HALF * s + f, :], xp[:, s % 2, f, k:k + T]
                            if k == 0:
                                dve.wait_ge(xpc.sem, xpc.at(b, f + 1))
                                ins = dve.tensor_scalar(out, x, conv_w[:, f, 0:1], conv_b[:, f:f + 1], ALU.mult,
                                                        ALU.add)
                            else:
                                dve.wait_ge(conv.sem, conv.at(b, 2 * k + f - 1))
                                ins = dve.scalar_tensor_tensor(out=out, in0=x, scalar=conv_w[:, f, k:k + 1], in1=out,
                                                               op0=ALU.mult, op1=ALU.add)
                            ins.then_inc(conv.sem, 1)

                def split_bc(b, s):
                    bank = 4 * (s % 2)
                    dve.wait_ge(dbl.sem, dbl.at(b, 1))
                    dve.wait_ge(dtp.sem, dtp.at(b, 0))
                    dve.tensor_copy(dts[32:40, :], ps[32:40, bank, :]).then_inc(split.sem, 1)
                    dve.tensor_copy(bc[0:32, s, :], ps[0:32, bank, :]).then_inc(split.sem, 1)
                    dve.wait_ge(split.sem, split.at(b, 2))
                    dve.tensor_tensor(r1[:, :], ps[0:32, bank, :], bc[0:32, s, :], ALU.subtract).then_inc(split.sem, 1)
                    dve.wait_ge(split.sem, split.at(b, 3))
                    dve.tensor_copy(mid[:, :], r1[:, :]).then_inc(split.sem, 1)
                    dve.tensor_copy(bc[32:64, s, :], r1[:, :]).then_inc(split.sem, 1)
                    dve.wait_ge(split.sem, split.at(b, 4))
                    dve.tensor_tensor(r2[:, :], r1[:, :], mid[:, :], ALU.subtract).then_inc(split.sem, 1)
                    dve.wait_ge(split.sem, split.at(b, 6))
                    dve.tensor_copy(bc[64:96, s, :], r2[:, :]).then_inc(split.sem, 1)

                def relu(b, s):
                    dve.wait_ge(dtp.sem, dtp.at(b, 1))
                    dve.wait_ge(absd.sem, absd.at(b, 1))
                    for f in range(HALF):
                        last = dve.tensor_scalar(dt[:, HALF * s + f, :], ps[:, 4 * (s % 2) + 1 + f, :],
                                                 dt_b[:, f:f + 1], 0.0, ALU.add, ALU.max)
                    last.then_inc(dmax.sem, 1)

                def scan(b, n, k):
                    dve.wait_ge(decay.sem, decay.at(b, n + 1))
                    dve.wait_ge(driven.sem, driven.at(b, n + 1))
                    dve.wait_ge(read.sem, read.at(b, n - 2))
                    dve.tensor_tensor_scan(hh[:, k % 3, :, :].rearrange("p h t -> p (h t)"),
                                           dA[:, k % 3, :, :].rearrange("p h t -> p (h t)"),
                                           dBu[:, k % 3, :, :].rearrange("p h t -> p (h t)"), 0.0,
                                           ALU.mult, ALU.add).then_inc(scanned.sem, 1)

                def read_state(b, n, k):
                    dve.wait_ge(scanned.sem, scanned.at(b, n + 1))
                    dve.wait_ge(ccast.sem, ccast.at(b, n + 1))
                    dve.wait_ge(ysum.sem, ysum.at(b, n))
                    dve.tensor_tensor(hc[:, n % 2, :, :], hh[:, k % 3, :, :],
                                      ps[:, 4 + n % 2, :].unsqueeze(1).to_broadcast([P, HALF, T]),
                                      ALU.mult).then_inc(read.sem, 1)

                def gate(b, s):
                    dve.wait_ge(ysum.sem, ysum.at(b, DS + 1))
                    dve.tensor_tensor(pair(sz, s), ps[:, y_bank(s):y_bank(s) + HALF, :], pair(sz, s),
                                      ALU.mult).then_inc(gated.sem, 1)

                with dve.Fori(0, G) as g:
                    for s in range(GROUP):
                        convolve(GROUP * g + s, s)
                    for s in range(GROUP):
                        split_bc(GROUP * g + s, s)
                        relu(GROUP * g + s, s)
                    scan(GROUP * g, 0, 0)
                    for k, (s, n) in enumerate(order):
                        if k + 1 < len(order):
                            scan(GROUP * g + order[k + 1][0], order[k + 1][1], k + 1)
                        read_state(GROUP * g + s, n, k)
                        if n == 1 and s:
                            gate(GROUP * g + s - 1, s - 1)
                    gate(GROUP * g + GROUP - 1, GROUP - 1)
                    for s in range(GROUP):
                        b = GROUP * g + s
                        dve.wait_ge(orsd.sem, orsd.at(b, 1))
                        dve.scalar_tensor_tensor(out=oc(s), in0=ps[:, s, :], scalar=ln_w, in1=osd(s), op0=ALU.mult,
                                                 op1=ALU.mult).then_inc(oinv.sem, 1)
                        dve.wait_ge(oinv.sem, oinv.at(b, 1))
                        dve.scalar_tensor_tensor(out=cols(XR, b), in0=oc(s), scalar=ln_b, in1=cols(XR, b), op0=ALU.add,
                                                 op1=ALU.add).then_inc(fin.sem, 1)

        for step in (xz, xpc, szd, conv, ud, dbl, split, dtp, absd, expd, lnd, dmax, dtd, dtud, bcast, ccast, decay, bcopy,
                     driven, scanned, read, ysum, gated, outp, osqd, ovar, oroot, orsd, oinv, fin):
            step.end(B)


def add_stream(pr, scale):
    nc, added = pr.nc, pr.step("stream_added", B)
    with nc.Block() as block:
        @block.vector
        def _(dve):
            for b in range(B):
                x, y = pr.X[:, b * T:(b + 1) * T], pr.XN[:, b * T:(b + 1) * T]
                dve.scalar_tensor_tensor(out=x, in0=y, scalar=scale, in1=x, op0=ALU.mult,
                                         op1=ALU.add).then_inc(added.sem, 1)
    added.end(1)


def cell_phase(pr, tag, packed):
    nc, ps, X, XN = pr.nc, pr.psum, pr.X, pr.XN
    o = CELL_PACK
    with ExitStack() as ctx:
        def sb(name):
            return pr.sb(name + tag, [P, 2, T], ctx=ctx)

        W = pr.sb("cw" + tag, [P, o["total"]], ctx=ctx)

        def part(name):
            return W[:, o[name][0]:o[name][1]]

        xp, al, be, v, bv, h, sh, co = (sb(x) for x in ("cxp", "cal", "cbe", "cv_", "cbv", "ch", "csh", "cco"))
        w_in = pr.step("c_packed", 1, 16)
        proj = pr.step("c_proj", 2)
        xpd = pr.step("c_xp", 2)
        gates = pr.step("c_gates", 2)
        acts = pr.step("c_acts", 2)
        bvd = pr.step("c_bv", 2)
        scanned = pr.step("c_scanned", 2)
        shd = pr.step("c_silu_h", 2)
        cod = pr.step("c_out", 2)
        outp = pr.step("c_out_proj", 2)
        fin = pr.step("c_done", 2)
        n = B // 2
        with nc.Block() as block:
            @block.sync
            def _(sp):
                sp.dma_start(W[:, :], packed).then_inc(w_in.sem, 16)

            @block.tensor
            def _(pe):
                pe.wait_ge(w_in.sem, w_in.at(0, 1))
                with pe.Fori(0, n) as i:
                    for s in range(2):
                        pe.wait_ge(xpd.sem, xpd.at(i, s - 1))
                        pe.wait_ge(fin.sem, fin.at(i, s - 1))
                        pe.matmul(ps[:, 4 * s, :], lhsT=part("w_in"), rhs=cols(XN, 2 * i + s), start=True,
                                  stop=True).then_inc(proj.sem, 1)
                    for s in range(2):
                        pe.wait_ge(xpd.sem, xpd.at(i, s + 1))
                        pe.wait_ge(acts.sem, acts.at(i, s - 1))
                        for k, name in enumerate(("w_a", "w_b", "w_v")):
                            last = pe.matmul(ps[:, 4 * s + 1 + k, :], lhsT=part(name), rhs=xp[:, s, :], start=True, stop=True)
                        last.then_inc(gates.sem, 1)
                    for s in range(2):
                        pe.wait_ge(cod.sem, cod.at(i, s + 1))
                        pe.matmul(ps[:, 4 * s, :], lhsT=part("w_out"), rhs=co[:, s, :], start=True,
                                  stop=True).then_inc(outp.sem, 1)

            @block.scalar
            def _(act):
                with act.Fori(0, n) as i:
                    for s in range(2):
                        act.wait_ge(proj.sem, proj.at(i, s + 1))
                        act.wait_ge(gates.sem, gates.at(i, s - 1))
                        act.activation(xp[:, s, :], ps[:, 4 * s, :], ACT.Silu).then_inc(xpd.sem, 1)
                    for s in range(2):
                        act.wait_ge(gates.sem, gates.at(i, s + 1))
                        act.wait_ge(scanned.sem, scanned.at(i, s - 1))
                        act.activation(al[:, s, :], ps[:, 4 * s + 1, :], ACT.Sigmoid, bias=part("b_a"))
                        act.activation(be[:, s, :], ps[:, 4 * s + 2, :], ACT.Sigmoid, bias=part("b_b"))
                        act.activation(v[:, s, :], ps[:, 4 * s + 3, :], ACT.Tanh, bias=part("b_v")).then_inc(acts.sem, 1)
                    for s in range(2):
                        act.wait_ge(scanned.sem, scanned.at(i, s + 1))
                        act.wait_ge(cod.sem, cod.at(i, s - 1))
                        act.activation(sh[:, s, :], h[:, s, :], ACT.Silu).then_inc(shd.sem, 1)

            @block.vector
            def _(dve):
                with dve.Fori(0, n) as i:
                    for s in range(2):
                        dve.wait_ge(acts.sem, acts.at(i, s + 1))
                        dve.wait_ge(scanned.sem, scanned.at(i, s - 1))
                        dve.tensor_tensor(bv[:, s, :], be[:, s, :], v[:, s, :], ALU.mult).then_inc(bvd.sem, 1)
                    for s in range(2):
                        dve.wait_ge(bvd.sem, bvd.at(i, s + 1))
                        dve.wait_ge(shd.sem, shd.at(i, s - 1))
                        dve.wait_ge(cod.sem, cod.at(i, s - 1))
                        dve.tensor_tensor_scan(h[:, s, :], al[:, s, :], bv[:, s, :], 0.0, ALU.mult,
                                               ALU.add).then_inc(scanned.sem, 1)
                    for s in range(2):
                        dve.wait_ge(shd.sem, shd.at(i, s + 1))
                        dve.wait_ge(scanned.sem, scanned.at(i, s + 1))
                        dve.wait_ge(outp.sem, outp.at(i, s - 1))
                        dve.tensor_tensor(co[:, s, :], h[:, s, :], sh[:, s, :], ALU.mult).then_inc(cod.sem, 1)
                    for s in range(2):
                        dve.wait_ge(outp.sem, outp.at(i, s + 1))
                        x = cols(X, 2 * i + s)
                        dve.tensor_tensor(x, x, ps[:, 4 * s, :], ALU.add).then_inc(fin.sem, 1)

        w_in.end(1)
        for s in (proj, xpd, gates, acts, bvd, scanned, shd, cod, outp, fin):
            s.end(n)


def attention_layer(pr, tag, packed, tables):
    nc = pr.nc
    o = FFN_PACK
    cut = o["w2"][1]
    ctx = ExitStack()
    with ctx:
        Wh = pr.sb("fwh" + tag, [P, cut], F32R, ctx)
        Wl = pr.sb("fwl" + tag, [P, cut], F32R, ctx)
        vec = pr.sb("fvec" + tag, [P, o["total"] - cut], ctx=ctx)
        rot = pr.sb("rot" + tag, [P, 4, T], ctx=ctx)

        def both(name):
            return Wh[:, o[name][0]:o[name][1]], Wl[:, o[name][0]:o[name][1]]

        def part(name):
            return vec[:, o[name][0] - cut:o[name][1] - cut]

        pieces = [slice(cut * k // 4, cut * (k + 1) // 4) for k in range(4)]
        loads = [pr.step(f"f_packed_{k}", 1, 16) for k in "abcd"]
        w_in = pr.step("f_packed", 2, 16)
        w_high = pr.step("f_w_high", 4)
        ready = pr.step("f_ready", 8)
        with ExitStack() as tctx:
            stage = pr.sb("fstage" + tag, [P, cut], ctx=tctx)
            with nc.Block() as block:
                @block.sync
                def _(sp):
                    for load, c in zip(loads, pieces):
                        sp.dma_start(stage[:, c], packed[:, c]).then_inc(load.sem, 16)
                    sp.dma_start(vec[:, :], packed[:, cut:]).then_inc(w_in.sem, 16)
                    sp.dma_start(rot[:, :, :].rearrange("p c t -> p (c t)"), tables).then_inc(w_in.sem, 16)

                @block.scalar
                def _(act):
                    for load, c in zip(loads, pieces):
                        act.wait_ge(load.sem, load.at(0, 1))
                        act.activation(Wh[:, c], stage[:, c], ACT.Copy).then_inc(w_high.sem, 1)

                @block.vector
                def _(dve):
                    for k, c in enumerate(pieces):
                        dve.wait_ge(w_high.sem, w_high.at(0, k + 1))
                        dve.tensor_tensor(Wl[:, c], stage[:, c], Wh[:, c].bitcast(F32),
                                          ALU.subtract).then_inc(ready.sem, 1)
                    dve.wait_ge(w_in.sem, w_in.at(0, 2))
                    for k, name in enumerate(("qs", "qsr", "ks", "ksr")):
                        dve.tensor_scalar(rot[:, k, :], rot[:, k, :], part(name), None, ALU.mult).then_inc(ready.sem, 1)
        for step in (*loads, w_in, w_high, ready):
            step.end(1)
        with ExitStack() as actx:
            attention_phase(pr, tag, actx, both, rot)
        with ExitStack() as fctx:
            feed_forward_phase(pr, tag, fctx, both, part)


def attention_phase(pr, tag, ctx, both, rot):
    nc, ps, XR = pr.nc, pr.psum, pr.XN

    def sb(name, shape, dt=F32):
        return pr.sb(name + tag, shape, dt, ctx)

    hTh = sb("hTh", [P, WIN + T], F32R)
    hTl = sb("hTl", [P, WIN + T], F32R)
    sq = sb("sq_", [P, 4, T])
    rot_a = sb("rot_a", [P, 2, T])
    rot_b = sb("rot_b", [P, 2, T])
    qf = sb("qf", [P, PAIRS, T])
    kr = sb("kr", [P, PAIRS, T])
    kn = sb("kn", [P, PAIRS, T])
    kf = sb("kf", [P, PAIRS, WIN + T])
    cr = sb("cr", [P, PAIRS * NW])
    cq = sb("cq", [P, PAIRS * NW])
    V = sb("V", [P, NW, HEADS * DH])
    mx = sb("mx", [P, NW])
    nb = sb("nb", [P, 2, NW])
    sm = sb("sm", [P, 2, NW])
    rsm = sb("rsm", [P, 2, NW])
    Pr = sb("Pr", [P, 2, NW, P])
    PT = sb("PT", [P, NW, P])
    oTh = sb("oTh", [P, PAIRS, T], F32R)
    oTl = sb("oTl", [P, PAIRS, T], F32R)

    padded = pr.step("f_padded", 3)
    with nc.Block() as block:
        @block.vector
        def _(dve):
            dve.memset(hTh[:, 0:WIN + 1].bitcast(F32), 0.0).then_inc(padded.sem, 1)
            dve.memset(hTl[:, 0:WIN + 1].bitcast(F32), 0.0).then_inc(padded.sem, 1)
            dve.memset(kf[:, :, 0:WIN], 0.0).then_inc(padded.sem, 1)
    padded.end(1)

    shifted = pr.step("f_shifted", 2)
    shift_low = pr.step("f_shifted_low", 2)
    proj = pr.step("f_proj", 2 * PAIRS)
    squared = pr.step("f_squared", 2 * PAIRS)
    rota = pr.step("f_rotated_parts", 2 * PAIRS)
    rotb = pr.step("f_rotated", 2 * PAIRS)
    knorm = pr.step("f_k_norm", PAIRS)
    ksd = pr.step("f_k_norm_kept", PAIRS)
    kroot = pr.step("f_k_root", PAIRS)
    kinv = pr.step("f_k_inv", PAIRS)
    kfd = pr.step("f_k", PAIRS)
    qnorm = pr.step("f_q_norm", PAIRS)
    cqs = pr.step("f_q_norm_kept", PAIRS)
    qroot = pr.step("f_q_root", PAIRS)
    qlog = pr.step("f_q_log", PAIRS)
    vp = pr.step("f_v_proj", NW)
    va = pr.step("f_v_even", NW // 2)
    vb = pr.step("f_v_odd", NW // 2)
    sim = pr.step("f_sim", PAIRS)
    maxed = pr.step("f_max", PAIRS)
    nbd = pr.step("f_bias", PAIRS)
    expd = pr.step("f_exp", PAIRS)
    rsd = pr.step("f_sum_inv", PAIRS)
    pn = pr.step("f_probs", PAIRS)
    turned = pr.step("f_turned", PAIRS)
    pta = pr.step("f_turned_copied_a", PAIRS)
    ptb = pr.step("f_turned_copied_b", PAIRS)
    pv = pr.step("f_pv", PAIRS)
    oTd = pr.step("f_o", 2 * PAIRS)
    wod = pr.step("f_wo", 1)
    x1d = pr.step("f_x1", 1)
    heads = [slice(a * DH, (a + 1) * DH) for a in range(2)]
    SCORE, TURN, PROJ, OUT, NORM = 0, 2, 4, 6, 7
    VALUE = (PROJ, PROJ + 1, TURN, TURN + 1)

    def three_passes(pe, out, w, x, start, stop):
        (wh, wl), (xh, xl) = w, x
        pe.matmul(out, lhsT=wh, rhs=xh, start=start, stop=False)
        pe.matmul(out, lhsT=wl, rhs=xh, start=False, stop=False)
        return pe.matmul(out, lhsT=wh, rhs=xl, start=False, stop=stop)

    with nc.Block() as block:
        @block.tensor
        def _(pe):
            def project(b, p, isk):
                unit = 2 * p + isk
                if unit == 0:
                    pe.wait_ge(shift_low.sem, shift_low.at(b, 2))
                    pe.wait_ge(va.sem, va.at(b, 0))
                    pe.wait_ge(vb.sem, vb.at(b, 0))
                pe.wait_ge(rota.sem, rota.at(b, unit))
                for r, name in enumerate(("wk", "wkr") if isk else ("wq", "wqr")):
                    h, l = both(name)
                    c = slice(p * P, (p + 1) * P)
                    last = three_passes(pe, ps[:, PROJ + r, :], (h[:, c], l[:, c]), (hTh[:, WIN:], hTl[:, WIN:]),
                                        True, True)
                last.then_inc(proj.sem, 1)

            def k_norm(b, p):
                pe.wait_ge(squared.sem, squared.at(b, 2 * p + 2))
                pe.wait_ge(cqs.sem, cqs.at(b, p))
                pe.matmul(ps[:, NORM, :], lhsT=pr.heads[:, :], rhs=sq[:, (2 * p + 1) % 4, :], start=True,
                          stop=True).then_inc(knorm.sem, 1)

            def q_norm(b, p):
                pe.wait_ge(ksd.sem, ksd.at(b, p + 1))
                for w in range(NW // 2):
                    last = pe.matmul(ps[:, NORM, w:w + NW // 2 + 1:NW // 2], lhsT=sq[:, (2 * p) % 4, w * P:(w + 1) * P],
                                     rhs=pr.heads[:, DH - 1:DH + 1], start=True, stop=True)
                last.then_inc(qnorm.sem, 1)

            def values_of(b, windows):
                wv = both("wv")
                for w in windows:
                    if w == 0:
                        pe.wait_ge(rota.sem, rota.at(b, 2 * PAIRS))
                    elif w == 2:
                        pe.wait_ge(pta.sem, pta.at(b, 0))
                        pe.wait_ge(ptb.sem, ptb.at(b, 0))
                    elif w >= 4 and w % 2 == 0:
                        pe.wait_ge(va.sem, va.at(b, w // 2 - 1))
                    elif w >= 4:
                        pe.wait_ge(vb.sem, vb.at(b, w // 2 - 1))
                    c = slice(w * WIN, (w + 2) * WIN)
                    three_passes(pe, ps[:, VALUE[w % 4], :], (hTh[:, c], hTl[:, c]), wv, True, True).then_inc(vp.sem, 1)

            def scores(b, p):
                pe.wait_ge(kfd.sem, kfd.at(b, p + 1))
                pe.wait_ge(rotb.sem, rotb.at(b, 2 * p + 1))
                pe.wait_ge(expd.sem, expd.at(b, p))
                for half in range(2):
                    pe.matmul(ps[:, SCORE + half, :], lhsT=pr.ident_b[:, :], rhs=pr.mask[:, :], start=True, stop=False,
                              skip_group_check=True)
                for w in range(NW):
                    for a in range(2):
                        at = w // 2
                        last = pe.matmul(ps[heads[w % 2], SCORE + a, at * P:(at + 1) * P],
                                         lhsT=qf[heads[a], p, w * WIN:(w + 1) * WIN],
                                         rhs=kf[heads[a], p, w * WIN:(w + 2) * WIN], start=False, stop=True,
                                         skip_group_check=True)
                last.then_inc(sim.sem, 1)

            def turn(b, p):
                if p == 0:
                    pe.wait_ge(va.sem, va.at(b, NW // 2))
                    pe.wait_ge(vb.sem, vb.at(b, NW // 2))
                pe.wait_ge(pn.sem, pn.at(b, p + 1))
                pe.wait_ge(pta.sem, pta.at(b, p))
                pe.wait_ge(ptb.sem, ptb.at(b, p))
                for at in range(NW):
                    last = pe.transpose(ps[:, TURN + at // 4, (at % 4) * P:(at % 4 + 1) * P], Pr[:, p % 2, at, :],
                                        pr.ident[:, :])
                last.then_inc(turned.sem, 1)

            def weigh(b, p):
                pe.wait_ge(pta.sem, pta.at(b, p + 1))
                pe.wait_ge(ptb.sem, ptb.at(b, p + 1))
                if p == 0:
                    pe.wait_ge(va.sem, va.at(b, NW // 2))
                    pe.wait_ge(vb.sem, vb.at(b, NW // 2))
                    pe.wait_ge(x1d.sem, x1d.at(b, 0))
                pe.wait_ge(oTd.sem, oTd.at(b, 2 * p))
                for w in range(NW):
                    for a in range(2):
                        last = pe.matmul(ps[heads[a], OUT, w * WIN:(w + 1) * WIN],
                                         lhsT=V[:, w, (2 * p + a) * DH:(2 * p + a + 1) * DH],
                                         rhs=PT[:, NW // 2 * a + w // 2, heads[w % 2]], start=True, stop=True)
                last.then_inc(pv.sem, 1)

            def out_product(b, pairs):
                pe.wait_ge(oTd.sem, oTd.at(b, 2 * PAIRS))
                h, l = both("wo")
                for p in pairs:
                    c = slice(p * P, (p + 1) * P)
                    last = three_passes(pe, ps[:, OUT, :], (h[:, c], l[:, c]), (oTh[:, p, :], oTl[:, p, :]), p == 0,
                                        p == PAIRS - 1)
                if p == PAIRS - 1:
                    last.then_inc(wod.sem, 1)

            def sequence(b, nxt, before):
                for p in range(PAIRS):
                    if p:
                        scores(b, p)
                    elif before is not None:
                        out_product(before, (0, 1))
                    if nxt is not None:
                        project(nxt, p, 0)
                    if p:
                        turn(b, p - 1)
                    elif before is not None:
                        out_product(before, (2, 3))
                    if nxt is not None:
                        if p:
                            q_norm(nxt, p - 1)
                        project(nxt, p, 1)
                    if p:
                        weigh(b, p - 1)
                    if nxt is not None:
                        k_norm(nxt, p)
                if nxt is not None:
                    scores(nxt, 0)
                    q_norm(nxt, PAIRS - 1)
                    values_of(nxt, (0, 1))
                turn(b, PAIRS - 1)
                weigh(b, PAIRS - 1)
                if nxt is not None:
                    values_of(nxt, range(2, NW))

            for p in range(PAIRS):
                project(0, p, 0)
                if p:
                    k_norm(0, p - 1)
                project(0, p, 1)
                if p:
                    q_norm(0, p - 1)
            k_norm(0, PAIRS - 1)
            q_norm(0, PAIRS - 1)
            scores(0, 0)
            values_of(0, range(NW))
            sequence(0, 1, None)
            with pe.Fori(0, B - 2) as i:
                sequence(i + 1, i + 2, i)
            sequence(B - 1, None, B - 2)
            out_product(B - 1, range(PAIRS))

        @block.scalar
        def _(act):
            act.preload_act_table_set(LOG_EXP)

            def square(b, p, isk):
                unit = 2 * p + isk
                act.wait_ge(proj.sem, proj.at(b, unit + 1))
                act.wait_ge(qnorm.sem, qnorm.at(b, p - 1))
                act.activation(sq[:, unit % 4, :], ps[:, PROJ, :], ACT.Square).then_inc(squared.sem, 1)

            def probs(b, p, half):
                if half == 0:
                    act.wait_ge(nbd.sem, nbd.at(b, p + 1))
                    act.wait_ge(turned.sem, turned.at(b, p - 1))
                    act.wait_ge(rsd.sem, rsd.at(b, p - 1))
                for w in range(4 * half, 4 * half + 4):
                    last = act.activation(Pr[:, p % 2, w, :], ps[:, SCORE + w // 4, (w % 4) * P:(w % 4 + 1) * P],
                                          ACT.Exp, bias=nb[:, p % 2, w:w + 1],
                                          scale=cq[:, p * NW + w:p * NW + w + 1],
                                          accum_out=sm[:, p % 2, w:w + 1])
                if half:
                    last.then_inc(expd.sem, 1)

            def copy_turned(b, p):
                act.wait_ge(turned.sem, turned.at(b, p + 1))
                act.wait_ge(pv.sem, pv.at(b, p))
                act.activation(PT[:, 0:4, :].rearrange("p w q -> p (w q)"), ps[:, TURN, :],
                               ACT.Copy).then_inc(pta.sem, 1)

            def roots(b, p):
                act.wait_ge(ksd.sem, ksd.at(b, p + 1))
                act.activation(kn[:, p, :], kn[:, p, :], ACT.Ln).then_inc(kroot.sem, 1)
                act.wait_ge(cqs.sem, cqs.at(b, p + 1))
                c = slice(p * NW, (p + 1) * NW)
                act.activation(cr[:, c], cr[:, c], ACT.Ln).then_inc(qlog.sem, 1)
                act.wait_ge(kroot.sem, kroot.at(b, p + 1))
                act.activation(kn[:, p, :], kn[:, p, :], ACT.Exp, scale=-0.5).then_inc(kinv.sem, 1)
                act.wait_ge(qlog.sem, qlog.at(b, p + 1))
                act.wait_ge(expd.sem, expd.at(b, p + 1 - PAIRS))
                act.wait_ge(nbd.sem, nbd.at(b, p + 1 - PAIRS))
                act.activation(cq[:, c], cr[:, c], ACT.Exp, scale=-0.5).then_inc(qroot.sem, 1)

            def copy_values(b):
                act.wait_ge(pv.sem, pv.at(b, 0))
                for w in range(0, NW, 2):
                    act.wait_ge(vp.sem, vp.at(b, w + 1))
                    act.activation(V[:, w, :], ps[:, VALUE[w % 4], :], ACT.Copy).then_inc(va.sem, 1)

            def sequence(b, nxt):
                for p in range(PAIRS):
                    if nxt is not None:
                        square(nxt, p, 0)
                    if p:
                        probs(b, p, 0)
                        copy_turned(b, p - 1)
                    if nxt is not None:
                        square(nxt, p, 1)
                    if p:
                        probs(b, p, 1)
                    if nxt is not None and p:
                        roots(nxt, p - 1)
                copy_turned(b, PAIRS - 1)
                if nxt is not None:
                    probs(nxt, 0, 0)
                    copy_values(nxt)
                    probs(nxt, 0, 1)
                    roots(nxt, PAIRS - 1)

            for p in range(PAIRS):
                square(0, p, 0)
                square(0, p, 1)
                if p:
                    roots(0, p - 1)
            roots(0, PAIRS - 1)
            probs(0, 0, 0)
            probs(0, 0, 1)
            copy_values(0)
            with act.Fori(0, B - 1) as i:
                sequence(i, i + 1)
            sequence(B - 1, None)

        @block.gpsimd
        def _(pool):
            def rotate(b, p, isk):
                unit = 2 * p + isk
                pool.wait_ge(rota.sem, rota.at(b, unit + 1))
                if isk:
                    pool.wait_ge(kfd.sem, kfd.at(b, p + 1 - PAIRS))
                else:
                    pool.wait_ge(sim.sem, sim.at(b, p + 1 - PAIRS))
                dst = kr if isk else qf
                pool.tensor_tensor(dst[:, p, :], rot_a[:, unit % 2, :], rot_b[:, unit % 2, :],
                                   ALU.add).then_inc(rotb.sem, 1)

            def normalise(b, p):
                pool.wait_ge(rsd.sem, rsd.at(b, p + 1))
                pool.tensor_tensor(Pr[:, p % 2, :, :], Pr[:, p % 2, :, :],
                                   rsm[:, p % 2, :].unsqueeze(2).to_broadcast([P, NW, P]),
                                   ALU.mult).then_inc(pn.sem, 1)

            def keys(b, p):
                pool.wait_ge(kinv.sem, kinv.at(b, p + 1))
                pool.wait_ge(rotb.sem, rotb.at(b, 2 * p + 2))
                pool.wait_ge(sim.sem, sim.at(b, p + 1 - PAIRS))
                pool.tensor_tensor(kf[:, p, WIN:], kr[:, p, :], kn[:, p, :], ALU.mult).then_inc(kfd.sem, 1)

            def sequence(b, nxt):
                for p in range(PAIRS):
                    if p:
                        normalise(b, p - 1)
                    if nxt is not None:
                        rotate(nxt, p, 0)
                        rotate(nxt, p, 1)
                        if p:
                            keys(nxt, p - 1)
                normalise(b, PAIRS - 1)
                if nxt is not None:
                    keys(nxt, PAIRS - 1)

            for p in range(PAIRS):
                rotate(0, p, 0)
                rotate(0, p, 1)
                if p:
                    keys(0, p - 1)
            keys(0, PAIRS - 1)
            with pool.Fori(0, B - 1) as i:
                sequence(i, i + 1)
            sequence(B - 1, None)

        @block.vector
        def _(dve):
            def shift(b):
                dve.wait_ge(vp.sem, vp.at(b, 0))
                dve.tensor_copy(hTh[0:DH, WIN:], XR[0:DH, bass.ds(b * T, T)]).then_inc(shifted.sem, 1)
                dve.tensor_copy(hTh[DH:P, WIN + 1:], XR[DH:P, bass.ds(b * T, T - 1)]).then_inc(shifted.sem, 1)
                dve.wait_ge(shifted.sem, shifted.at(b, 2))
                dve.tensor_tensor(hTl[0:DH, WIN:], XR[0:DH, bass.ds(b * T, T)], hTh[0:DH, WIN:].bitcast(F32),
                                  ALU.subtract).then_inc(shift_low.sem, 1)
                dve.tensor_tensor(hTl[DH:P, WIN + 1:], XR[DH:P, bass.ds(b * T, T - 1)],
                                  hTh[DH:P, WIN + 1:].bitcast(F32), ALU.subtract).then_inc(shift_low.sem, 1)

            def rotate(b, p, isk):
                unit = 2 * p + isk
                dve.wait_ge(proj.sem, proj.at(b, unit + 1))
                dve.wait_ge(rotb.sem, rotb.at(b, unit - 1))
                dve.tensor_tensor(rot_b[:, unit % 2, :], ps[:, PROJ + 1, :], rot[:, 2 * isk + 1, :], ALU.mult)
                dve.wait_ge(squared.sem, squared.at(b, unit + 1))
                dve.tensor_tensor(rot_a[:, unit % 2, :], ps[:, PROJ, :], rot[:, 2 * isk, :],
                                  ALU.mult).then_inc(rota.sem, 1)

            def keep_k(b, p):
                dve.wait_ge(knorm.sem, knorm.at(b, p + 1))
                dve.wait_ge(kfd.sem, kfd.at(b, p + 1 - PAIRS))
                dve.tensor_scalar(kn[:, p, :], ps[:, NORM, :], 1e-24, None, ALU.max).then_inc(ksd.sem, 1)

            def keep_q(b, p):
                dve.wait_ge(qnorm.sem, qnorm.at(b, p + 1))
                dve.wait_ge(qlog.sem, qlog.at(b, p + 1 - PAIRS))
                dve.tensor_scalar(cr[:, p * NW:(p + 1) * NW], ps[:, NORM, 0:NW], 1e-24, QK_SCALE ** -2, ALU.max,
                                  ALU.mult).then_inc(cqs.sem, 1)

            def copy_values(b):
                dve.wait_ge(pv.sem, pv.at(b, 0))
                for w in range(1, NW, 2):
                    dve.wait_ge(vp.sem, vp.at(b, w + 1))
                    dve.tensor_copy(V[:, w, :], ps[:, VALUE[w % 4], :]).then_inc(vb.sem, 1)

            def row_max(b, p):
                dve.wait_ge(sim.sem, sim.at(b, p + 1))
                dve.wait_ge(nbd.sem, nbd.at(b, p))
                dve.tensor_reduce(mx[:, :], ps[:, SCORE:SCORE + 2, :].rearrange("p b (w k) -> p (b w) k", k=P),
                                  AX_X, ALU.max).then_inc(maxed.sem, 1)
                dve.wait_ge(maxed.sem, maxed.at(b, p + 1))
                dve.wait_ge(qroot.sem, qroot.at(b, p + 1))
                dve.wait_ge(expd.sem, expd.at(b, p - 1))
                dve.scalar_tensor_tensor(out=nb[:, p % 2, :], in0=mx[:, :], scalar=-1.0,
                                         in1=cq[:, p * NW:(p + 1) * NW], op0=ALU.mult,
                                         op1=ALU.mult).then_inc(nbd.sem, 1)

            def sum_inverse(b, p):
                dve.wait_ge(expd.sem, expd.at(b, p + 1))
                dve.wait_ge(pn.sem, pn.at(b, p - 1))
                dve.reciprocal(rsm[:, p % 2, :], sm[:, p % 2, :]).then_inc(rsd.sem, 1)

            def copy_turned(b, p):
                dve.wait_ge(turned.sem, turned.at(b, p + 1))
                dve.wait_ge(pv.sem, pv.at(b, p))
                dve.tensor_copy(PT[:, 4:8, :].rearrange("p w q -> p (w q)"), ps[:, TURN + 1, :]).then_inc(ptb.sem, 1)

            def split_o(b, p):
                dve.wait_ge(pv.sem, pv.at(b, p + 1))
                dve.wait_ge(wod.sem, wod.at(b, 0))
                dve.tensor_copy(oTh[:, p, :], ps[:, OUT, :]).then_inc(oTd.sem, 1)
                dve.wait_ge(oTd.sem, oTd.at(b, 2 * p + 1))
                dve.tensor_tensor(oTl[:, p, :], ps[:, OUT, :], oTh[:, p, :].bitcast(F32),
                                  ALU.subtract).then_inc(oTd.sem, 1)

            def add_product(b):
                dve.wait_ge(wod.sem, wod.at(b, 1))
                x = XR[:, bass.ds(b * T, T)]
                dve.tensor_tensor(x, x, ps[:, OUT, :], ALU.add).then_inc(x1d.sem, 1)

            def sequence(b, nxt, before):
                if nxt is not None:
                    shift(nxt)
                for p in range(PAIRS):
                    if p:
                        sum_inverse(b, p - 1)
                        row_max(b, p)
                    if nxt is not None:
                        rotate(nxt, p, 0)
                    if p:
                        copy_turned(b, p - 1)
                        if nxt is not None:
                            keep_q(nxt, p - 1)
                    elif before is not None:
                        add_product(before)
                    if nxt is not None:
                        rotate(nxt, p, 1)
                    if p:
                        split_o(b, p - 1)
                    if nxt is not None:
                        keep_k(nxt, p)
                sum_inverse(b, PAIRS - 1)
                if nxt is not None:
                    row_max(nxt, 0)
                    keep_q(nxt, PAIRS - 1)
                copy_turned(b, PAIRS - 1)
                split_o(b, PAIRS - 1)
                if nxt is not None:
                    copy_values(nxt)

            shift(0)
            for p in range(PAIRS):
                rotate(0, p, 0)
                if p:
                    keep_k(0, p - 1)
                rotate(0, p, 1)
                if p:
                    keep_q(0, p - 1)
            keep_k(0, PAIRS - 1)
            keep_q(0, PAIRS - 1)
            row_max(0, 0)
            copy_values(0)
            sequence(0, 1, None)
            with dve.Fori(0, B - 2) as i:
                sequence(i + 1, i + 2, i)
            sequence(B - 1, None, B - 2)
            add_product(B - 1)

    for step in (shifted, shift_low, proj, squared, rota, rotb, knorm, ksd, kroot, kinv, kfd, qnorm, cqs, qroot, qlog, vp,
                 va, vb, sim, maxed, nbd, expd, rsd, pn, turned, pta, ptb, pv, oTd, wod, x1d):
        step.end(B)


def shifted_norm_phase(pr, tag, part, xh, xl):
    nc, ps, XR = pr.nc, pr.psum, pr.XN
    U = 4
    with ExitStack() as ctx:
        def sb(name):
            return pr.sb(name + tag, [P, U, T], ctx=ctx)

        sq, rs, xc, xn = (sb(x) for x in ("fsq", "frs", "fxc", "fxn"))
        h2 = pr.sb("h2" + tag, [P, AHEAD, T], ctx=ctx)
        padded = pr.step("f_padded", 1)
        shifted = pr.step("g_shifted", 2 * B)
        cent = pr.step("g_centered", B)
        squared = pr.step("g_squared", B)
        var = pr.step("g_var", B)
        root = pr.step("g_root", B)
        inv = pr.step("g_inv", B)
        scaled = pr.step("g_scaled", B)
        normed = pr.step("g_normed", B)
        high = pr.step("g_high", B)
        low = pr.step("g_low", B)
        with nc.Block() as block:
            @block.tensor
            def _(pe):
                def center(s):
                    pe.wait_ge(shifted.sem, shifted.at(0, 2 * s + 2))
                    pe.wait_ge(padded.sem, padded.at(0, 1))
                    if s >= AHEAD:
                        pe.wait_ge(scaled.sem, scaled.at(0, s + 1 - AHEAD))
                    pe.matmul(ps[:, s % AHEAD, :], lhsT=pr.center[:, :], rhs=h2[:, s % AHEAD, :], start=True,
                              stop=True).then_inc(cent.sem, 1)

                for s in range(AHEAD):
                    center(s)
                for s in range(B):
                    pe.wait_ge(squared.sem, squared.at(0, s + 1))
                    if s >= VARS:
                        pe.wait_ge(root.sem, root.at(0, s + 1 - VARS))
                    pe.matmul(ps[:, AHEAD + s % VARS, :], lhsT=pr.mean[:, :], rhs=sq[:, s % U, :], start=True,
                              stop=True).then_inc(var.sem, 1)
                    if 1 <= s <= B - AHEAD:
                        center(s - 1 + AHEAD)

            @block.scalar
            def _(act):
                def square(s):
                    act.wait_ge(cent.sem, cent.at(0, s + 1))
                    if s >= U:
                        act.wait_ge(var.sem, var.at(0, s + 1 - U))
                    act.activation(sq[:, s % U, :], ps[:, s % AHEAD, :], ACT.Square).then_inc(squared.sem, 1)

                def log(s):
                    act.wait_ge(var.sem, var.at(0, s + 1))
                    if s >= U:
                        act.wait_ge(scaled.sem, scaled.at(0, s + 1 - U))
                    act.activation(rs[:, s % U, :], ps[:, AHEAD + s % VARS, :], ACT.Ln,
                                   bias=pr.eps[:, 0:1]).then_inc(root.sem, 1)

                def exp(s):
                    act.wait_ge(root.sem, root.at(0, s + 1))
                    act.activation(rs[:, s % U, :], rs[:, s % U, :], ACT.Exp, scale=-0.5).then_inc(inv.sem, 1)

                def high_part(s):
                    act.wait_ge(normed.sem, normed.at(0, s + 1))
                    act.activation(xh[:, s, :], xn[:, s % U, :], ACT.Copy).then_inc(high.sem, 1)

                act.preload_act_table_set(LOG_EXP)
                square(0)
                square(1)
                for s in range(B):
                    if s + 2 < B:
                        square(s + 2)
                    log(s)
                    exp(s)
                    if s:
                        high_part(s - 1)
                high_part(B - 1)

            @block.gpsimd
            def _(pool):
                for s in range(B):
                    pool.wait_ge(high.sem, high.at(0, s + 1))
                    pool.tensor_tensor(xl[:, s, :], xn[:, s % U, :], xh[:, s, :].bitcast(F32),
                                       ALU.subtract).then_inc(low.sem, 1)

            @block.vector
            def _(dve):
                def shift(s):
                    if s >= AHEAD:
                        dve.wait_ge(cent.sem, cent.at(0, s + 1 - AHEAD))
                    dve.tensor_copy(h2[0:DH, s % AHEAD, :], XR[0:DH, s * T:(s + 1) * T]).then_inc(shifted.sem, 1)
                    dve.tensor_copy(h2[DH:P, s % AHEAD, 1:], XR[DH:P, s * T:(s + 1) * T - 1]).then_inc(shifted.sem, 1)

                def norm(s):
                    dve.wait_ge(inv.sem, inv.at(0, s + 1))
                    dve.wait_ge(cent.sem, cent.at(0, s + 1))
                    if s >= U:
                        dve.wait_ge(low.sem, low.at(0, s + 1 - U))
                    dve.scalar_tensor_tensor(out=xc[:, s % U, :], in0=ps[:, s % AHEAD, :], scalar=part("ln_g"),
                                             in1=rs[:, s % U, :], op0=ALU.mult, op1=ALU.mult).then_inc(scaled.sem, 1)
                    dve.wait_ge(scaled.sem, scaled.at(0, s + 1))
                    dve.tensor_scalar(xn[:, s % U, :], xc[:, s % U, :], part("ln_b"), None,
                                      ALU.add).then_inc(normed.sem, 1)

                dve.memset(h2[:, :, 0:1], 0.0).then_inc(padded.sem, 1)
                dve.wait_ge(padded.sem, padded.at(0, 1))
                for s in range(AHEAD):
                    shift(s)
                for s in range(B):
                    norm(s)
                    if s + AHEAD < B:
                        shift(s + AHEAD)

        padded.end(1)
        for step in (shifted, cent, squared, var, root, inv, scaled, normed, high, low):
            step.end(1)


def feed_forward_phase(pr, tag, ctx, both, part):
    nc, ps, XR = pr.nc, pr.psum, pr.XN

    def sb(name, shape, dt=F32):
        return pr.sb(name + tag, shape, dt, ctx)

    xh = sb("fxh", [P, B, T], F32R)
    xl = sb("fxl", [P, B, T], F32R)
    gg = sb("gg", [P, 2, 3, T])
    hm = sb("hm", [P, 2, 3, T])
    hh = sb("fhh", [P, 2, 3, T], F32R)
    hl = sb("fhl", [P, 2, 3, T], F32R)
    b1, b2 = part("b1"), part("b2")
    (w1h, w1l), (w2h, w2l) = both("w1"), both("w2")
    xh_all, xl_all = (x[:, :, :].rearrange("p b t -> p (b t)") for x in (xh, xl))
    shifted_norm_phase(pr, tag, part, xh, xl)

    up = pr.step("g_up", 3)
    gelu = pr.step("g_gelu", 3)
    hid = pr.step("g_hidden", 3)
    hhigh = pr.step("g_hidden_high", 3)
    hlow = pr.step("g_hidden_low", 3)
    dn = pr.step("g_down", 1)
    fin = pr.step("g_done", 1)

    def bank(s, c):
        return 4 * s + (0 if c == 1 else 2)

    with nc.Block() as block:
        @block.tensor
        def _(pe):
            def up_product(j, s, c):
                if c == 0:
                    pe.wait_ge(hid.sem, hid.at(j - 1, 0))
                if c == 1:
                    pe.wait_ge(fin.sem, fin.at(j, -1))
                if c == 2:
                    pe.wait_ge(hid.sem, hid.at(j, 1))
                high, low = cols(xh_all, j), cols(xl_all, j)
                for half in range(2):
                    at, m = half * HID + c * P, HB[c]
                    out = ps[0:m, bank(s, c) + half, :]
                    pe.matmul(out, lhsT=w1h[:, at:at + m], rhs=high, start=True, stop=False)
                    pe.matmul(out, lhsT=w1l[:, at:at + m], rhs=high, start=False, stop=False)
                    last = pe.matmul(out, lhsT=w1h[:, at:at + m], rhs=low, start=False, stop=True)
                last.then_inc(up.sem, 1)

            def down_product(j, s, c):
                m, w, out = HB[c], slice(c * P, (c + 1) * P), ps[:, 4 * s, :]
                if c == 0:
                    pe.wait_ge(hid.sem, hid.at(j, 2))
                pe.wait_ge(hlow.sem, hlow.at(j, c + 1))
                pe.matmul(out, lhsT=w2h[0:m, w], rhs=hh[0:m, s, c, :], start=(c == 0), stop=False)
                pe.matmul(out, lhsT=w2l[0:m, w], rhs=hh[0:m, s, c, :], start=False, stop=False)
                last = pe.matmul(out, lhsT=w2h[0:m, w], rhs=hl[0:m, s, c, :], start=False, stop=(c == 2))
                if c == 2:
                    last.then_inc(dn.sem, 1)

            def both_products(j, s):
                up_product(j, s, 0)
                up_product(j, s, 1)
                down_product(j - 1, 1 - s, 0)
                down_product(j - 1, 1 - s, 1)
                up_product(j, s, 2)
                down_product(j - 1, 1 - s, 2)

            for c in range(3):
                up_product(0, 0, c)
            with pe.Fori(0, B // 2 - 1) as i:
                both_products(2 * i + 1, 1)
                both_products(2 * i + 2, 0)
            both_products(B - 1, 1)
            for c in range(3):
                down_product(B - 1, 1, c)

        @block.scalar
        def _(act):
            act.preload_act_table_set("gelu_and_others")
            with act.Fori(0, B // 2) as i:
                for s in range(2):
                    j = 2 * i + s
                    for c in range(3):
                        m = HB[c]
                        act.wait_ge(up.sem, up.at(j, c + 1))
                        act.wait_ge(hid.sem, hid.at(j, c - 5))
                        act.activation(gg[0:m, s, c, :], ps[0:m, bank(s, c) + 1, :], ACT.Gelu,
                                       bias=b1[0:m, 3 + c:4 + c]).then_inc(gelu.sem, 1)

        @block.gpsimd
        def _(pool):
            with pool.Fori(0, B // 2) as i:
                for s in range(2):
                    j = 2 * i + s
                    for c in range(3):
                        m = HB[c]
                        pool.wait_ge(hhigh.sem, hhigh.at(j, c + 1))
                        pool.wait_ge(dn.sem, dn.at(j, -1))
                        pool.tensor_tensor(hl[0:m, s, c, :], hm[0:m, s, c, :], hh[0:m, s, c, :].bitcast(F32),
                                           ALU.subtract).then_inc(hlow.sem, 1)

        @block.vector
        def _(dve):
            def hidden(j, s, tiles):
                for c in tiles:
                    m = HB[c]
                    dve.wait_ge(gelu.sem, gelu.at(j, c + 1))
                    dve.wait_ge(hlow.sem, hlow.at(j, c - 5))
                    dve.scalar_tensor_tensor(out=hm[0:m, s, c, :], in0=ps[0:m, bank(s, c), :], scalar=b1[0:m, c:c + 1],
                                             in1=gg[0:m, s, c, :], op0=ALU.add, op1=ALU.mult).then_inc(hid.sem, 1)
                    dve.wait_ge(hid.sem, hid.at(j, c + 1))
                    dve.wait_ge(dn.sem, dn.at(j, -1))
                    dve.tensor_copy(hh[0:m, s, c, :], hm[0:m, s, c, :]).then_inc(hhigh.sem, 1)

            def add_down(j, s):
                dve.wait_ge(dn.sem, dn.at(j, 1))
                x = cols(XR, j)
                dve.scalar_tensor_tensor(out=x, in0=ps[:, 4 * s, :], scalar=b2, in1=x, op0=ALU.add,
                                         op1=ALU.add).then_inc(fin.sem, 1)

            def step(j, s):
                hidden(j, s, (0, 1))
                add_down(j - 1, 1 - s)
                hidden(j, s, (2,))

            hidden(0, 0, range(3))
            with dve.Fori(0, B // 2 - 1) as i:
                step(2 * i + 1, 1)
                step(2 * i + 2, 0)
            step(B - 1, 1)
            add_down(B - 1, 1)

    for step in (up, gelu, hid, hhigh, hlow, dn, fin):
        step.end(B)


def macaron_kernel(nc, x, gate_w, gate_b, experts, mamba, cell, ffn, consts, out):
    o = CONST_PACK
    with ExitStack() as ctx:
        pr = Program(nc, ctx)
        pr.psum = ctx.enter_context(nc.psum_tensor("banks", [P, 8, T], F32))
        pr.X = pr.sb("X", [P, N])
        pr.XN = pr.sb("XN", [P, N])
        pr.ident = pr.sb("ident", [P, P])
        pr.ident_b = pr.sb("ident_b", [P, P], BF16)
        pr.mean = pr.sb("mean", [P, P])
        pr.center = pr.sb("center", [P, P])
        pr.heads = pr.sb("heads", [P, P])
        pr.tri = pr.sb("tri", [P, NG * NG])
        pr.mask = pr.sb("mask", [P, T], BF16)
        pr.sel = pr.sb("sel", [96, 2 * DS, P], BF16)
        pr.eps = pr.sb("eps", [P, 1])
        const_in = ctx.enter_context(nc.semaphore("const_in"))
        const_ready = ctx.enter_context(nc.semaphore("const_ready"))
        stored = ctx.enter_context(nc.semaphore("stored"))
        for name, inc in STEP_NAMES:
            pr.step(name, 1, inc)
        with ExitStack() as tctx:
            stage = pr.sb("stage", [P, T], ctx=tctx)
            sel_f = pr.sb("sel_f", [96, 2 * DS * P], ctx=tctx)
            with nc.Block() as block:
                @block.sync
                def _(sp):
                    sp.dma_start(pr.X[:, :], x).then_inc(const_in, 16)
                    for t, name in ((pr.ident, "ident"), (pr.mean, "mean"), (pr.heads, "heads"), (pr.tri, "tri")):
                        sp.dma_start(t[:, :], consts[:, o[name][0]:o[name][1]]).then_inc(const_in, 16)
                    sp.dma_start(stage[:, :], consts[:, o["mask"][0]:o["mask"][1]]).then_inc(const_in, 16)
                    sp.dma_start(sel_f[:, :], consts[0:96, o["sel"][0]:o["sel"][1]]).then_inc(const_in, 16)
                    sp.wait_ge(const_in, 16 * 7)

                @block.gpsimd
                def _(pool):
                    for step in pr.steps.values():
                        pool.sem_inc(step.sem, CREDIT)

                @block.vector
                def _(dve):
                    dve.memset(pr.eps[:, :], LN_EPS)
                    dve.wait_ge(const_in, 16 * 7)
                    dve.tensor_copy(pr.ident_b[:, :], pr.ident[:, :])
                    dve.tensor_tensor(pr.center[:, :], pr.ident[:, :], pr.mean[:, :], ALU.subtract)
                    dve.tensor_copy(pr.mask[:, :], stage[:, :])
                    dve.tensor_copy(pr.sel[:, :, :].rearrange("p n q -> p (n q)"), sel_f[:, :]).then_inc(const_ready, 1)
                    dve.wait_ge(const_ready, 1)

        tables = consts[:, o["cos_q"][0]:o["sin_k"][1]]
        X, XN = pr.X, pr.XN

        def moe(tag):
            layer_norm_phase(pr, tag, X, XN)
            moe_phase(pr, tag, gate_w, gate_b, experts)

        def attention(tag):
            layer_norm_phase(pr, tag, X, XN)
            for layer in range(2):
                attention_layer(pr, f"{tag}{layer}", ffn[layer], tables)
            add_stream(pr, 0.5)

        moe("m0")
        layer_norm_phase(pr, "n1", X, XN)
        for layer in range(2):
            mamba_layer(pr, f"a{layer}", mamba[layer])
        add_stream(pr, 1.0)
        moe("m2")
        attention("f3")
        layer_norm_phase(pr, "n4", X, XN)
        cell_phase(pr, "c4", cell)
        attention("f5")
        with nc.Block() as block:
            @block.sync
            def _(sp):
                sp.dma_start(out, X[:, :]).then_inc(stored, 16)
                sp.wait_ge(stored, 16)


STEP_NAMES = [
    ("ln_centered", 1), ("ln_squared", 1), ("ln_var", 1), ("ln_log", 1), ("ln_inv", 1), ("ln_normed", 1),
    ("gate_in", 16), ("logits", 1), ("scored", 1), ("route", 1), ("turned", 1), ("weights_turned", 1),
    ("token_parts", 1), ("w_high", 1), ("w_low", 1), ("gate_up", 1), ("silu", 1), ("product", 1), ("hidden", 1),
    ("hidden_high", 1), ("hidden_low", 1), ("down", 1), ("added", 1), ("m_packed", 16), ("m_ready", 1),
    ("m_xz", 1), ("m_xp_copied", 1), ("m_silu_z", 1), ("m_conv", 1), ("m_x_dbl", 1), ("m_split", 1),
    ("m_dt_proj", 1), ("m_abs", 1), ("m_softplus_exp", 1), ("m_softplus_log", 1), ("m_dt_relu", 1), ("m_dt", 1),
    ("m_dtu", 1), ("m_b_spread", 1), ("m_c_spread", 1), ("m_decay", 1), ("m_b_copied", 1), ("m_driven", 1),
    ("m_scanned", 1), ("m_state_read", 1), ("m_y_summed", 1), ("m_out", 1), ("m_squared", 1), ("m_var", 1),
    ("m_root", 1), ("m_inv", 1), ("m_scaled", 1), ("m_done", 1), ("stream_added", 1), ("c_packed", 16),
    ("c_proj", 1), ("c_xp", 1), ("c_gates", 1), ("c_acts", 1), ("c_bv", 1), ("c_scanned", 1), ("c_silu_h", 1),
    ("c_out", 1), ("c_out_proj", 1), ("c_done", 1), ("f_packed_a", 16), ("f_packed_b", 16), ("f_packed_c", 16),
    ("f_packed_d", 16), ("f_packed", 16), ("f_w_high", 1), ("f_ready", 1), ("f_padded", 1), ("f_shifted", 1),
    ("f_shifted_low", 1), ("f_proj", 1), ("f_squared", 1), ("f_rotated_parts", 1), ("f_rotated", 1),
    ("f_k_norm", 1), ("f_k_norm_kept", 1), ("f_k_root", 1), ("f_k_inv", 1), ("f_k", 1), ("f_q_norm", 1),
    ("f_q_norm_kept", 1), ("f_q_root", 1), ("f_q_log", 1), ("f_v_proj", 1), ("f_v_even", 1), ("f_v_odd", 1),
    ("f_sim", 1), ("f_max", 1), ("f_bias", 1), ("f_exp", 1), ("f_sum_inv", 1), ("f_probs", 1), ("f_turned", 1),
    ("f_turned_copied_a", 1), ("f_turned_copied_b", 1), ("f_pv", 1), ("f_o", 1), ("f_wo", 1), ("f_x1", 1),
    ("g_shifted", 1), ("g_centered", 1), ("g_squared", 1), ("g_var", 1), ("g_root", 1), ("g_inv", 1),
    ("g_scaled", 1), ("g_normed", 1), ("g_low", 1), ("g_up", 1), ("g_gelu", 1), ("g_hidden", 1),
    ("g_hidden_high", 1), ("g_hidden_low", 1), ("g_down", 1), ("g_done", 1), ("chunk_in_a", 16),
    ("chunk_in_b", 16), ("chunk_in_c", 16), ("chunk_in_d", 16), ("m_u", 1), ("m_gated", 1), ("g_high", 1)]


def rotary_tables(np):
    f = np.float32
    half = np.arange(0, DH, 2, dtype=f)
    inv_freq = (f(1.0) / np.power(f(10000.0), half / f(DH))).astype(f)
    t = np.arange(T, dtype=f)
    freqs = (t[:, None] * inv_freq[None, :]).astype(f)
    freqs = np.concatenate([freqs, freqs], axis=-1).astype(np.float64)
    base = (half + 0.4 * DH) / (1.4 * DH)
    power = (t - T // 2) / float(WIN // 2)
    scale = base[None, :].astype(np.float64) ** power[:, None]
    scale = np.concatenate([scale, scale], axis=-1)
    sign = np.concatenate([-np.ones(DH // 2), np.ones(DH // 2)])
    cos, sin = np.cos(freqs), np.sin(freqs) * sign
    return [np.tile(a.T, (2, 1)).astype(f) for a in (cos * scale, sin * scale, cos / scale, sin / scale)]


def constants(np):
    f = np.float32
    r = np.arange(P)
    parts = {"ident": np.eye(P, dtype=f), "mean": np.full((P, P), 1.0 / P, f),
             "heads": (r[:, None] // DH == r[None, :] // DH).astype(f)}
    g = np.arange(NG)
    parts["tri"] = np.tile((g[None, :] < g[:, None]).astype(f).reshape(1, -1), (P, 1))
    q, k = (r % WIN)[:, None], r[None, :]
    inside = (q <= k) & (k <= q + WIN)
    mask = np.where(inside, 0.0, MASKED).astype(f)
    first = np.where(inside & (k >= WIN), 0.0, MASKED).astype(f)
    opening = np.where((r < WIN)[:, None], first, mask)
    parts["mask"] = np.concatenate([opening] + [mask] * (T // P - 1), axis=1)
    for name, table in zip(("cos_q", "sin_q", "cos_k", "sin_k"), rotary_tables(np)):
        parts[name] = table
    sel = np.zeros((P, 2 * DS, P), f)
    for p in range(96):
        sel[p, p % 32, :] = 1.0
    parts["sel"] = sel.reshape(P, -1)
    return pack(np, CONST_PACK, parts)


def pack(np, layout, parts):
    out = np.zeros((P, layout["total"]), np.float32)
    for name, a in parts.items():
        lo, hi = layout[name]
        a = np.asarray(a).reshape(a.shape[0], -1)
        assert a.shape[1] == hi - lo, name
        at = 32 if name == "dt_w" else 0
        out[at:at + a.shape[0], lo:hi] = a
    return out


def tiles(np, v, n):
    out = np.zeros((n * P,) + v.shape[1:], np.float32)
    out[:v.shape[0]] = v
    return np.moveaxis(out.reshape((n, P) + v.shape[1:]), 0, 1)


def kernel(**inputs):
    import numpy as np
    import concourse.bacc as _bacc
    from concourse.bass_utils import run_bass_kernel_spmd as _run

    a = {k: np.asarray(v) for k, v in inputs.items()}
    arrays = {"x": a["L0_attn_x"].reshape(N, P).T,
              "gate_w": a["L0_ffn_gate_w"].T,
              "gate_b": np.tile(a["L0_ffn_gate_bias"][None, :], (P, 1)),
              "consts": constants(np)}

    def chunk_pack(gate, up, down, experts_of):
        n = -(-gate.shape[0] // P)
        out = np.zeros((n, P, 4, P), np.float32)
        for c in range(n):
            r = slice(c * P, min((c + 1) * P, gate.shape[0]))
            w = r.stop - r.start
            out[c, :, 0, :w], out[c, :, 1, :w], out[c, :w, 2, :] = gate[r].T, up[r].T, down[r]
            if experts_of is not None:
                for d, e in enumerate(experts_of[r]):
                    out[c, [e, E + e], 3, d] = 1.0
        return out.reshape(n, P, 4 * P)

    flat = lambda w: w.reshape(E * I_MOE, P)
    arrays["experts"] = np.concatenate([
        chunk_pack(a["L0_ffn_Sg"], a["L0_ffn_Su"], a["L0_ffn_Sd"].T, None),
        chunk_pack(flat(a["L0_ffn_Wg"]), flat(a["L0_ffn_Wu"]), flat(a["L0_ffn_Wd"].transpose(0, 2, 1)),
                   np.repeat(np.arange(E), I_MOE))])

    for l in range(2):
        m = {k[len("L0_attn_"):]: v[l] for k, v in a.items() if k.startswith("L0_attn_") and k != "L0_attn_x"}
        xp_w = m["x_proj_w"]
        xp_w = np.concatenate([xp_w[DR:], xp_w[:DR]], axis=0)
        arrays[f"mamba{l}"] = pack(np, MAMBA_PACK, {
            "in_w": m["in_proj_w"].T, "xp_w": tiles(np, xp_w.T, HALF), "dt_w": m["dt_proj_w"].T,
            "out_w": tiles(np, m["out_proj_w"].T, HALF), "conv_w": tiles(np, m["conv_w"], HALF),
            "conv_b": tiles(np, m["conv_b"], HALF), "dt_b": tiles(np, m["dt_proj_b"], HALF),
            "A_log": tiles(np, m["A_log"], HALF), "D": tiles(np, m["Dskip"], HALF),
            "ln_w": m["ln_w"][:, None], "ln_b": m["ln_b"][:, None]})
        w = {k[len("L1_ffn_"):]: v[l] for k, v in a.items() if k.startswith("L1_ffn_")}
        d = np.arange(DH)
        turn = (d + DH // 2) % DH
        order = np.concatenate([h * DH + turn for h in range(HEADS)])
        wq, wk, wv = w["wqkv"][:, 0:512], w["wqkv"][:, 512:1024], w["wqkv"][:, 1024:1536]
        twice = lambda v: np.concatenate([v, v])[:, None]
        b1 = np.concatenate([tiles(np, w["b1"][:HID], 3), tiles(np, w["b1"][HID:], 3)], axis=1)
        arrays[f"ffn{l}"] = pack(np, FFN_PACK, {
            "wq": wq, "wqr": wq[:, order], "wk": wk, "wkr": wk[:, order], "wv": wv, "wo": tiles(np, w["wo"], PAIRS),
            "w1": w["w1"], "w2": tiles(np, w["w2"], 3), "b1": b1, "ln_g": w["ln_g"][:, None],
            "ln_b": w["ln_b"][:, None], "b2": w["b2"][:, None], "qs": twice(w["q_scale"]),
            "qsr": twice(w["q_scale"][turn]), "ks": twice(w["k_scale"]), "ksr": twice(w["k_scale"][turn])})
    c = {k[len("L1_attn_"):]: v for k, v in a.items() if k.startswith("L1_attn_")}
    arrays["cell"] = pack(np, CELL_PACK, {
        "w_in": c["W_in"].T, "w_a": c["W_alpha"].T, "w_b": c["W_beta"].T, "w_v": c["W_v"].T, "w_out": c["W_out"].T,
        "b_a": c["b_alpha"][:, None], "b_b": c["b_beta"][:, None], "b_v": c["b_v"][:, None]})

    nc = _bacc.Bacc("TRN2", target_bir_lowering=False, num_devices=1)
    arrays = {k: np.ascontiguousarray(v) for k, v in arrays.items()}
    t = {k: nc.dram_tensor(f"in_{k}", v.shape, F32, kind="ExternalInput").ap() for k, v in arrays.items()}
    out = nc.dram_tensor("out_x", (P, N), F32, kind="ExternalOutput").ap()
    macaron_kernel(nc, t["x"], t["gate_w"], t["gate_b"], t["experts"], [t["mamba0"], t["mamba1"]], t["cell"],
                   [t["ffn0"], t["ffn1"]], t["consts"], out)
    r = _run(nc, [{f"in_{k}": v for k, v in arrays.items()}], core_ids=[0])
    return np.ascontiguousarray(r.results[0]["out_x"].T.reshape(B, T, P))
```
